# Optimizing a Trainium2 kernel written in Bass

```python
import numpy as np
import jax
import jax.numpy as jnp

def _softmax(x, axis=-1):
    return jax.nn.softmax(x, axis=axis)

def _gelu(x):
    return jax.nn.gelu(x, approximate=True)

def _silu(x):
    return jax.nn.silu(x)

def _sigmoid(x):
    return jax.nn.sigmoid(x)

def _layernorm(x, axis=-1, eps=1e-05):
    m = jnp.mean(x, axis=axis, keepdims=True)
    v = jnp.var(x, axis=axis, keepdims=True)
    return (x - m) / jnp.sqrt(v + eps)

def _scatter_add(tgt, idx, src, axis=0):
    return tgt.at[idx].add(src)

def _segment_sum(src, seg, n):
    return jax.ops.segment_sum(src, seg, n)
kernel_name = 'mk_flamingo_gated_d4_seqx_r8_8317c4'

def setup_inputs(seed: int=0):
    np.random.seed(seed)
    _w = jnp.asarray

    def _rec_inputs():
        import jax
        import jax.numpy as jnp
        _rk = jax.random.key(seed)
        x = -0.0003929 + 0.9999 * jax.random.normal(jax.random.fold_in(_rk, 1), (4, 256, 128), jnp.float32)
        _lenS = 256 - jax.random.randint(jax.random.fold_in(_rk, 7), (4,), 0, max(1, 256 // 4) + 1, jnp.int32)
        _lenS2 = 256 - jax.random.randint(jax.random.fold_in(_rk, 8), (4,), 0, max(1, 256 // 4) + 1, jnp.int32)
        _ctx_1024P = jax.random.normal(jax.random.fold_in(_rk, 11), (4, 16, 128), jnp.float32)
        _ctx_1024c = jax.random.dirichlet(jax.random.fold_in(_rk, 511), 0.3 * jnp.ones((16,), jnp.float32), (4, 256))
        _ctx_1024t = jnp.einsum('bsk,bkd->bsd', _ctx_1024c, _ctx_1024P)
        _ctx_1024t = _ctx_1024t * jax.lax.rsqrt(jnp.mean(jnp.square(_ctx_1024t)) + 1e-12) * 0.953939
        ctx_1024 = 2.81802e-05 + 1.00001 * (_ctx_1024t + 0.3 * jax.random.normal(jax.random.fold_in(_rk, 611), (4, 256, 128), jnp.float32))
        _validS = jnp.arange(256)[None, :] < _lenS[:, None]
        _validS2 = jnp.arange(256)[None, :] < _lenS2[:, None]
        _causal = jnp.tril(jnp.ones((256, 256), dtype=bool))
        mask_1x1xSxS2_ik1 = jnp.where(jnp.broadcast_to(_validS2[0:1, None, None, :], (1, 1, 256, 256)), 1, 0).astype(jnp.int32)
        _g = jax.random.normal(jax.random.fold_in(_rk, 9001), (2, 4), jnp.float32)
        _g = jnp.sign(_g) * jnp.maximum(jnp.abs(_g), 1.0) + (_g == 0) * 1.0
        g_xattn = _g[0]
        g_ffn = _g[1]
        return (x, ctx_1024, mask_1x1xSxS2_ik1, g_xattn, g_ffn)
    x, ctx_1024, mask_1x1xSxS2_ik1, g_xattn, g_ffn = _rec_inputs()

    def _L0_xattn_setup():
        import jax, jax.numpy as jnp
        import numpy as np
        import math
        D_MODEL = 128
        N_HEADS = 16
        C = 1
        B, L = (8, 256)

        def _glorot(key, fan):
            lim = np.sqrt(6.0 / (fan + fan)).astype(np.float32)
            return jax.random.uniform(key, (fan, fan), jnp.float32, -lim, lim)
        key = jax.random.key(seed)
        ks = jax.random.split(key, 7)
        queries = jax.random.normal(ks[0], (B, L, D_MODEL), jnp.float32)
        keys = jax.random.normal(ks[1], (B, L, D_MODEL), jnp.float32)
        values = jax.random.normal(ks[2], (B, L, D_MODEL), jnp.float32)
        wq = _glorot(ks[3], D_MODEL)
        wk = _glorot(ks[4], D_MODEL)
        wv = _glorot(ks[5], D_MODEL)
        wo = _glorot(ks[6], D_MODEL)
        return {'queries': queries, 'keys': keys, 'values': values, 'wq': wq, 'wk': wk, 'wv': wv, 'wo': wo}
    _L0_xattn_all = _L0_xattn_setup()
    _L0_xattn_in = {k: v for k, v in _L0_xattn_all.items() if k in ('wq', 'wk', 'wv', 'wo')}
    del _L0_xattn_all

    def _L0_ffn_setup():
        import jax, jax.numpy as jnp
        import numpy as np
        B, S, H = (2, 256, 128)
        I = 64
        E_R, E_Z = (32, 8)
        E_T = E_R + E_Z
        K = 6
        SCALE = 2.5
        W_INIT = 0.02
        key = jax.random.key(seed)
        k0, k1, k2, k3 = jax.random.split(key, 4)
        return {'hidden_states': jax.random.normal(k0, (B, S, H), jnp.float32), 'classifier_weight': jax.random.normal(k1, (E_T, H), jnp.float32) * W_INIT, 'e_score_correction_bias': jnp.zeros((E_T,), jnp.float32), 'gate_up_proj': jax.random.normal(k2, (E_T, 2 * I, H), jnp.float32) * W_INIT, 'down_proj': jax.random.normal(k3, (E_R, H, I), jnp.float32) * W_INIT}
    _L0_ffn_all = _L0_ffn_setup()
    _L0_ffn_in = {k: v for k, v in _L0_ffn_all.items() if k in ('classifier_weight', 'e_score_correction_bias', 'gate_up_proj', 'down_proj')}
    del _L0_ffn_all

    def _L1_xattn_setup():
        import jax, jax.numpy as jnp
        import numpy as np
        D_MODEL = 128
        NHEAD = 16
        HEAD_DIM = D_MODEL // NHEAD
        key = jax.random.key(seed)
        ks = jax.random.split(key, 11)
        B, S, D = (4, 256, D_MODEL)
        scale = 1.0 / np.sqrt(D)
        inp = {'q': jax.random.normal(ks[0], (B, S, D), jnp.float32), 'k': jax.random.normal(ks[1], (B, S, D), jnp.float32), 'v': jax.random.normal(ks[2], (B, S, D), jnp.float32), 'Wq': jax.random.normal(ks[3], (D, D), jnp.float32) * scale, 'bq': jnp.zeros((D,), jnp.float32), 'Wk': jax.random.normal(ks[4], (D, D), jnp.float32) * scale, 'bk': jnp.zeros((D,), jnp.float32), 'Wv': jax.random.normal(ks[5], (D, D), jnp.float32) * scale, 'bv': jnp.zeros((D,), jnp.float32), 'Wo': jax.random.normal(ks[6], (D, D), jnp.float32) * scale, 'bo': jnp.zeros((D,), jnp.float32)}
        return inp
    _L1_xattn_all = _L1_xattn_setup()
    _L1_xattn_in = {k: v for k, v in _L1_xattn_all.items() if k in ('Wq', 'bq', 'Wk', 'bk', 'Wv', 'bv', 'Wo', 'bo')}
    del _L1_xattn_all

    def _L1_ffn_setup():
        import jax, jax.numpy as jnp
        import numpy as np
        HIDDEN = 128
        MOE_FF = 64
        SHARED_FF = 352
        NUM_EXPERTS = 16
        TOP_K = 2
        NORM_TOPK = True
        key = jax.random.key(seed)
        ks = jax.random.split(key, 8)
        s = 0.02
        return {'layer_input': jax.random.normal(ks[0], (1, 256, HIDDEN), dtype=jnp.float32), 'gate_w': jax.random.normal(ks[1], (NUM_EXPERTS, HIDDEN), dtype=jnp.float32) * s, 'w_gate_up': jax.random.normal(ks[2], (NUM_EXPERTS, HIDDEN, 2 * MOE_FF), dtype=jnp.float32) * s, 'w_down': jax.random.normal(ks[3], (NUM_EXPERTS, MOE_FF, HIDDEN), dtype=jnp.float32) * s, 'shared_w_gate': jax.random.normal(ks[4], (SHARED_FF, HIDDEN), dtype=jnp.float32) * s, 'shared_w_up': jax.random.normal(ks[5], (SHARED_FF, HIDDEN), dtype=jnp.float32) * s, 'shared_w_down': jax.random.normal(ks[6], (HIDDEN, SHARED_FF), dtype=jnp.float32) * s, 'shared_gate_w': jax.random.normal(ks[7], (1, HIDDEN), dtype=jnp.float32) * s}
    _L1_ffn_all = _L1_ffn_setup()
    _L1_ffn_in = {k: v for k, v in _L1_ffn_all.items() if k in ('gate_w', 'w_gate_up', 'w_down', 'shared_w_gate', 'shared_w_up', 'shared_w_down', 'shared_gate_w')}
    del _L1_ffn_all

    def _L2_xattn_setup():
        import jax, jax.numpy as jnp
        import numpy as np
        WINDOW = 32

        def _band_attention(qh, k, v, w):
            B, H, L, hd = qh.shape
            nb = L // w
            qb = qh.reshape(B, H, nb, w, hd)
            kp = jnp.pad(k, ((0, 0), (w, w), (0, 0))).reshape(B, nb + 2, w, hd)
            vp = jnp.pad(v, ((0, 0), (w, w), (0, 0))).reshape(B, nb + 2, w, hd)
            kwin = jnp.concatenate([kp[:, :-2], kp[:, 1:-1], kp[:, 2:]], axis=2)
            vwin = jnp.concatenate([vp[:, :-2], vp[:, 1:-1], vp[:, 2:]], axis=2)
            scores = jnp.einsum('bhnqd,bnkd->bhnqk', qb, kwin)
            qpos = jnp.arange(w)
            kpos = jnp.arange(3 * w)
            rel = kpos[None, :] - (w + qpos[:, None])
            band = jnp.abs(rel) <= w
            absk = jnp.arange(nb)[:, None, None] * w + kpos[None, None, :] - w
            valid = band[None] & (absk >= 0) & (absk < L)
            neg = jnp.asarray(jnp.finfo(scores.dtype).min, scores.dtype)
            scores = jnp.where(valid[None, None], scores, neg)
            probs = jax.nn.softmax(scores, axis=-1)
            out = jnp.einsum('bhnqk,bnkd->bhnqd', probs, vwin)
            return out.reshape(B, H, L, hd)
        key = jax.random.key(seed)
        kq, kkv, k1, k2, k3 = jax.random.split(key, 5)
        B, L, D, H = (1, 1024, 128, 16)
        hd = D // H
        s = D ** (-0.5)
        return {'q': jax.random.normal(kq, (B, L, D), jnp.float32), 'kv': jax.random.normal(kkv, (B, L, D), jnp.float32), 'w_q': jax.random.normal(k1, (D, D), jnp.float32) * s, 'w_kv': jax.random.normal(k2, (D, 2 * hd), jnp.float32) * s, 'w_o': jax.random.normal(k3, (D, D), jnp.float32) * s}
    _L2_xattn_all = _L2_xattn_setup()
    _L2_xattn_in = {k: v for k, v in _L2_xattn_all.items() if k in ('w_q', 'w_kv', 'w_o')}
    del _L2_xattn_all

    def _L2_ffn_setup():
        import jax, jax.numpy as jnp
        import numpy as np
        B, S, DIM = (4, 256, 128)
        INTER = int(int(DIM * 4) * 0.25)
        E = 32 - 1
        K = 4 - 1

        def _gelu(t):
            return jax.nn.gelu(t, approximate=False)
        key = jax.random.key(seed)
        ks = jax.random.split(key, 12)
        s = 0.02
        return {'x': jax.random.normal(ks[0], (B, S, DIM), jnp.float32), 'ws1': jax.random.normal(ks[1], (DIM, INTER), jnp.float32) * s, 'bs1': jnp.zeros((INTER,), jnp.float32), 'ws2': jax.random.normal(ks[2], (INTER, DIM), jnp.float32) * s, 'bs2': jnp.zeros((DIM,), jnp.float32), 'We1': jax.random.normal(ks[3], (E, DIM, INTER), jnp.float32) * s, 'Be1': jnp.zeros((E, INTER), jnp.float32), 'We2': jax.random.normal(ks[4], (E, INTER, DIM), jnp.float32) * s, 'Be2': jnp.zeros((E, DIM), jnp.float32), 'Wr': jax.random.normal(ks[5], (DIM, E), jnp.float32) * s, 'br': jnp.zeros((E,), jnp.float32)}
    _L2_ffn_all = _L2_ffn_setup()
    _L2_ffn_in = {k: v for k, v in _L2_ffn_all.items() if k in ('ws1', 'bs1', 'ws2', 'bs2', 'We1', 'Be1', 'We2', 'Be2', 'Wr', 'br')}
    del _L2_ffn_all

    def _L3_xattn_setup():
        import jax, jax.numpy as jnp
        import numpy as np
        D_MODEL = 128
        N_HEAD = 16
        HEAD = D_MODEL // N_HEAD

        def _split_heads(x):
            B, S, _ = x.shape
            return x.reshape(B, S, N_HEAD, HEAD).transpose(0, 2, 1, 3)
        key = jax.random.key(seed)
        ks = jax.random.split(key, 12)
        B, S = (2, 256)
        s = 1.0 / np.sqrt(D_MODEL)
        inp = {'q': jax.random.normal(ks[0], (B, S, D_MODEL), jnp.float32), 'k': jax.random.normal(ks[1], (B, S, D_MODEL), jnp.float32), 'v': jax.random.normal(ks[2], (B, S, D_MODEL), jnp.float32), 'mask': jax.random.randint(ks[3], (1, 1, S, S), 0, 2, jnp.int32), 'wq': jax.random.normal(ks[4], (D_MODEL, D_MODEL), jnp.float32) * s, 'bq': jnp.zeros((D_MODEL,), jnp.float32), 'wk': jax.random.normal(ks[5], (D_MODEL, D_MODEL), jnp.float32) * s, 'bk': jnp.zeros((D_MODEL,), jnp.float32), 'wv': jax.random.normal(ks[6], (D_MODEL, D_MODEL), jnp.float32) * s, 'bv': jnp.zeros((D_MODEL,), jnp.float32), 'wo': jax.random.normal(ks[7], (D_MODEL, D_MODEL), jnp.float32) * s, 'bo': jnp.zeros((D_MODEL,), jnp.float32)}
        return inp
    _L3_xattn_all = _L3_xattn_setup()
    _L3_xattn_in = {k: v for k, v in _L3_xattn_all.items() if k in ('wq', 'bq', 'wk', 'bk', 'wv', 'bv', 'wo', 'bo')}
    del _L3_xattn_all

    def _L3_ffn_setup():
        import jax, jax.numpy as jnp
        import numpy as np
        NUM_EXPERTS = 8
        TOP_K = 2
        key = jax.random.key(seed)
        ks = jax.random.split(key, 6)
        B, S, D, H, E = (4, 128, 128, 256, NUM_EXPERTS)
        x = jax.random.normal(ks[0], (B, S, D), dtype=jnp.float32)
        Wg = jax.random.normal(ks[1], (D, E), dtype=jnp.float32) * 0.02
        W1 = jax.random.normal(ks[2], (E, D, H), dtype=jnp.float32) * 0.02
        b1 = jax.random.normal(ks[3], (E, H), dtype=jnp.float32) * 0.02
        W2 = jax.random.normal(ks[4], (E, H, D), dtype=jnp.float32) * 0.02
        b2 = jax.random.normal(ks[5], (E, D), dtype=jnp.float32) * 0.02
        return {'x': x, 'Wg': Wg, 'W1': W1, 'b1': b1, 'W2': W2, 'b2': b2}
    _L3_ffn_all = _L3_ffn_setup()
    _L3_ffn_in = {k: v for k, v in _L3_ffn_all.items() if k in ('Wg', 'W1', 'b1', 'W2', 'b2')}
    del _L3_ffn_all
    return {'x': x, 'ctx_1024': ctx_1024, 'mask_1x1xSxS2_ik1': mask_1x1xSxS2_ik1, 'g_xattn': g_xattn, 'g_ffn': g_ffn, 'L0_xattn_wq': _L0_xattn_in['wq'], 'L0_xattn_wk': _L0_xattn_in['wk'], 'L0_xattn_wv': _L0_xattn_in['wv'], 'L0_xattn_wo': _L0_xattn_in['wo'], 'L0_ffn_classifier_weight': _L0_ffn_in['classifier_weight'], 'L0_ffn_e_score_correction_bias': _L0_ffn_in['e_score_correction_bias'], 'L0_ffn_gate_up_proj': _L0_ffn_in['gate_up_proj'], 'L0_ffn_down_proj': _L0_ffn_in['down_proj'], 'L1_xattn_Wq': _L1_xattn_in['Wq'], 'L1_xattn_bq': _L1_xattn_in['bq'], 'L1_xattn_Wk': _L1_xattn_in['Wk'], 'L1_xattn_bk': _L1_xattn_in['bk'], 'L1_xattn_Wv': _L1_xattn_in['Wv'], 'L1_xattn_bv': _L1_xattn_in['bv'], 'L1_xattn_Wo': _L1_xattn_in['Wo'], 'L1_xattn_bo': _L1_xattn_in['bo'], 'L1_ffn_gate_w': _L1_ffn_in['gate_w'], 'L1_ffn_w_gate_up': _L1_ffn_in['w_gate_up'], 'L1_ffn_w_down': _L1_ffn_in['w_down'], 'L1_ffn_shared_w_gate': _L1_ffn_in['shared_w_gate'], 'L1_ffn_shared_w_up': _L1_ffn_in['shared_w_up'], 'L1_ffn_shared_w_down': _L1_ffn_in['shared_w_down'], 'L1_ffn_shared_gate_w': _L1_ffn_in['shared_gate_w'], 'L2_xattn_w_q': _L2_xattn_in['w_q'], 'L2_xattn_w_kv': _L2_xattn_in['w_kv'], 'L2_xattn_w_o': _L2_xattn_in['w_o'], 'L2_ffn_ws1': _L2_ffn_in['ws1'], 'L2_ffn_bs1': _L2_ffn_in['bs1'], 'L2_ffn_ws2': _L2_ffn_in['ws2'], 'L2_ffn_bs2': _L2_ffn_in['bs2'], 'L2_ffn_We1': _L2_ffn_in['We1'], 'L2_ffn_Be1': _L2_ffn_in['Be1'], 'L2_ffn_We2': _L2_ffn_in['We2'], 'L2_ffn_Be2': _L2_ffn_in['Be2'], 'L2_ffn_Wr': _L2_ffn_in['Wr'], 'L2_ffn_br': _L2_ffn_in['br'], 'L3_xattn_wq': _L3_xattn_in['wq'], 'L3_xattn_bq': _L3_xattn_in['bq'], 'L3_xattn_wk': _L3_xattn_in['wk'], 'L3_xattn_bk': _L3_xattn_in['bk'], 'L3_xattn_wv': _L3_xattn_in['wv'], 'L3_xattn_bv': _L3_xattn_in['bv'], 'L3_xattn_wo': _L3_xattn_in['wo'], 'L3_xattn_bo': _L3_xattn_in['bo'], 'L3_ffn_Wg': _L3_ffn_in['Wg'], 'L3_ffn_W1': _L3_ffn_in['W1'], 'L3_ffn_b1': _L3_ffn_in['b1'], 'L3_ffn_W2': _L3_ffn_in['W2'], 'L3_ffn_b2': _L3_ffn_in['b2']}

def reference(x, ctx_1024, mask_1x1xSxS2_ik1, g_xattn, g_ffn, L0_xattn_wq, L0_xattn_wk, L0_xattn_wv, L0_xattn_wo, L0_ffn_classifier_weight, L0_ffn_e_score_correction_bias, L0_ffn_gate_up_proj, L0_ffn_down_proj, L1_xattn_Wq, L1_xattn_bq, L1_xattn_Wk, L1_xattn_bk, L1_xattn_Wv, L1_xattn_bv, L1_xattn_Wo, L1_xattn_bo, L1_ffn_gate_w, L1_ffn_w_gate_up, L1_ffn_w_down, L1_ffn_shared_w_gate, L1_ffn_shared_w_up, L1_ffn_shared_w_down, L1_ffn_shared_gate_w, L2_xattn_w_q, L2_xattn_w_kv, L2_xattn_w_o, L2_ffn_ws1, L2_ffn_bs1, L2_ffn_ws2, L2_ffn_bs2, L2_ffn_We1, L2_ffn_Be1, L2_ffn_We2, L2_ffn_Be2, L2_ffn_Wr, L2_ffn_br, L3_xattn_wq, L3_xattn_bq, L3_xattn_wk, L3_xattn_bk, L3_xattn_wv, L3_xattn_bv, L3_xattn_wo, L3_xattn_bo, L3_ffn_Wg, L3_ffn_W1, L3_ffn_b1, L3_ffn_W2, L3_ffn_b2):
    import jax
    import jax.numpy as jnp

    def _L0_xattn_ref(queries, keys, values, wq, wk, wv, wo):
        import jax, jax.numpy as jnp
        import numpy as np
        import math
        D_MODEL = 128
        N_HEADS = 16
        C = 1
        B, L = (8, 256)

        def _glorot(key, fan):
            lim = np.sqrt(6.0 / (fan + fan)).astype(np.float32)
            return jax.random.uniform(key, (fan, fan), jnp.float32, -lim, lim)
        Bv, Lv, _ = queries.shape
        H = N_HEADS
        Dh = D_MODEL // N_HEADS
        Q = (queries @ wq).reshape(Bv, Lv, H, Dh).transpose(0, 2, 3, 1)
        K = (keys @ wk).reshape(Bv, Lv, H, Dh).transpose(0, 2, 3, 1)
        V = (values @ wv).reshape(Bv, Lv, H, Dh).transpose(0, 2, 3, 1)
        corr = jnp.fft.irfft(jnp.fft.rfft(Q, axis=-1) * jnp.conj(jnp.fft.rfft(K, axis=-1)), n=Lv, axis=-1)
        k_top = int(math.floor(C * math.log(Lv)))
        top_vals, top_idx = jax.lax.top_k(corr, k_top)
        w = jax.nn.softmax(top_vals, axis=-1)
        t = jnp.arange(Dh)
        out = jnp.zeros_like(V)
        for i in range(k_top):
            gather_idx = (t[None, None, :] - top_idx[..., i]) % Dh
            rolled = jnp.take_along_axis(V, gather_idx[..., None], axis=2)
            out = out + w[..., i, None] * rolled
        out = out.transpose(0, 2, 1, 3).reshape(Bv, Lv, D_MODEL)
        return out @ wo

    def _L0_ffn_ref(hidden_states, classifier_weight, e_score_correction_bias, gate_up_proj, down_proj):
        import jax, jax.numpy as jnp
        import numpy as np
        B, S, H = (2, 256, 128)
        I = 64
        E_R, E_Z = (32, 8)
        E_T = E_R + E_Z
        K = 6
        SCALE = 2.5
        W_INIT = 0.02
        orig_shape = hidden_states.shape
        x = hidden_states.reshape(-1, H).astype(jnp.float32)
        T = x.shape[0]
        logits = x @ classifier_weight.T
        scores = jax.nn.softmax(logits, axis=-1)
        _, topk_idx = jax.lax.top_k(scores + e_score_correction_bias[None, :], K)
        topk_w = jnp.take_along_axis(scores, topk_idx, axis=1) * SCALE
        w_full = jnp.zeros((T, E_T), jnp.float32).at[jnp.arange(T)[:, None], topk_idx].add(topk_w)
        zero_w = w_full[:, E_R:].sum(axis=-1, keepdims=True)
        out0 = x * zero_w
        routed_w = w_full[:, :E_R].T

        def body(out, xs):
            Wgu, Wd, we = xs
            gate, up = jnp.split(x @ Wgu.T, 2, axis=-1)
            y = jax.nn.silu(gate) * up @ Wd.T
            return (out + we[:, None] * y, None)
        out, _ = jax.lax.scan(body, out0, (gate_up_proj[:E_R], down_proj, routed_w))
        return out.reshape(orig_shape).astype(hidden_states.dtype)

    def _L1_xattn_ref(q, k, v, Wq, bq, Wk, bk, Wv, bv, Wo, bo):
        import jax, jax.numpy as jnp
        import numpy as np
        D_MODEL = 128
        NHEAD = 16
        HEAD_DIM = D_MODEL // NHEAD
        B, S, D = q.shape
        H, Hd = (NHEAD, HEAD_DIM)
        qh = (q @ Wq.T + bq).reshape(B, S, H, Hd).transpose(0, 2, 1, 3)
        kh = (k @ Wk.T + bk).reshape(B, S, H, Hd).transpose(0, 2, 1, 3)
        vh = (v @ Wv.T + bv).reshape(B, S, H, Hd).transpose(0, 2, 1, 3)
        scores = jnp.einsum('bhqd,bhkd->bhqk', qh, kh) / jnp.sqrt(jnp.float32(Hd))
        attn = jax.nn.softmax(scores, axis=-1)
        out = jnp.einsum('bhqk,bhkd->bhqd', attn, vh)
        out = out.transpose(0, 2, 1, 3).reshape(B, S, D)
        return out @ Wo.T + bo

    def _L1_ffn_ref(layer_input, gate_w, w_gate_up, w_down, shared_w_gate, shared_w_up, shared_w_down, shared_gate_w):
        import jax, jax.numpy as jnp
        import numpy as np
        HIDDEN = 128
        MOE_FF = 64
        SHARED_FF = 352
        NUM_EXPERTS = 16
        TOP_K = 2
        NORM_TOPK = True
        B, S, D = layer_input.shape
        x = layer_input.reshape(-1, D)
        N = x.shape[0]
        shared = jax.nn.silu(x @ shared_w_gate.T) * (x @ shared_w_up.T) @ shared_w_down.T
        shared = shared * jax.nn.sigmoid(x @ shared_gate_w.T)
        logits = x @ gate_w.T
        probs = jax.nn.softmax(logits.astype(jnp.float32), axis=-1)
        rw, sel = jax.lax.top_k(probs, TOP_K)
        if NORM_TOPK:
            rw = rw / rw.sum(axis=-1, keepdims=True)
        rw = rw.astype(x.dtype)
        combine = jnp.zeros((N, NUM_EXPERTS), x.dtype).at[jnp.arange(N)[:, None], sel].set(rw)
        gu = jnp.einsum('nd,edf->nef', x, w_gate_up)
        g, h = jnp.split(gu, 2, axis=-1)
        h = jax.nn.silu(g) * h
        expert_out = jnp.einsum('nef,efd,ne->nd', h, w_down, combine)
        out = expert_out + shared
        return out.reshape(B, S, D)

    def _L2_xattn_ref(q, kv, w_q, w_kv, w_o):
        import jax, jax.numpy as jnp
        import numpy as np
        WINDOW = 32

        def _band_attention(qh, k, v, w):
            B, H, L, hd = qh.shape
            nb = L // w
            qb = qh.reshape(B, H, nb, w, hd)
            kp = jnp.pad(k, ((0, 0), (w, w), (0, 0))).reshape(B, nb + 2, w, hd)
            vp = jnp.pad(v, ((0, 0), (w, w), (0, 0))).reshape(B, nb + 2, w, hd)
            kwin = jnp.concatenate([kp[:, :-2], kp[:, 1:-1], kp[:, 2:]], axis=2)
            vwin = jnp.concatenate([vp[:, :-2], vp[:, 1:-1], vp[:, 2:]], axis=2)
            scores = jnp.einsum('bhnqd,bnkd->bhnqk', qb, kwin)
            qpos = jnp.arange(w)
            kpos = jnp.arange(3 * w)
            rel = kpos[None, :] - (w + qpos[:, None])
            band = jnp.abs(rel) <= w
            absk = jnp.arange(nb)[:, None, None] * w + kpos[None, None, :] - w
            valid = band[None] & (absk >= 0) & (absk < L)
            neg = jnp.asarray(jnp.finfo(scores.dtype).min, scores.dtype)
            scores = jnp.where(valid[None, None], scores, neg)
            probs = jax.nn.softmax(scores, axis=-1)
            out = jnp.einsum('bhnqk,bnkd->bhnqd', probs, vwin)
            return out.reshape(B, H, L, hd)
        B, L, D = q.shape
        hd = w_kv.shape[-1] // 2
        H = D // hd
        qh = (q @ w_q).reshape(B, L, H, hd).transpose(0, 2, 1, 3)
        k, v = jnp.split(kv @ w_kv, 2, axis=-1)
        o = _band_attention(qh, k, v, WINDOW)
        o = o.transpose(0, 2, 1, 3).reshape(B, L, D)
        return o @ w_o

    def _L2_ffn_ref(x, ws1, bs1, ws2, bs2, We1, Be1, We2, Be2, Wr, br):
        import jax, jax.numpy as jnp
        import numpy as np
        B, S, DIM = (4, 256, 128)
        INTER = int(int(DIM * 4) * 0.25)
        E = 32 - 1
        K = 4 - 1

        def _gelu(t):
            return jax.nn.gelu(t, approximate=False)
        shared = _gelu(x @ ws1 + bs1) @ ws2 + bs2
        aff = jax.nn.softmax(x @ Wr + br, axis=-1)
        vals, idx = jax.lax.top_k(aff, K)
        gates = jnp.sum(jax.nn.one_hot(idx, E, dtype=x.dtype) * vals[..., None], axis=-2)
        gates_e = jnp.moveaxis(gates, -1, 0)

        def step(acc, p):
            W1, B1, W2, B2, g = p
            h = _gelu(x @ W1 + B1)
            return (acc + g[..., None] * (h @ W2 + B2), None)
        routed, _ = jax.lax.scan(step, jnp.zeros_like(x), (We1, Be1, We2, Be2, gates_e))
        return shared + routed + x

    def _L3_xattn_ref(q, k, v, mask, wq, bq, wk, bk, wv, bv, wo, bo):
        import jax, jax.numpy as jnp
        import numpy as np
        D_MODEL = 128
        N_HEAD = 16
        HEAD = D_MODEL // N_HEAD

        def _split_heads(x):
            B, S, _ = x.shape
            return x.reshape(B, S, N_HEAD, HEAD).transpose(0, 2, 1, 3)
        q_s = _split_heads(q @ wq.T + bq)
        k_s = _split_heads(k @ wk.T + bk)
        v_s = _split_heads(v @ wv.T + bv)
        scale = 1.0 / np.sqrt(HEAD)
        score = jnp.einsum('bhqd,bhkd->bhqk', q_s, k_s) * scale
        score = jnp.where(mask == 0, jnp.float32(-10000.0), score)
        attn = jax.nn.softmax(score, axis=-1)
        out = jnp.einsum('bhqk,bhkd->bhqd', attn, v_s)
        B, H, S, Dh = out.shape
        out = out.transpose(0, 2, 1, 3).reshape(B, S, H * Dh)
        return out @ wo.T + bo

    def _L3_ffn_ref(x, Wg, W1, b1, W2, b2):
        import jax, jax.numpy as jnp
        import numpy as np
        NUM_EXPERTS = 8
        TOP_K = 2
        B, S, D = x.shape
        E, _, H = W1.shape
        OUT = W2.shape[2]
        xm = x.reshape(-1, D)
        logits = xm @ Wg
        probs = jax.nn.softmax(logits, axis=-1)
        topk_p, topk_i = jax.lax.top_k(probs, TOP_K)
        flat_e = topk_i.reshape(-1)
        flat_p = topk_p.reshape(-1)
        order = jnp.argsort(flat_e)
        tok_idx = order // TOP_K
        e_sorted = flat_e[order]
        p_sorted = flat_p[order]
        xs = xm[tok_idx]
        y = jnp.zeros((xs.shape[0], OUT), dtype=xs.dtype)
        for e in range(E):
            h = jax.nn.relu(xs @ W1[e] + b1[e])
            ye = h @ W2[e] + b2[e]
            m = (e_sorted == e)[:, None].astype(xs.dtype)
            y = y + m * ye
        y = y * p_sorted[:, None]
        out = jnp.zeros((B * S, OUT), dtype=y.dtype).at[tok_idx].add(y)
        return out.reshape(B, S, OUT)
    x = x + jnp.tanh(g_xattn[0]) * _L0_xattn_ref(_layernorm(x, axis=-1), ctx_1024, ctx_1024, L0_xattn_wq, L0_xattn_wk, L0_xattn_wv, L0_xattn_wo)
    x = x + jnp.tanh(g_ffn[0]) * _L0_ffn_ref(_layernorm(x, axis=-1), L0_ffn_classifier_weight, L0_ffn_e_score_correction_bias, L0_ffn_gate_up_proj, L0_ffn_down_proj)
    x = x + jnp.tanh(g_xattn[1]) * _L1_xattn_ref(_layernorm(x, axis=-1), ctx_1024, ctx_1024, L1_xattn_Wq, L1_xattn_bq, L1_xattn_Wk, L1_xattn_bk, L1_xattn_Wv, L1_xattn_bv, L1_xattn_Wo, L1_xattn_bo)
    x = x + jnp.tanh(g_ffn[1]) * _L1_ffn_ref(_layernorm(x, axis=-1), L1_ffn_gate_w, L1_ffn_w_gate_up, L1_ffn_w_down, L1_ffn_shared_w_gate, L1_ffn_shared_w_up, L1_ffn_shared_w_down, L1_ffn_shared_gate_w)
    x = x + jnp.tanh(g_xattn[2]) * _L2_xattn_ref(_layernorm(x, axis=-1), ctx_1024, L2_xattn_w_q, L2_xattn_w_kv, L2_xattn_w_o)
    x = x + jnp.tanh(g_ffn[2]) * _L2_ffn_ref(_layernorm(x, axis=-1), L2_ffn_ws1, L2_ffn_bs1, L2_ffn_ws2, L2_ffn_bs2, L2_ffn_We1, L2_ffn_Be1, L2_ffn_We2, L2_ffn_Be2, L2_ffn_Wr, L2_ffn_br)
    x = x + jnp.tanh(g_xattn[3]) * _L3_xattn_ref(_layernorm(x, axis=-1), ctx_1024, ctx_1024, mask_1x1xSxS2_ik1, L3_xattn_wq, L3_xattn_bq, L3_xattn_wk, L3_xattn_bk, L3_xattn_wv, L3_xattn_bv, L3_xattn_wo, L3_xattn_bo)
    x = x + jnp.tanh(g_ffn[3]) * _L3_ffn_ref(_layernorm(x, axis=-1), L3_ffn_Wg, L3_ffn_W1, L3_ffn_b1, L3_ffn_W2, L3_ffn_b2)
    return x

_drawn_inputs = setup_inputs


def setup_inputs(seed=0):
    import zlib

    import numpy as np

    out = dict(_drawn_inputs(seed))
    spreads = {'L0_ffn_e_score_correction_bias': (0.0, 0.1),
     'L1_xattn_bq': (0.0, 0.537),
     'L1_xattn_bk': (0.0, 2.0),
     'L1_xattn_bv': (0.0, 0.1),
     'L1_xattn_bo': (0.0, 0.1),
     'L2_ffn_bs1': (0.0, 1.775),
     'L2_ffn_bs2': (0.0, 0.1),
     'L2_ffn_Be1': (0.0, 0.8),
     'L2_ffn_Be2': (0.0, 0.8),
     'L2_ffn_br': (0.0, 0.8),
     'L3_xattn_bq': (0.0, 1.163),
     'L3_xattn_bk': (0.0, 2.0),
     'L3_xattn_bv': (0.0, 0.283),
     'L3_xattn_bo': (0.0, 0.31)}
    factors = {'g_ffn': 8.0,
     'L0_ffn_gate_up_proj': 8.0,
     'L0_ffn_down_proj': 8.0,
     'L1_ffn_gate_w': 8.0,
     'L1_ffn_w_gate_up': 8.0,
     'L1_ffn_w_down': 8.0,
     'L1_ffn_shared_w_gate': 8.0,
     'L1_ffn_shared_w_up': 8.0,
     'L1_ffn_shared_w_down': 8.0,
     'L1_ffn_shared_gate_w': 8.0,
     'L2_ffn_We1': 8.0,
     'L2_ffn_We2': 8.0,
     'L2_ffn_Wr': 6.885,
     'L3_ffn_Wg': 4.633,
     'L3_ffn_W1': 5.368,
     'L3_ffn_b1': 23.404,
     'L3_ffn_W2': 4.426,
     'L3_ffn_b2': 21.794,
     'L2_ffn_ws1': 5.01}
    for name, (base, spread) in spreads.items():
        noise = np.random.default_rng([zlib.crc32(name.encode()), seed]).standard_normal(out[name].shape)
        drawn = base * np.exp(spread * noise) if base else spread * noise
        out[name] = jnp.asarray(drawn.astype(out[name].dtype))
    for name, factor in factors.items():
        out[name] = (out[name] * factor).astype(out[name].dtype)
    return out
```

```python
from contextlib import ExitStack

import numpy as np
import concourse.bass as bass
from concourse import mybir

B, S, D, H, HD = 4, 256, 128, 16, 8
N = B * S
P = 128
NT = N // P
TB = S // P
NHALF, HALF = 2, 512
PARTS = 3
STACK = PARTS * PARTS * HD
SROWS = STACK + PARTS
TOPLAGS = 5
BAND = 32
EP = 32
RING = 4
NEG = -1.0e30
FLAG = -3.0e38
LN_EPS = 1e-5
MASKED = -10000.0

ROUTE = [dict(E=40, SM=40, K=6, ENT=16), dict(E=17, SM=16, K=2, ENT=11),
         dict(E=31, SM=31, K=3, ENT=32), dict(E=8, SM=8, K=2, ENT=16)]
GLU_COLS, MLP_COLS = 3 * P, 2 * P + 1
R_REAL = 32
SHARED_TILES = 3
SCALE = [None, 1.0 / HD ** 0.5, 1.0, 1.0 / HD ** 0.5]

C_ID, C_DFT, C_INV, C_BLK, C_DPOS, C_IOTA, C_ID3, C_BAND = 0, 128, 640, 1408, 1424, 1425, 1433, 1465
C_ALL = C_BAND + TB * S


def build(nc, t, out):
    f32, bf16, i32, u32 = mybir.dt.float32, mybir.dt.bfloat16, mybir.dt.int32, mybir.dt.uint32
    ALU, ACT, AX = mybir.AluOpType, mybir.ActivationFunctionType, mybir.AxisListType
    ctx = ExitStack()
    with ctx:
        def sb(name, shape, dt=f32):
            return ctx.enter_context(nc.sbuf_tensor(name, shape, dt))

        def sem(name):
            return ctx.enter_context(nc.semaphore(name))

        x = sb("x_res", [P, NT, D])
        xn = sb("xn", [P, NT, D])
        xnT = sb("xnT", [P, N])
        ctx_tok = sb("ctx_tok", [P, NT, D])
        ctxT = sb("ctxT", [P, N])
        consts = sb("consts", [P, C_ALL])
        ident = consts[:, C_ID:C_ID + P]
        identb = sb("identb", [P, P], bf16)
        ones_row = sb("ones_row", [1, P])
        zerob = sb("zerob", [P, HALF], bf16)
        pick64 = sb("pick64", [PARTS * EP, EP, P // 2], bf16)
        pick128 = sb("pick128", [PARTS * EP, EP, P], bf16)
        gates = sb("gates", [P, 8])
        gtan = sb("gtan", [P, 8])
        stats = sb("stats", [P, NT, 6])
        mv = sb("mv", [P, NT, 2])
        veps = sb("veps", [P, NT])
        mhalf = sb("mhalf", [P, NT])
        rstd = sb("rstd", [P, NT])
        att_w = [sb(f"att_w{L}", [P, 4 * P + 2]) for L in range(4)]
        att_row = [None] + [sb(f"att_row{L}", [1, P + HALF]) for L in range(1, 4)]
        wr = [sb(f"wr{L}", [P, ROUTE[L]["E"]]) for L in range(4)]
        br2 = sb("br2", [1, ROUTE[2]["E"]])
        cbias = sb("cbias", [P, ROUTE[0]["E"]])
        b2 = {2: sb("b2_2", [EP, P]), 3: sb("b2_3", [EP, P])}
        rmax = sb("rmax", [P, NT])
        rsum = sb("rsum", [P, NT])
        rrec = sb("rrec", [P, NT])
        shifted = sb("shifted", [P, NT, 40])
        probs = sb("probs", [P, NT, 40])
        ranked = shifted
        flagged = sb("flagged", [P, NT, 40])
        picked = sb("picked", [P, NT, 40])
        top8 = sb("top8", [P, NT, 8])
        gzero = sb("gzero", [P, NT])
        zsg = sb("zsg", [P, NT])
        wtab = sb("wtab", [P, NT, EP])
        wrest = sb("wrest", [P, NT, EP])
        wpart = sb("wpart", [P, NT, PARTS, EP], bf16)
        wT = sb("wT", [PARTS * EP, N], bf16)
        ring = sb("ring", [P, RING, GLU_COLS])
        qf, kf = sb("qf", [P, N]), sb("kf", [P, N])
        qp, kp = sb("qp", [P, PARTS, N], bf16), sb("kp", [P, PARTS, N], bf16)
        rest = sb("rest", [P, HALF])
        qst, kst = sb("qst", [96, H, N], bf16), sb("kst", [96, H, N], bf16)
        vall = sb("vall", [P, NT, H, 32])
        pT = sb("pT", [P, 8, 2 * S])
        negmax = sb("negmax", [P, B, TB, H])
        nmrest = sb("nmrest", [P, TB, H])
        nmpart = sb("nmpart", [P, B, TB, PARTS, H], bf16)
        nmT = sb("nmT", [PARTS * H * TB, B, P], bf16)
        oT = sb("oT", [P, 4 * S])
        orec = sb("orec", [P, TB, H])
        ocor = sb("ocor", [P, TB, H, 9])
        ocomb = sb("ocomb", [P, TB, H, 9])
        emask = sb("emask", [P, B, TB, H])
        onrm = xn
        onT = pT[:, 6:8, :].rearrange("p a n -> p (a n)")
        act_out, gated, hid = pT[:, 0:2, :], pT[:, 2:4, :], pT[:, 4:6, :]
        yT = oT
        wTf = qf[0:EP, :]
        mask_i = qp[:, 0:2, :].rearrange("p a n -> p (a n)").bitcast(i32).rearrange("p (a k n) -> p a k n", a=2, k=TB)
        negq = ctx_tok[:, 4:8, :].rearrange("p a n -> p (a n)").bitcast(bf16).rearrange("p (a k n) -> p a k n", a=2, k=TB)
        negk = sb("negk", [P, TB, S], bf16)
        maskedT = ctx_tok[:, 0:4, :].rearrange("p a n -> p (a n)").rearrange("p (k n) -> p k n", k=TB)
        umask = consts[:, C_DFT:C_DFT + B * TB * H * 9].rearrange("p (b q n) -> p b q n", b=B, q=TB)
        negfloor = sb("negfloor", [P, TB])
        dft_in = kf
        kfreq = qf[:, :].rearrange("p (a n) -> p a n", a=2)
        prod = pT[:, 0:5, :]
        corr8 = sb("corr8", [P, B, 8])
        lag8 = sb("lag8", [P, B, 8], u32)
        cw = sb("cw", [P, 4, B * TOPLAGS])
        csum = sb("csum", [P, 2, B])
        roll_i = sb("roll_i", [P, 2, B * TOPLAGS], i32)
        sel = sb("sel", [P, B * TOPLAGS, HD])
        mix8 = sb("mix8", [P, B, HD])
        mixT = onT[:, 0:B * P].rearrange("p (b n) -> p b n", b=B)
        mixo = onT[:, B * P:2 * B * P]
        vo = oT
        ctx_nat = kp[:, 0:2, :].rearrange("p a n -> p (a n)").bitcast(f32).rearrange("p (t d) -> p t d", t=NT)

        PS = ctx.enter_context(nc.psum_tensor("PS", [P, 8, HALF], f32))

        def banks(a, n=2):
            return PS[:, a:a + n, :].rearrange("p a n -> p (a n)")

        ld_x, ld_ctx, ld_ctxT, ld_const, ld_gate = sem("ld_x"), sem("ld_ctx"), sem("ld_ctxT"), sem("ld_const"), sem("ld_gate")
        ld_att = [sem(f"ld_att{L}") for L in range(4)]
        ld_route = sem("ld_route")
        ld_mask = sem("ld_mask")
        stored = sem("stored")
        set_pool, set_dve, gate_ready = sem("set_pool"), sem("set_dve"), sem("gate_ready")
        dstep, astep = sem("dstep"), sem("astep")
        ln_var, ln_rstd, ln_xn, ln_tr, ln_xnT = sem("ln_var"), sem("ln_rstd"), sem("ln_xn"), sem("ln_tr"), [sem("ln_xnT0"), sem("ln_xnT1")]
        masks_ready = sem("masks_ready")
        ac = {n: sem("ac_" + n) for n in ("kin", "kine", "kfreq", "kfe", "qin", "qine", "qfreq", "prod", "corr", "top",
                                          "exp", "mix", "mo", "moe", "z", "ze", "vo", "voe", "out")}
        adds = dict(q=2, k=2, v=1, kf=4, qf=4, kparts=2, qparts=2, vall=2, s=B * H, mx=B * H, nmp=B, nmt=B, nmc=B,
                    st=B * H, p=B * H, pv=4 * B, oe=B, ot=B, on=B, fin_t=2, fin_e=2, fin=2)
        at = {n: sem(f"at_{n}") for n in (*adds, "u", "ue", "em")}
        at_kst = [None] + [[sem(f"at{L}_kst{h}") for h in range(NHALF)] for L in range(1, 4)]
        at_qst = [None] + [[sem(f"at{L}_qst{h}") for h in range(NHALF)] for L in range(1, 4)]
        at_nmd = [sem(f"at_nmd{b}") for b in range(B)]
        rt = {n: sem("rt_" + n) for n in ("logits", "shift", "exp", "parts", "tr", "wT")}
        ring_in = [sem(f"ring_in{k}") for k in range(RING)]
        mo = [{n: sem(f"mo{L}_{n}") for n in ("up", "act", "gated", "hid", "y", "yT", "ytr")} for L in range(4)]
        x_done = sem("x_done")

        block = ctx.enter_context(nc.Block())
        glu_w = {0: t["glu0"], 1: t["glu1"]}
        mlp_w = {2: t["mlp2"], 3: t["mlp3"]}
        before = [[sum(len(range(k, ROUTE[M]["ENT"], RING)) for M in range(L)) for k in range(RING)] for L in range(4)]
        UP_AHEAD = 2
        LAG = 24
        NU = B * H

        def groups(entries):
            return (entries - 1) // RING

        @block.sync
        def _(sp):
            sp.dma_start(x[:, :, :], t["x"]).then_inc(ld_x, 16)
            sp.dma_start(consts[:, :], t["consts"]).then_inc(ld_const, 16)
            sp.dma_start(ctx_tok[:, :, :], t["ctx_tok"]).then_inc(ld_ctx, 16)
            sp.dma_start(ctx_nat[:, :, :], t["ctx_nat"]).then_inc(ld_ctx, 16)
            sp.dma_start(ctxT[:, :], t["ctxT"]).then_inc(ld_ctxT, 16)
            sp.dma_start(att_w[0][:, :], t["att_w0"]).then_inc(ld_att[0], 16)
            sp.dma_start(gates[:, :], t["gates"].partition_broadcast(P)).then_inc(ld_gate, 16)
            for L in range(4):
                sp.dma_start(wr[L][:, :], t[f"wr{L}"]).then_inc(ld_route, 16)
            sp.dma_start(br2[:, :], t["br2"]).then_inc(ld_route, 16)
            sp.dma_start(cbias[:, :], t["cbias"].partition_broadcast(P)).then_inc(ld_route, 16)
            for L in (2, 3):
                sp.dma_start(b2[L][:, :], t[f"b2_{L}"]).then_inc(ld_route, 16)
            for L in range(1, 4):
                sp.dma_start(att_w[L][:, :], t[f"att_w{L}"]).then_inc(ld_att[L], 16)
                sp.dma_start(att_row[L][:, :], t[f"att_row{L}"]).then_inc(ld_att[L], 16)
            sp.dma_start(mask_i[:, 0, :, :], t["mask_q"]).then_inc(ld_mask, 16)
            sp.dma_start(mask_i[:, 1, :, :], t["mask_k"]).then_inc(ld_mask, 16)

            def load_ring(L, w, cols):
                M = mo[L]
                n = ROUTE[L]["ENT"]
                for k in range(RING):
                    if L > 0 and k == 0:
                        sp.wait_ge(mo[L - 1]["y"], UP_AHEAD + 2 * ROUTE[L - 1]["ENT"])
                    sp.dma_start(ring[:, k, 0:cols], w[k, :, :]).then_inc(ring_in[k], 16)
                with sp.Fori(0, n // RING - 1) as i:
                    for k in range(RING):
                        sp.wait_ge(M["y"], 2 * RING * i + 2 * (k + 1) + UP_AHEAD)
                        sp.dma_start(ring[:, k, 0:cols], w[RING * i + RING + k, :, :]).then_inc(ring_in[k], 16)
                for e in range(n - n % RING, n):
                    sp.wait_ge(M["y"], 2 * (e - RING) + 2 + UP_AHEAD)
                    sp.dma_start(ring[:, e % RING, 0:cols], w[e, :, :]).then_inc(ring_in[e % RING], 16)

            def attention(L):
                A, pre = at, {n: (L - 1) * k for n, k in adds.items()}
                for hf in range(NHALF):
                    sp.wait_ge(A["kparts"], pre["kparts"] + hf + 1)
                    for g in range(PARTS):
                        for a in range(PARTS):
                            r = a * PARTS * HD + g * HD
                            sp.dma_start(kst[r:r + HD, :, hf * HALF:(hf + 1) * HALF],
                                         kp[:, g, hf * HALF:(hf + 1) * HALF]).then_inc(at_kst[L][hf], 16)
                for hf in range(NHALF):
                    sp.wait_ge(A["qparts"], pre["qparts"] + hf + 1)
                    for g in range(PARTS):
                        for a in range(PARTS):
                            r = g * PARTS * HD + a * HD
                            sp.dma_start(qst[r:r + HD, :, hf * HALF:(hf + 1) * HALF],
                                         qp[:, g, hf * HALF:(hf + 1) * HALF]).then_inc(at_qst[L][hf], 16)
                for b in range(B):
                    sp.wait_ge(A["nmc"], pre["nmc"] + b + 1)
                    for q in range(TB):
                        sp.dma_start(qst[STACK:SROWS, :, b * S + q * P:b * S + (q + 1) * P],
                                     nmT[q * PARTS * H:(q + 1) * PARTS * H, b, :]).then_inc(at_nmd[b], 16)

            load_ring(0, glu_w[0], GLU_COLS)
            attention(1)
            load_ring(1, glu_w[1], GLU_COLS)
            attention(2)
            load_ring(2, mlp_w[2], MLP_COLS)
            attention(3)
            load_ring(3, mlp_w[3], MLP_COLS)
            sp.wait_ge(x_done, NHALF)
            sp.dma_start(out, x[:, :, :]).then_inc(stored, 16)
            sp.wait_ge(stored, 16)

        @block.gpsimd
        def _(pool):
            pool.memset(mhalf[:, :], -0.5).then_inc(set_pool, 1)
            pool.memset(ones_row[:, :], 1.0).then_inc(set_pool, 1)
            pool.memset(zerob[:, :], 0.0).then_inc(set_pool, 1)
            pool.memset(vall[:, :, :, 8:9], 1.0).then_inc(set_pool, 1)
            pool.memset(vall[:, :, :, 9:32], 0.0).then_inc(set_pool, 1)
            pool.wait_ge(set_pool, 5)
            pool.memset(kst[64:96, :, :], 1.0).then_inc(set_pool, 1)

            def layer_norm(s):
                pool.wait_ge(ln_var, s + 1)
                pool.tensor_tensor(rstd[:, :], veps[:, :], mhalf[:, :], ALU.pow).then_inc(ln_rstd, 1)

            pool.wait_ge(set_pool, 6)
            for s in range(8):
                layer_norm(s)

        @block.tensor
        def _(pe):
            def layer_norm(s):
                for hf in range(NHALF):
                    pe.wait_ge(ln_xn, NT * s + 4 * hf + 4)
                    for k in range(4):
                        mm = pe.transpose(PS[:, 6 + hf, k * P:(k + 1) * P], xn[:, 4 * hf + k, :], ident)
                    mm.then_inc(ln_tr, 1)

            def autocorrelation():
                W = att_w[0]
                dft = consts[:, C_DFT:C_DFT + 2 * S]
                inv = consts[:, C_INV:C_INV + 3 * S]

                def dft_tokens(src, bank, done):
                    for b in range(B):
                        for k in range(TB):
                            mm = pe.matmul(PS[:, bank + b // 2, (b % 2) * S:(b % 2 + 1) * S], src[:, TB * b + k, :],
                                           dft[:, k * S:(k + 1) * S], start=(k == 0), stop=(k == TB - 1))
                    mm.then_inc(done, 1)

                def project(bank, w, done):
                    for f in range(2):
                        for b in range(B):
                            mm = pe.matmul(PS[:, bank + f, b * P:(b + 1) * P],
                                           dft_in[:, b * S + f * P:b * S + (f + 1) * P], w, start=True, stop=True)
                    mm.then_inc(done, 1)

                pe.wait_ge(ld_const, 16)
                pe.wait_ge(ld_ctx, 32)
                dft_tokens(ctx_tok, 0, ac["kin"])
                pe.wait_ge(ac["kine"], 2)
                pe.wait_ge(ld_att[0], 16)
                project(2, W[:, P:2 * P], ac["kfreq"])
                pe.wait_ge(ld_ctx, 32)
                for i in range(NT):
                    mm = pe.matmul(PS[:, 4 + i // 4, (i % 4) * P:(i % 4 + 1) * P], ctx_nat[:, i, :], W[:, 3 * P:4 * P],
                                   start=True, stop=True)
                mm.then_inc(ac["z"], 1)
                pe.wait_ge(ac["ze"], 1)
                for hf in range(NHALF):
                    mm = pe.matmul(PS[:, 6 + hf, :], W[:, 2 * P:3 * P], vo[:, hf * HALF:(hf + 1) * HALF],
                                   start=True, stop=True)
                mm.then_inc(ac["vo"], 1)
                pe.wait_ge(ac["voe"], 1)
                layer_norm(0)
                dft_tokens(xn, 0, ac["qin"])
                pe.wait_ge(ac["qine"], 2)
                project(4, W[:, 0:P], ac["qfreq"])
                pe.wait_ge(ac["prod"], 5)
                for b in range(B):
                    o = PS[:, b // 2, (b % 2) * S:(b % 2 + 1) * S]
                    for n, j in enumerate((0, 1, 4)):
                        mm = pe.matmul(o, prod[:, j, b * P:(b + 1) * P], inv[:, n * S:(n + 1) * S],
                                       start=(n == 0), stop=(n == 2))
                mm.then_inc(ac["corr"], 1)
                pe.wait_ge(ac["mix"], B)
                for b in range(B):
                    mm = pe.transpose(PS[:, 2, b * P:(b + 1) * P], mixT[:, b, :], ident)
                mm.then_inc(ac["mo"], 1)
                pe.wait_ge(ac["moe"], 1)
                for b in range(B):
                    mm = pe.matmul(PS[:, 4 + b // 2, (b % 2) * S:(b % 2 + 1) * S], mixo[:, b * P:(b + 1) * P],
                                   vo[:, b * S:(b + 1) * S], start=True, stop=True)
                mm.then_inc(ac["out"], 1)

            def route(L):
                E = ROUTE[L]["E"]
                if L == 0:
                    pe.wait_ge(ld_route, 16 * 8)
                for i in range(NT):
                    o = PS[:, 2, i * E:(i + 1) * E]
                    if i % 4 == 0:
                        pe.wait_ge(ln_xnT[i // 4], 2 * L + 2)
                    mm = pe.matmul(o, xnT[:, i * P:(i + 1) * P], wr[L][:, :], start=True, stop=(L != 2))
                    if L == 2:
                        mm = pe.matmul(o, ones_row[:, :], br2[:, :], start=False, stop=True)
                mm.then_inc(rt["logits"], 1)
                pe.wait_ge(rt["parts"], L + 1)
                for i in range(NT):
                    mm = pe.transpose(PS[0:PARTS * EP, 3, i * 64:(i + 1) * 64].bitcast(bf16),
                                      wpart[:, i, :, :].rearrange("p a e -> p (a e)"), identb[:, :])
                if L >= 2:
                    for i in range(NT):
                        mm = pe.transpose(PS[0:EP, 4 + i // 4, (i % 4) * P:(i % 4 + 1) * P], wtab[:, i, :], ident)
                mm.then_inc(rt["tr"], 1)
                pe.wait_ge(rt["wT"], L + 1)

            def experts(L, glu):
                M, n = mo[L], ROUTE[L]["ENT"]
                pick = (pick64[:, :, :].rearrange("k e f -> k (e f)") if glu
                        else pick128[:, :, :].rearrange("k e f -> k (e f)"))

                def up(unit, entry, slot, hf, full):
                    if hf == 0:
                        pe.wait_ge(ring_in[slot], full)
                    pe.wait_ge(M["hid"], unit + 1)
                    rhs = xnT[:, hf * HALF:(hf + 1) * HALF]
                    pe.matmul(PS[:, 2 + hf, :], ring[:, slot, 0:P], rhs, start=True, stop=True)
                    if glu:
                        pe.matmul(PS[:, 4 + hf, :], ring[:, slot, P:2 * P], rhs, start=True, stop=True)
                    pe.matmul(PS[:, 6 + hf, :], pick[:, bass.ds(entry * P, P)], wT[:, hf * HALF:(hf + 1) * HALF],
                              start=True, stop=True).then_inc(M["up"], 1)

                def down(unit, slot, hf):
                    pe.wait_ge(M["hid"], unit + 1 + UP_AHEAD)
                    w = ring[:, slot, 2 * P:3 * P] if glu else ring[:, slot, P:2 * P]
                    pe.matmul(PS[:, hf, :], w, hid[:, hf, :], start=False, stop=False,
                              skip_group_check=True).then_inc(M["y"], 1)

                for hf in range(NHALF):
                    if glu:
                        mm = pe.matmul(PS[:, hf, :], zerob[:, 0:P], zerob[:, :], start=True, stop=False,
                                       skip_group_check=True)
                    else:
                        mm = pe.matmul(PS[:, hf, :], b2[L][:, :], wTf[:, hf * HALF:(hf + 1) * HALF], start=True,
                                       stop=False, skip_group_check=True)
                    mm.then_inc(M["y"], 1)
                up(0, 0, 0, 0, 16 * (before[L][0] + 1))
                with pe.Fori(0, groups(n)) as i:
                    for k in range(RING):
                        for hf in range(NHALF):
                            u = 2 * RING * i + 2 * k + hf
                            nk = (k + hf) % RING
                            wrap = (k + hf) // RING
                            up(u + 1, RING * i + k + hf, nk, 1 - hf, 16 * i + 16 * (before[L][nk] + 1 + wrap))
                            down(u, k, hf)
                for e in range(RING * groups(n), n):
                    for hf in range(NHALF):
                        u, ne = 2 * e + hf, e + hf
                        if ne < n:
                            up(u + 1, ne, ne % RING, 1 - hf, 16 * (before[L][ne % RING] + ne // RING + 1))
                        down(u, e % RING, hf)
                pe.wait_ge(M["yT"], NHALF)
                for i in range(NT):
                    mm = pe.transpose(PS[:, 2 + i // 4, (i % 4) * P:(i % 4 + 1) * P], yT[:, i * P:(i + 1) * P], ident)
                    if i % 4 == 3:
                        mm.then_inc(M["ytr"], 1)

            def attention(L):
                A, W, row = at, att_w[L], att_row[L]
                pre = {n: (L - 1) * k for n, k in adds.items()}
                pe.wait_ge(ld_att[L], 32)
                for hf in range(NHALF):
                    if hf == 0:
                        pe.wait_ge(ln_xnT[0], 2 * L + 1)
                    pe.matmul(PS[:, 2 + hf, :], W[:, P:2 * P], ctxT[:, hf * HALF:(hf + 1) * HALF],
                              start=True, stop=True).then_inc(A["k"], 1)
                for hf in range(NHALF):
                    pe.wait_ge(ln_xnT[hf], 2 * L + 1)
                    pe.matmul(PS[:, hf, :], W[:, 0:P], xnT[:, hf * HALF:(hf + 1) * HALF],
                              start=True, stop=True).then_inc(A["q"], 1)
                for i in range(NT):
                    o = PS[:, 4 + i // 4, (i % 4) * P:(i % 4 + 1) * P]
                    pe.matmul(o, ctxT[:, i * P:(i + 1) * P], W[:, 2 * P:3 * P], start=True, stop=False)
                    mm = pe.matmul(o, ones_row[:, :], row[:, 0:P], start=False, stop=True)
                mm.then_inc(A["v"], 1)
                if L == 3:
                    pe.wait_ge(A["vall"], pre["vall"] + 2)
                    pe.wait_ge(masks_ready, 1)
                    for b in range(B):
                        if b >= 2:
                            pe.wait_ge(A["ue"], b - 1)
                        for q in range(TB):
                            for k in range(TB):
                                mm = pe.matmul(PS[:, 6 + b % 2, q * H * 9:(q + 1) * H * 9],
                                               maskedT[:, k, q * P:(q + 1) * P], vall[:, TB * b + k, :, 0:9],
                                               start=(k == 0), stop=(k == TB - 1))
                        mm.then_inc(A["u"], 1)
                    pe.wait_ge(A["ue"], B)
                if L == 2:
                    pe.wait_ge(masks_ready, 1)

                def max_scores(v):
                    b, u = divmod(v, H)
                    q, h0 = divmod(u, H // 2)
                    h0 *= 2
                    if u == 0 and b % 2 == 0:
                        pe.wait_ge(at_kst[L][b // 2], 16 * PARTS * PARTS)
                        pe.wait_ge(at_qst[L][b // 2], 16 * PARTS * PARTS)
                    if v >= 2:
                        pe.wait_ge(A["mx"], pre["mx"] + v - 1)
                    if L >= 2:
                        pe.matmul(PS[:, v % 2, :], identb[:, :],
                                  negq[:, L - 2, q:q + 1, :].broadcast_to([P, 2, S]), start=True, stop=False,
                                  skip_group_check=True)
                    for j in range(2):
                        mm = pe.matmul(PS[:, v % 2, j * S:(j + 1) * S],
                                       qst[0:STACK, h0 + j, b * S + q * P:b * S + (q + 1) * P],
                                       kst[0:STACK, h0 + j, b * S:(b + 1) * S], start=(L == 1), stop=True,
                                       skip_group_check=True)
                    mm.then_inc(A["s"], 1)

                def turn_max(b):
                    pe.wait_ge(A["nmp"], pre["nmp"] + b + 1)
                    if b >= 1:
                        pe.wait_ge(A["nmc"], pre["nmc"] + b)
                    if b >= 2:
                        pe.wait_ge(A["on"], pre["on"] + b - 1)
                    pe.transpose(PS[0:PARTS * H * TB, 6, 0:64].bitcast(bf16),
                                 nmpart[:, b, :, :, :].rearrange("p q a n -> p (q a n)"), identb[:, :]).then_inc(A["nmt"], 1)

                def shifted_scores(w):
                    b, h = divmod(w, H)
                    if h == 0:
                        pe.wait_ge(at_nmd[b], 16 * TB * L)
                    if w >= 2:
                        pe.wait_ge(A["p"], pre["p"] + w - 1)
                    if L >= 2:
                        neg = (negq[:, 0, :, :] if L == 2 else negk[:, :, :]).rearrange("p k n -> p (k n)")
                        pe.matmul(PS[:, 2 + w % 2, :], identb[:, :], neg, start=True, stop=False,
                                  skip_group_check=True)
                    for k in range(TB):
                        mm = pe.matmul(PS[:, 2 + w % 2, k * S:(k + 1) * S],
                                       kst[0:SROWS, h, b * S + k * P:b * S + (k + 1) * P],
                                       qst[0:SROWS, h, b * S:(b + 1) * S], start=(L == 1), stop=True,
                                       skip_group_check=True)
                    mm.then_inc(A["st"], 1)

                def weigh_values(b, g):
                    pe.wait_ge(A["p"], pre["p"] + H * b + 4 * g + 4)
                    if g == 0:
                        if b > 0:
                            pe.wait_ge(A["oe"], pre["oe"] + b)
                        else:
                            pe.wait_ge(A["vall"], pre["vall"] + 2)
                    for k in range(TB):
                        for j in range(4):
                            h = 4 * g + j
                            mm = pe.matmul(PS[32 * j:32 * j + 32, 4 + g // 2, (g % 2) * S:(g % 2 + 1) * S],
                                           vall[:, TB * b + k, h, :], pT[:, (H * b + h) % 8, k * S:(k + 1) * S],
                                           start=(k == 0), stop=(k == TB - 1), skip_group_check=True)
                    mm.then_inc(A["pv"], 1)

                def turn_outputs(b):
                    pe.wait_ge(A["oe"], pre["oe"] + b + 1)
                    pe.wait_ge(A["nmc"], pre["nmc"] + min(b + 2, B))
                    if b >= 1:
                        pe.wait_ge(A["on"], pre["on"] + b)
                    for q in range(TB):
                        for g in range(4):
                            mm = pe.transpose(PS[:, 6 + q, g * P:(g + 1) * P],
                                              oT[:, g * S + q * P:g * S + (q + 1) * P], ident)
                    mm.then_inc(A["ot"], 1)

                pe.wait_ge(A["kf"], pre["kf"] + 4)
                pe.wait_ge(A["qf"], pre["qf"] + 4)
                for p in range(NU + LAG):
                    if p < NU:
                        max_scores(p)
                    if p >= H + 2 and (p - 2) % H == 0 and (p - 2) // H <= B:
                        turn_max((p - 2) // H - 1)
                    w = p - LAG
                    if w >= 0:
                        shifted_scores(w)
                        if w >= 5 and w % 4 == 1:
                            weigh_values(*divmod((w - 5) // 4, 4))
                        if w >= H + 5 and w % H == 5:
                            turn_outputs(w // H - 1)
                weigh_values(B - 1, 3)
                turn_outputs(B - 1)
                pe.wait_ge(A["on"], pre["on"] + B)
                pe.wait_ge(A["mx"], pre["mx"] + NU)
                for i in range(NT):
                    mm = pe.transpose(PS[:, i // 4, (i % 4) * P:(i % 4 + 1) * P], onrm[:, i, :], ident)
                    if i % 4 == 3:
                        mm.then_inc(A["fin_t"], 1)
                pe.wait_ge(A["fin_e"], pre["fin_e"] + 2)
                for hf in range(NHALF):
                    pe.matmul(PS[:, 2 + hf, :], ones_row[:, :], row[:, P:P + HALF], start=True, stop=False,
                              skip_group_check=True)
                    for k in range(4):
                        i = 4 * hf + k
                        mm = pe.matmul(PS[:, 2 + hf, k * P:(k + 1) * P], onT[:, i * P:(i + 1) * P],
                                       W[:, 3 * P:4 * P], start=False, stop=True, skip_group_check=True)
                    mm.then_inc(A["fin"], 1)

            pe.wait_ge(set_pool, 6)
            pe.wait_ge(set_dve, 3)
            autocorrelation()
            layer_norm(1)
            route(0)
            experts(0, True)
            for L in range(1, 4):
                layer_norm(2 * L)
                attention(L)
                layer_norm(2 * L + 1)
                route(L)
                experts(L, L < 2)

        @block.scalar
        def _(act):
            def layer_norm(s):
                act.wait_ge(ln_tr, 2 * s + 1)
                act.activation(xnT[:, 0:HALF], PS[:, 6, :], ACT.Copy).then_inc(ln_xnT[0], 1)

            def route(L):
                SM = ROUTE[L]["SM"]
                act.wait_ge(rt["shift"], L + 1)
                act.activation(probs[:, :, 0:SM], shifted[:, :, 0:SM], ACT.Exp).then_inc(rt["exp"], 1)
                if L == 1:
                    act.activation(zsg[:, :], shifted[:, :, 16], ACT.Exp, scale=-1.0).then_inc(rt["exp"], 1)
                act.wait_ge(rt["tr"], L + 1)
                if L >= 2:
                    act.activation(wTf[:, :], PS[0:EP, 4:6, :].rearrange("p a n -> p (a n)"), ACT.Copy).then_inc(astep, 1)
                    act.wait_ge(astep, L - 1)
                act.activation(wT[:, :], PS[0:PARTS * EP, 3, :].bitcast(bf16), ACT.Copy).then_inc(rt["wT"], 1)

            def experts(L, glu):
                M, n = mo[L], ROUTE[L]["ENT"]
                func = ACT.Silu if glu else (ACT.Gelu if L == 2 else ACT.Relu)

                def unit(u, slot, hf):
                    act.wait_ge(M["up"], u + 1)
                    act.wait_ge(M["gated"] if glu else M["hid"], u + 1)
                    bias = 0.0 if glu else ring[:, slot, 2 * P:2 * P + 1]
                    act.activation(act_out[:, hf, :], PS[:, 2 + hf, :], func, bias=bias).then_inc(M["act"], 1)

                with act.Fori(0, groups(n)) as i:
                    for k in range(RING):
                        for hf in range(NHALF):
                            unit(2 * RING * i + 2 * k + hf, k, hf)
                for e in range(RING * groups(n), n):
                    for hf in range(NHALF):
                        unit(2 * e + hf, e % RING, hf)
                act.wait_ge(M["y"], UP_AHEAD + 2 * n - 1)
                act.activation(yT[:, 0:HALF], PS[:, 0, :], ACT.Copy, scale=gtan[:, 4 + L:5 + L]).then_inc(M["yT"], 1)

            def attention(L):
                A, W, sc = at, att_w[L], SCALE[L]
                pre = {n: (L - 1) * k for n, k in adds.items()}
                for src, dst, parts, bank, done, bias in ((A["k"], kf, kp, 2, A["kf"], 4 * P + 1),
                                                          (A["q"], qf, qp, 0, A["qf"], 4 * P)):
                    for hf in range(NHALF):
                        act.wait_ge(src, 2 * (L - 1) + hf + 1)
                        c = slice(hf * HALF, (hf + 1) * HALF)
                        act.activation(dst[:, c], PS[:, bank + hf, :], ACT.Identity,
                                       bias=W[:, bias:bias + 1]).then_inc(done, 1)
                        act.activation(parts[:, 0, c], PS[:, bank + hf, :], ACT.Identity,
                                       bias=W[:, bias:bias + 1]).then_inc(done, 1)
                act.wait_ge(A["v"], pre["v"] + 1)
                for hf in range(NHALF):
                    act.activation(vall[:, 4 * hf:4 * hf + 4, :, 0:HD],
                                   PS[:, 4 + hf, :].rearrange("p (t h d) -> p t h d", t=4, h=H),
                                   ACT.Copy).then_inc(A["vall"], 1)
                if L == 3:
                    for b in range(B):
                        act.wait_ge(A["u"], b + 1)
                        act.activation(umask[:, b, :, :], PS[:, 6 + b % 2, 0:TB * H * 9].rearrange("p (q n) -> p q n", q=TB),
                                       ACT.Copy).then_inc(A["ue"], 1)

                def copy_max(b):
                    act.wait_ge(A["nmt"], pre["nmt"] + b + 1)
                    act.activation(nmT[:, b, :], PS[0:PARTS * H * TB, 6, 0:64].bitcast(bf16), ACT.Copy).then_inc(A["nmc"], 1)
                    if L == 3:
                        act.activation(emask[:, b, :, :], emask[:, b, :, :], ACT.Exp, scale=sc).then_inc(A["em"], 1)

                def take_outputs(b):
                    act.wait_ge(A["pv"], pre["pv"] + 4 * (b + 1))
                    if b >= 1:
                        act.wait_ge(A["ot"], pre["ot"] + b)
                    act.activation(oT[:, :], banks(4), ACT.Copy).then_inc(A["oe"], 1)

                copy_max(0)
                for w in range(NU):
                    if w % H == H - 5 and w < NU - H:
                        copy_max(w // H + 1)
                    if w >= H + 3 and w % H == 3:
                        take_outputs(w // H - 1)
                    act.wait_ge(A["st"], pre["st"] + w + 1)
                    if w >= 8:
                        act.wait_ge(A["pv"], pre["pv"] + (w - 8) // 4 + 1)
                    act.activation(pT[:, w % 8, :], PS[:, 2 + w % 2, :], ACT.Exp, scale=sc).then_inc(A["p"], 1)
                take_outputs(B - 1)
                act.wait_ge(A["fin_t"], pre["fin_t"] + 1)
                act.activation(onT[:, 0:HALF], PS[:, 0, :], ACT.Copy).then_inc(A["fin_e"], 1)

            act.wait_ge(ac["kin"], 1)
            act.activation(dft_in[:, 0:HALF], PS[:, 0, :], ACT.Copy).then_inc(ac["kine"], 1)
            act.wait_ge(ac["kfreq"], 1)
            act.activation(kfreq[:, 0, :], PS[:, 2, :], ACT.Copy).then_inc(ac["kfe"], 1)
            act.activation(kfreq[:, 1, :], PS[:, 3, :], ACT.Copy).then_inc(ac["kfe"], 1)
            act.wait_ge(ac["z"], 1)
            act.activation(vo[:, :], banks(4), ACT.Copy).then_inc(ac["ze"], 1)
            act.wait_ge(ac["vo"], 1)
            act.activation(vo[:, :], banks(6), ACT.Copy).then_inc(ac["voe"], 1)
            act.wait_ge(ld_gate, 16)
            act.activation(gtan[:, :], gates[:, :], ACT.Tanh).then_inc(gate_ready, 1)
            layer_norm(0)
            act.wait_ge(ac["qin"], 1)
            act.activation(dft_in[:, 0:HALF], PS[:, 0, :], ACT.Copy).then_inc(ac["qine"], 1)
            act.wait_ge(ac["top"], 1)
            act.activation(cw[:, 1, :], cw[:, 0, :], ACT.Exp).then_inc(ac["exp"], 1)
            act.wait_ge(ac["mo"], 1)
            act.activation(mixo, PS[:, 2, :], ACT.Copy).then_inc(ac["moe"], 1)
            layer_norm(1)
            route(0)
            experts(0, True)
            for L in range(1, 4):
                layer_norm(2 * L)
                attention(L)
                layer_norm(2 * L + 1)
                route(L)
                experts(L, L < 2)

        @block.vector
        def _(dve):
            steps = [0]

            def link(ins):
                steps[0] += 1
                ins.then_inc(dstep, 1)
                dve.wait_ge(dstep, steps[0])

            def layer_norm(s):
                for i in range(NT):
                    ins = dve.bn_stats(stats[:, i, :], x[:, i, :])
                    if i < NT - 1:
                        steps[0] += 1
                        ins.then_inc(dstep, 1)
                link(ins)
                for i in range(NT):
                    ins = dve.bn_aggr(mv[:, i, :], stats[:, i, :])
                    if i < NT - 1:
                        steps[0] += 1
                        ins.then_inc(dstep, 1)
                link(ins)
                dve.tensor_scalar(veps[:, :], mv[:, :, 1], LN_EPS, None, ALU.add).then_inc(ln_var, 1)
                dve.wait_ge(ln_rstd, s + 1)
                for i in range(NT):
                    dve.tensor_scalar(xn[:, i, :], x[:, i, :], mv[:, i, 0:1], rstd[:, i:i + 1],
                                      ALU.subtract, ALU.mult).then_inc(ln_xn, 1)
                dve.wait_ge(ln_tr, 2 * s + 2)
                dve.tensor_copy(xnT[:, HALF:N], PS[:, 7, :]).then_inc(ln_xnT[1], 1)

            def add_to_x(bank, g, ready, first):
                for hf in range(NHALF):
                    dve.wait_ge(ready, first + hf)
                    xs = x[:, 4 * hf:4 * hf + 4, :].rearrange("p a n -> p (a n)")
                    if g is None:
                        ins = dve.tensor_tensor(xs, PS[:, bank + hf, :], xs, ALU.add)
                    else:
                        ins = dve.scalar_tensor_tensor(out=xs, in0=PS[:, bank + hf, :], scalar=gtan[:, g:g + 1], in1=xs,
                                                       op0=ALU.mult, op1=ALU.add)
                    link(ins)
                return ins

            def autocorrelation():
                dve.wait_ge(ac["kin"], 1)
                dve.tensor_copy(dft_in[:, HALF:N], PS[:, 1, :]).then_inc(ac["kine"], 1)
                layer_norm(0)
                dve.wait_ge(ac["qin"], 1)
                dve.tensor_copy(dft_in[:, HALF:N], PS[:, 1, :]).then_inc(ac["qine"], 1)
                dve.wait_ge(ac["kfe"], 2)
                dve.wait_ge(ac["qfreq"], 1)
                for j, (qx, kx) in enumerate(((0, 0), (1, 1), (1, 0), (0, 1))):
                    dve.tensor_tensor(prod[:, j, :], PS[:, 4 + qx, :], kfreq[:, kx, :], ALU.mult).then_inc(ac["prod"], 1)
                dve.wait_ge(ac["prod"], 4)
                dve.tensor_tensor(prod[:, 4, :], prod[:, 2, :], prod[:, 3, :], ALU.subtract).then_inc(ac["prod"], 1)
                dve.wait_ge(ac["corr"], 1)
                for b in range(B):
                    c = PS[:, b // 2, (b % 2) * S:(b % 2 + 1) * S]
                    link(dve.max(corr8[:, b, :], c))
                    link(dve.max_index(lag8[:, b, :], corr8[:, b, :], c))
                top = corr8[:, :, 0:TOPLAGS]
                w0, w1, w2, w3 = (cw[:, j, :].rearrange("p (b i) -> p b i", b=B) for j in range(4))
                dve.tensor_tensor(w0, top, corr8[:, :, 0:1].broadcast_to([P, B, TOPLAGS]), ALU.subtract).then_inc(ac["top"], 1)
                link(dve.tensor_scalar(roll_i[:, 0, :].rearrange("p (b i) -> p b i", b=B), lag8[:, :, 0:TOPLAGS], -1.0,
                                       consts[:, C_DPOS:C_DPOS + 1], ALU.mult, ALU.add))
                link(dve.tensor_scalar(roll_i[:, 1, :], roll_i[:, 0, :], HD - 1, None, ALU.bitwise_and))
                dve.wait_ge(ac["exp"], 1)
                link(dve.tensor_reduce(csum[:, 0, :], w1, AX.X, ALU.add))
                link(dve.reciprocal(csum[:, 1, :], csum[:, 0, :]))
                link(dve.tensor_tensor(w2, w1, csum[:, 1, :].unsqueeze(2).broadcast_to([P, B, TOPLAGS]), ALU.mult))
                link(dve.tensor_tensor(sel[:, :, :], roll_i[:, 1, :].unsqueeze(2).broadcast_to([P, B * TOPLAGS, HD]),
                                       consts[:, C_IOTA:C_IOTA + HD].unsqueeze(1).broadcast_to([P, B * TOPLAGS, HD]),
                                       ALU.is_equal))
                link(dve.tensor_tensor(sel[:, :, :], sel[:, :, :],
                                       cw[:, 2, :].unsqueeze(2).broadcast_to([P, B * TOPLAGS, HD]), ALU.mult))
                link(dve.tensor_reduce(mix8[:, :, :], sel[:, :, :].rearrange("p (b i) r -> p b r i", b=B), AX.X, ALU.add))
                for b in range(B):
                    dve.tensor_tensor(mixT[:, b, :].rearrange("p (h r) -> p h r", h=H),
                                      mix8[:, b:b + 1, :].broadcast_to([P, H, HD]),
                                      consts[:, C_BLK:C_BLK + H].unsqueeze(2).broadcast_to([P, H, HD]),
                                      ALU.mult).then_inc(ac["mix"], 1)
                dve.wait_ge(ac["out"], 1)
                dve.wait_ge(gate_ready, 1)
                add_to_x(4, 0, ac["out"], 0)

            def route(L):
                r = ROUTE[L]
                E, SM, K = r["E"], r["SM"], r["K"]
                dve.wait_ge(rt["logits"], L + 1)
                lg = PS[:, 2, 0:NT * E].rearrange("p (t e) -> p t e", t=NT)
                link(dve.tensor_reduce(rmax[:, :], lg[:, :, 0:SM], AX.X, ALU.max))
                if L == 1:
                    link(dve.tensor_copy(shifted[:, :, 16], lg[:, :, 16]))
                dve.tensor_tensor(shifted[:, :, 0:SM], lg[:, :, 0:SM],
                                  rmax[:, :].unsqueeze(2).broadcast_to([P, NT, SM]), ALU.subtract).then_inc(rt["shift"], 1)
                dve.wait_ge(rt["exp"], L + 1 + (L >= 1))
                link(dve.tensor_reduce(rsum[:, :], probs[:, :, 0:SM], AX.X, ALU.add))
                link(dve.reciprocal(rrec[:, :], rsum[:, :]))
                link(dve.tensor_tensor(probs[:, :, 0:SM], probs[:, :, 0:SM],
                                       rrec[:, :].unsqueeze(2).broadcast_to([P, NT, SM]), ALU.mult))
                ranking = probs
                if L == 0:
                    ranking = ranked
                    link(dve.tensor_tensor(ranked[:, :, 0:SM], probs[:, :, 0:SM],
                                           cbias[:, :].unsqueeze(1).broadcast_to([P, NT, SM]), ALU.add))
                for i in range(NT):
                    ins = dve.max(top8[:, i, :], ranking[:, i, 0:SM])
                    if i < NT - 1:
                        steps[0] += 1
                        ins.then_inc(dstep, 1)
                link(ins)
                link(dve.memset(top8[:, :, K:8], FLAG))
                for i in range(NT):
                    ins = dve.match_replace(out=flagged[:, i, 0:SM], in_to_replace=top8[:, i, :],
                                            in_values=ranking[:, i, 0:SM], imm_value=FLAG)
                    if i < NT - 1:
                        steps[0] += 1
                        ins.then_inc(dstep, 1)
                link(ins)
                link(dve.scalar_tensor_tensor(out=picked[:, :, 0:SM], in0=flagged[:, :, 0:SM], scalar=FLAG,
                                              in1=probs[:, :, 0:SM], op0=ALU.is_equal, op1=ALU.mult))
                if L == 0:
                    link(dve.tensor_scalar(wtab[:, :, :], picked[:, :, 0:R_REAL], 2.5, None, ALU.mult))
                    link(dve.tensor_reduce(rsum[:, :], picked[:, :, R_REAL:SM], AX.X, ALU.add))
                    link(dve.tensor_scalar(gzero[:, :], rsum[:, :], 2.5, gtan[:, 4:5], ALU.mult, ALU.mult))
                elif L == 1:
                    link(dve.memset(wtab[:, :, SM + 2 * SHARED_TILES:EP], 0.0))
                    link(dve.tensor_reduce(rsum[:, :], picked[:, :, 0:SM], AX.X, ALU.add))
                    link(dve.reciprocal(rrec[:, :], rsum[:, :]))
                    link(dve.tensor_tensor(wtab[:, :, 0:SM], picked[:, :, 0:SM],
                                           rrec[:, :].unsqueeze(2).broadcast_to([P, NT, SM]), ALU.mult))
                    link(dve.tensor_scalar(rsum[:, :], zsg[:, :], 1.0, None, ALU.add))
                    link(dve.reciprocal(rrec[:, :], rsum[:, :]))
                    link(dve.tensor_copy(wtab[:, :, SM:SM + 2 * SHARED_TILES],
                                         rrec[:, :].unsqueeze(2).broadcast_to([P, NT, 2 * SHARED_TILES])))
                elif L == 2:
                    link(dve.tensor_copy(wtab[:, :, 0:SM], picked[:, :, 0:SM]))
                    link(dve.memset(wtab[:, :, SM:EP], 1.0))
                else:
                    link(dve.memset(wtab[:, :, 2 * SM:EP], 0.0))
                    for i in range(2):
                        link(dve.tensor_copy(wtab[:, :, i:2 * SM:2], picked[:, :, 0:SM]))
                link(dve.tensor_copy(wpart[:, :, 0, :], wtab[:, :, :]))
                link(dve.tensor_tensor(wrest[:, :, :], wtab[:, :, :], wpart[:, :, 0, :], ALU.subtract))
                link(dve.tensor_copy(wpart[:, :, 1, :], wrest[:, :, :]))
                dve.tensor_tensor(wpart[:, :, 2, :], wrest[:, :, :], wpart[:, :, 1, :], ALU.subtract).then_inc(rt["parts"], 1)

            def experts(L, glu):
                M, n = mo[L], ROUTE[L]["ENT"]
                if glu:
                    dve.sem_inc(M["gated"], UP_AHEAD)
                dve.sem_inc(M["hid"], UP_AHEAD)
                if L == 0:
                    for i in range(NT):
                        link(dve.scalar_tensor_tensor(out=x[:, i, :], in0=xn[:, i, :], scalar=gzero[:, i:i + 1],
                                                      in1=x[:, i, :], op0=ALU.mult, op1=ALU.add))
                if L == 2:
                    link(dve.scalar_tensor_tensor(out=x[:, :, :], in0=xn[:, :, :], scalar=gtan[:, 4 + L:5 + L],
                                                  in1=x[:, :, :], op0=ALU.mult, op1=ALU.add))

                def unit(u, hf):
                    dve.wait_ge(M["act"], u + 1)
                    src = act_out
                    if glu:
                        dve.tensor_tensor(gated[:, hf, :], act_out[:, hf, :], PS[:, 4 + hf, :],
                                          ALU.mult).then_inc(M["gated"], 1)
                        dve.wait_ge(M["gated"], u + 1 + UP_AHEAD)
                        src = gated
                    dve.wait_ge(M["y"], u + 1)
                    dve.tensor_tensor(hid[:, hf, :], src[:, hf, :], PS[:, 6 + hf, :], ALU.mult).then_inc(M["hid"], 1)

                with dve.Fori(0, groups(n)) as i:
                    for k in range(RING):
                        for hf in range(NHALF):
                            unit(2 * RING * i + 2 * k + hf, hf)
                for u in range(2 * RING * groups(n), 2 * n):
                    unit(u, u % 2)
                dve.wait_ge(M["y"], UP_AHEAD + 2 * n)
                dve.tensor_scalar(yT[:, HALF:N], PS[:, 1, :], gtan[:, 4 + L:5 + L], None, ALU.mult).then_inc(M["yT"], 1)
                if L < 3:
                    add_to_x(2, None, M["ytr"], 1)
                else:
                    for hf in range(NHALF):
                        dve.wait_ge(M["ytr"], hf + 1)
                        xs = x[:, 4 * hf:4 * hf + 4, :].rearrange("p a n -> p (a n)")
                        dve.tensor_tensor(xs, PS[:, 2 + hf, :], xs, ALU.add).then_inc(x_done, 1)

            def prepare_masks():
                dve.wait_ge(ld_const, 16)
                dve.wait_ge(ld_mask, 32)
                link(dve.tensor_copy(negq[:, 0, :, :].rearrange("p k n -> p (k n)"), consts[:, C_BAND:C_BAND + TB * S]))
                link(dve.tensor_scalar(negq[:, 1, :, :], mask_i[:, 0, :, :], 0.0, NEG, ALU.is_equal, ALU.mult))
                link(dve.tensor_scalar(negk[:, :, :], mask_i[:, 1, :, :], 0.0, NEG, ALU.is_equal, ALU.mult))
                link(dve.tensor_scalar(maskedT[:, :, :], mask_i[:, 1, :, :], 0.0, None, ALU.is_equal))
                link(dve.tensor_scalar(maskq_f, mask_i[:, 0, :, :], 0.0, None, ALU.is_equal))
                link(dve.tensor_reduce(negfloor[:, :], maskq_f, AX.X, ALU.max))
                dve.tensor_scalar(negfloor[:, :], negfloor[:, :], -3.0e37, 3.0e37, ALU.mult, ALU.add).then_inc(dstep, 1)
                steps[0] += 1
                dve.wait_ge(dstep, steps[0])
                dve.tensor_scalar(negfloor[:, :], negfloor[:, :], -MASKED / SCALE[3], None, ALU.max).then_inc(masks_ready, 1)

            maskq_f = onT[:, 0:TB * S].rearrange("p (k n) -> p k n", k=TB)

            def attention(L):
                A, pre = at, {n: (L - 1) * k for n, k in adds.items()}
                for f, parts, ready, done in ((kf, kp, A["kf"], A["kparts"]), (qf, qp, A["qf"], A["qparts"])):
                    for hf in range(NHALF):
                        c = slice(hf * HALF, (hf + 1) * HALF)
                        dve.wait_ge(ready, 4 * (L - 1) + 2 * hf + 2)
                        link(dve.tensor_tensor(rest[:, :], f[:, c], parts[:, 0, c], ALU.subtract))
                        link(dve.tensor_copy(parts[:, 1, c], rest[:, :]))
                        dve.tensor_tensor(parts[:, 2, c], rest[:, :], parts[:, 1, c], ALU.subtract).then_inc(done, 1)
                        dve.wait_ge(done, 2 * (L - 1) + hf + 1)

                def split_max(b):
                    nm = negmax[:, b, :, :]
                    if L == 3:
                        for q in range(TB):
                            link(dve.tensor_scalar(negmax[:, b, q, :], negmax[:, b, q, :], negfloor[:, q:q + 1], None,
                                                   ALU.min))
                        link(dve.tensor_scalar(emask[:, b, :, :], negmax[:, b, :, :], MASKED / SCALE[3], 0.0,
                                               ALU.add, ALU.min))
                    link(dve.tensor_copy(nmpart[:, b, :, 0, :], nm))
                    link(dve.tensor_tensor(nmrest[:, :, :], nm, nmpart[:, b, :, 0, :], ALU.subtract))
                    link(dve.tensor_copy(nmpart[:, b, :, 1, :], nmrest[:, :, :]))
                    dve.tensor_tensor(nmpart[:, b, :, 2, :], nmrest[:, :, :], nmpart[:, b, :, 1, :], ALU.subtract).then_inc(A["nmp"], 1)

                def normalise(b):
                    dve.wait_ge(A["ot"], pre["ot"] + b + 1)
                    o = PS[:, 6:8, :].rearrange("p q (h c) -> p q h c", h=H)[:, :, :, 0:9]
                    if L == 3:
                        dve.wait_ge(A["em"], b + 1)
                        for q in range(TB):
                            link(dve.tensor_tensor(ocor[:, q, :, :],
                                                   umask[:, b, q, :].rearrange("p (h c) -> p h c", h=H),
                                                   emask[:, b, q, :].unsqueeze(2).broadcast_to([P, H, 9]), ALU.mult))
                        link(dve.tensor_tensor(ocomb[:, :, :, :], o, ocor[:, :, :, :], ALU.add))
                        o = ocomb[:, :, :, :]
                    link(dve.reciprocal(orec[:, :, :], o[:, :, :, 8]))
                    for q in range(TB):
                        ins = dve.tensor_tensor(onrm[:, TB * b + q, :].rearrange("p (h d) -> p h d", h=H),
                                                o[:, q, :, 0:HD], orec[:, q, :].unsqueeze(2).broadcast_to([P, H, HD]),
                                                ALU.mult)
                        if q < TB - 1:
                            link(ins)
                    ins.then_inc(A["on"], 1)

                done_norm = 0
                for v in range(NU):
                    b, u = divmod(v, H)
                    q, h0 = divmod(u, H // 2)
                    dve.wait_ge(A["s"], pre["s"] + v + 1)
                    dve.tensor_reduce(negmax[:, b, q, 2 * h0:2 * h0 + 2], PS[:, v % 2, :].rearrange("p (h k) -> p h k", h=2),
                                      AX.X, ALU.max, negate=True).then_inc(A["mx"], 1)
                    if u == H - 1:
                        dve.wait_ge(A["mx"], pre["mx"] + v + 1)
                        split_max(b)
                    if v >= LAG + H + 6 and (v - LAG) % H == 6:
                        normalise(done_norm)
                        done_norm += 1
                for b in range(done_norm, B):
                    normalise(b)
                dve.wait_ge(A["fin_t"], pre["fin_t"] + 2)
                dve.tensor_copy(onT[:, HALF:N], PS[:, 1, :]).then_inc(A["fin_e"], 1)
                add_to_x(2, L, A["fin"], pre["fin"] + 1)

            dve.memset(cw[:, 3, :], 0.0).then_inc(set_dve, 1)
            dve.wait_ge(ld_const, 16)
            dve.tensor_copy(identb[:, :], ident).then_inc(set_dve, 1)
            id3 = consts[0:PARTS * EP, C_ID3:C_ID3 + EP]
            dve.tensor_copy(pick64[:, :, :], id3.unsqueeze(2).broadcast_to([PARTS * EP, EP, P // 2])).then_inc(set_dve, 1)
            dve.wait_ge(ld_x, 16)
            autocorrelation()
            layer_norm(1)
            route(0)
            experts(0, True)
            link(dve.tensor_copy(pick128[:, :, :], id3.unsqueeze(2).broadcast_to([PARTS * EP, EP, P])))
            prepare_masks()
            for L in range(1, 4):
                layer_norm(2 * L)
                attention(L)
                layer_norm(2 * L + 1)
                route(L)
                experts(L, L < 2)


def constants():
    c = np.zeros((P, C_ALL), np.float32)
    c[:, C_ID:C_ID + P] = np.eye(P)
    time, freq = np.arange(S), np.arange(P)
    angle = 2 * np.pi * np.outer(time, freq) / S
    nyq = (-1.0) ** time
    fwd = np.concatenate([np.cos(angle), np.sin(angle)], 1)
    fwd[:, P] = nyq
    c[:, C_DFT:C_DFT + 2 * S] = fwd.reshape(P, TB, 2 * P).reshape(P, -1)
    two = np.where(freq == 0, 1.0, 2.0)[:, None] / S
    icos, isin = two * np.cos(angle.T), two * np.sin(angle.T)
    icos2 = icos.copy()
    icos2[0] = nyq / S
    c[:, C_INV:C_INV + 3 * S] = np.concatenate([icos, icos2, isin], 1)
    c[:, C_BLK:C_BLK + H] = np.tile(np.eye(H), (HD, 1))
    c[:, C_DPOS] = np.arange(P) // H + S
    c[:, C_IOTA:C_IOTA + HD] = np.arange(HD)
    c[:PARTS * EP, C_ID3:C_ID3 + EP] = np.tile(np.eye(EP), (PARTS, 1))
    band = np.where(np.abs(np.subtract.outer(time, time)) <= BAND, 0.0, NEG)
    c[:, C_BAND:] = interleave(band)
    return c


def interleave(m):
    m = m.reshape(P, TB, P, TB)
    return m.transpose(0, 1, 3, 2).reshape(P, TB * S)


def tokens_on_partitions(a):
    return a.reshape(B, P, TB, D).transpose(1, 0, 2, 3).reshape(P, NT, D)


def arrays(i):
    i = {k: np.asarray(v) for k, v in i.items()}
    f = np.float32
    heads_minor = np.arange(P).reshape(H, HD).T.reshape(-1)
    col = lambda v: v.reshape(-1, 1)
    zero = np.zeros((P, 1), f)
    a = {"x": tokens_on_partitions(i["x"]), "ctx_tok": tokens_on_partitions(i["ctx_1024"]),
         "ctx_nat": i["ctx_1024"].reshape(NT, P, D).transpose(1, 0, 2),
         "ctxT": tokens_on_partitions(i["ctx_1024"]).transpose(2, 1, 0).reshape(D, N), "consts": constants(),
         "gates": np.concatenate([i["g_xattn"], i["g_ffn"]])}
    a["att_w0"] = np.concatenate([i["L0_xattn_wq"][:, heads_minor], i["L0_xattn_wk"][:, heads_minor], i["L0_xattn_wv"], i["L0_xattn_wo"], zero, zero], 1)
    wkv = i["L2_xattn_w_kv"]
    att = {1: (i["L1_xattn_Wq"].T, i["L1_xattn_Wk"].T, i["L1_xattn_Wv"].T, i["L1_xattn_Wo"].T, i["L1_xattn_bq"],
               i["L1_xattn_bk"], i["L1_xattn_bv"], i["L1_xattn_bo"]),
           2: (i["L2_xattn_w_q"], np.tile(wkv[:, :HD], (1, H)), np.tile(wkv[:, HD:], (1, H)), i["L2_xattn_w_o"],
               zero[:, 0], zero[:, 0], zero[:, 0], zero[:, 0]),
           3: (i["L3_xattn_wq"].T, i["L3_xattn_wk"].T, i["L3_xattn_wv"].T, i["L3_xattn_wo"].T, i["L3_xattn_bq"],
               i["L3_xattn_bk"], i["L3_xattn_bv"], i["L3_xattn_bo"])}
    for L, (wq, wk, wv, wo, bq, bk, bv, bo) in att.items():
        a[f"att_w{L}"] = np.concatenate([wq[:, heads_minor], wk[:, heads_minor], wv, wo, col(bq[heads_minor]),
                                         col(bk[heads_minor])], 1)
        a[f"att_row{L}"] = np.concatenate([bv, np.tile(bo, HALF // D)])[None]
    a["wr0"] = i["L0_ffn_classifier_weight"].T
    a["wr1"] = np.concatenate([i["L1_ffn_gate_w"], i["L1_ffn_shared_gate_w"]]).T
    a["wr2"], a["wr3"] = i["L2_ffn_Wr"], i["L3_ffn_Wg"]
    a["br2"] = i["L2_ffn_br"][None]
    a["cbias"] = i["L0_ffn_e_score_correction_bias"]

    def glu(gate, up, down):
        pair = lambda w: w.reshape(-1, P, D)
        return np.concatenate([pair(gate).transpose(0, 2, 1), pair(up).transpose(0, 2, 1), pair(down)], 2)

    gu = i["L0_ffn_gate_up_proj"][:R_REAL]
    a["glu0"] = glu(gu[:, :64], gu[:, 64:], i["L0_ffn_down_proj"].transpose(0, 2, 1))
    gu = i["L1_ffn_w_gate_up"].transpose(0, 2, 1)
    pad = lambda w: np.concatenate([w, np.zeros((SHARED_TILES * P - w.shape[0], D), f)]).reshape(-1, 64, D)
    a["glu1"] = np.concatenate([
        glu(gu[:, :64], gu[:, 64:], i["L1_ffn_w_down"]),
        glu(pad(i["L1_ffn_shared_w_gate"]), pad(i["L1_ffn_shared_w_up"]), pad(i["L1_ffn_shared_w_down"].T))])
    a["mlp2"] = np.concatenate([np.concatenate([i["L2_ffn_We1"], i["L2_ffn_ws1"][None]]),
                                np.concatenate([i["L2_ffn_We2"], i["L2_ffn_ws2"][None]]),
                                np.concatenate([i["L2_ffn_Be1"], i["L2_ffn_bs1"][None]])[:, :, None]], 2)
    a["b2_2"] = np.concatenate([i["L2_ffn_Be2"], i["L2_ffn_bs2"][None]])
    w1 = i["L3_ffn_W1"].reshape(8, D, 2, P).transpose(0, 2, 1, 3).reshape(16, D, P)
    a["mlp3"] = np.concatenate([w1, i["L3_ffn_W2"].reshape(16, P, D), i["L3_ffn_b1"].reshape(16, P, 1)], 2)
    b23 = np.zeros((EP, P), f)
    b23[0:16:2] = i["L3_ffn_b2"]
    a["b2_3"] = b23
    m = i["mask_1x1xSxS2_ik1"].reshape(S, S)
    a["mask_q"] = interleave(m).reshape(P, TB, S)
    a["mask_k"] = interleave(m.T).reshape(P, TB, S)
    return {k: np.ascontiguousarray(v) for k, v in a.items()}


def kernel(**inputs):
    import concourse.bacc as bacc
    from concourse.bass_utils import run_bass_kernel_spmd

    nc = bacc.Bacc("TRN2", target_bir_lowering=False, num_devices=1)
    data = arrays(inputs)
    t = {k: nc.dram_tensor(f"in_{k}", v.shape, mybir.dt.from_np(v.dtype), kind="ExternalInput").ap()
         for k, v in data.items()}
    out = nc.dram_tensor("out_x", (P, NT, D), mybir.dt.float32, kind="ExternalOutput").ap()
    build(nc, t, out)
    r = run_bass_kernel_spmd(nc, [{f"in_{k}": v for k, v in data.items()}], core_ids=[0])
    got = np.asarray(r.results[0]["out_x"])
    return got.reshape(P, B, TB, D).transpose(1, 0, 2, 3).reshape(B, S, D)
```

```python
from contextlib import ExitStack

import numpy as np
import concourse.bass as bass
from concourse import mybir

B, S, D, H, HD = 4, 256, 128, 16, 8
N = B * S
P = 128
NT = N // P
TB = S // P
NHALF, HALF = 2, 512
PARTS = 3
PAIRS = ((0, 0), (0, 1), (1, 0), (1, 1), (0, 2), (2, 0))
KROWS = 96
SROWS = KROWS + PARTS
TOPLAGS = 5
BAND = 32
EP = 32
RING = 4
NEG = -1.0e30
FLAG = -3.0e38
LN_EPS = 1e-5
MASKED = -10000.0

ROUTE = [dict(E=40, SM=40, K=6, ENT=16), dict(E=17, SM=16, K=2, ENT=11),
         dict(E=31, SM=31, K=3, ENT=32), dict(E=8, SM=8, K=2, ENT=16)]
GLU_COLS, MLP_COLS = 3 * P, 2 * P + 1
R_REAL = 32
SHARED_TILES = 3
SCALE = [None, 1.0 / HD ** 0.5, 1.0, 1.0 / HD ** 0.5]

C_ID, C_DFT, C_INV, C_BLK, C_DPOS, C_IOTA, C_ID3, C_BAND = 0, 128, 640, 1408, 1424, 1425, 1433, 1465
C_ALL = C_BAND + TB * S


def build(nc, t, out):
    f32, bf16, i32, u32 = mybir.dt.float32, mybir.dt.bfloat16, mybir.dt.int32, mybir.dt.uint32
    ALU, ACT, AX = mybir.AluOpType, mybir.ActivationFunctionType, mybir.AxisListType
    ctx = ExitStack()
    with ctx:
        def sb(name, shape, dt=f32):
            return ctx.enter_context(nc.sbuf_tensor(name, shape, dt))

        def sem(name):
            return ctx.enter_context(nc.semaphore(name))

        x = sb("x_res", [P, NT, D])
        xn = sb("xn", [P, NT, D])
        xnT = sb("xnT", [P, N])
        ctx_tok = sb("ctx_tok", [P, NT, D])
        ctxT = sb("ctxT", [P, N])
        consts = sb("consts", [P, C_ALL])
        ident = consts[:, C_ID:C_ID + P]
        identb = sb("identb", [P, P], bf16)
        ones_row = sb("ones_row", [1, P])
        zerob = sb("zerob", [P, HALF], bf16)
        pick64 = sb("pick64", [PARTS * EP, EP, P // 2], bf16)
        pick128 = sb("pick128", [PARTS * EP, EP, P], bf16)
        gates = sb("gates", [P, 8])
        gtan = sb("gtan", [P, 8])
        warm = sb("warm", [P, 1])
        stats = sb("stats", [P, NT, 6])
        mv = sb("mv", [P, NT, 2])
        veps = sb("veps", [P, NT])
        mhalf = sb("mhalf", [P, NT])
        rstd = sb("rstd", [P, NT])
        att_w = [sb(f"att_w{L}", [P, 4 * P + 2]) for L in range(4)]
        att_row = [None] + [sb(f"att_row{L}", [1, P]) for L in range(1, 4)]
        bo = {L: sb(f"bo{L}", [P, P]) for L in (1, 3)}
        wr = [sb(f"wr{L}", [P, ROUTE[L]["E"]]) for L in range(4)]
        br2 = sb("br2", [1, ROUTE[2]["E"]])
        cbias = sb("cbias", [P, ROUTE[0]["E"]])
        b2 = {2: sb("b2_2", [EP, P]), 3: sb("b2_3", [EP, P])}
        rmax = sb("rmax", [P, NT])
        rsum = sb("rsum", [P, NT])
        rrec = sb("rrec", [P, NT])
        shifted = sb("shifted", [P, NT, 40])
        probs = sb("probs", [P, NT, 40])
        ranked = shifted
        flagged = sb("flagged", [P, NT, 40])
        picked = sb("picked", [P, NT, 40])
        top8 = sb("top8", [P, NT, 8])
        gzero = sb("gzero", [P, NT])
        zsg = sb("zsg", [P, NT])
        wtab = sb("wtab", [P, NT, EP])
        wrest = sb("wrest", [P, NT, EP])
        wpart = sb("wpart", [P, NT, PARTS, EP], bf16)
        wT = sb("wT", [PARTS * EP, N], bf16)
        ring = sb("ring", [P, RING, GLU_COLS])
        qf, kf = sb("qf", [P, N]), sb("kf", [P, N])
        qp, kp = sb("qp", [P, PARTS, N], bf16), sb("kp", [P, PARTS, N], bf16)
        rest = sb("rest", [P, HALF])
        qst, kst = sb("qst", [P, H, N], bf16), sb("kst", [P, H, N], bf16)
        vall = sb("vall", [P, NT, H, 32])
        pT = sb("pT", [P, 8, 2 * S])
        negmax = sb("negmax", [P, B, TB, H])
        nmrest = sb("nmrest", [P, TB, 4])
        nmpart = sb("nmpart", [P, 4 * B, TB, PARTS, 4], bf16)
        nmT = sb("nmT", [TB * PARTS * 4, 4 * B, P], bf16)
        oT = sb("oT", [P, 4 * S])
        orec = sb("orec", [P, TB, H])
        ocor = sb("ocor", [P, TB, H, 9])
        ocomb = sb("ocomb", [P, TB, H, 9])
        emask = sb("emask", [P, B, TB, H])
        onrm = xn
        onT = qf
        act_out, gated, hid = pT[:, 0:2, :], pT[:, 2:4, :], pT[:, 4:6, :]
        yT = oT
        wTf = qf[0:EP, :]
        mask_i = oT[:, :].bitcast(i32).rearrange("p (a k n) -> p a k n", a=2, k=TB)
        negq = ctx_tok[:, 4:8, :].rearrange("p a n -> p (a n)").bitcast(bf16).rearrange("p (a k n) -> p a k n", a=2, k=TB)
        negk = sb("negk", [P, TB, S], bf16)
        maskedT = ctx_tok[:, 0:4, :].rearrange("p a n -> p (a n)").rearrange("p (k n) -> p k n", k=TB)
        umask = consts[:, C_DFT:C_DFT + B * TB * H * 9].rearrange("p (b q n) -> p b q n", b=B, q=TB)
        negfloor = sb("negfloor", [P, TB])
        dft_in = kf
        kfreq = qf[:, :].rearrange("p (a n) -> p a n", a=2)
        prod = pT[:, 0:5, :]
        corr8 = sb("corr8", [P, B, 8])
        lag8 = sb("lag8", [P, B, 8], u32)
        cw = sb("cw", [P, 4, B * TOPLAGS])
        csum = sb("csum", [P, 2, B])
        roll_i = sb("roll_i", [P, 2, B * TOPLAGS], i32)
        sel = sb("sel", [P, B * TOPLAGS, HD])
        mix8 = sb("mix8", [P, B, HD])
        mixT = pT[:, 6, :].rearrange("p (b n) -> p b n", b=B)
        mixo = pT[:, 7, :]
        vo = oT
        ctx_nat = kp[:, 0:2, :].rearrange("p a n -> p (a n)").bitcast(f32).rearrange("p (t d) -> p t d", t=NT)

        PS = ctx.enter_context(nc.psum_tensor("PS", [P, 8, HALF], f32))

        def banks(a, n=2):
            return PS[:, a:a + n, :].rearrange("p a n -> p (a n)")

        ld_x, ld_ctx, ld_ctxT, ld_const, ld_gate = sem("ld_x"), sem("ld_ctx"), sem("ld_ctxT"), sem("ld_const"), sem("ld_gate")
        ld_att = [sem(f"ld_att{L}") for L in range(4)]
        ld_route = sem("ld_route")
        ld_mask = sem("ld_mask")
        stored = sem("stored")
        set_pool, set_dve, gate_ready = sem("set_pool"), sem("set_dve"), sem("gate_ready")
        dstep, astep = sem("dstep"), sem("astep")
        ln_var, ln_rstd, ln_xn, ln_tr, ln_xnT = sem("ln_var"), sem("ln_rstd"), sem("ln_xn"), sem("ln_tr"), [sem("ln_xnT0"), sem("ln_xnT1")]
        masks_ready, stacks_set, kstep, biased = (sem(n) for n in ("masks_ready", "stacks_set", "kstep", "biased"))
        ac = {n: sem("ac_" + n) for n in ("kin", "kine", "kfreq", "kfe", "qin", "qine", "qfreq", "prod", "corr", "top",
                                          "exp", "mix", "mo", "moe", "z", "ze", "vo", "voe", "out")}
        adds = dict(q=2, k=2, v=1, kf=4, qf=4, kparts=2, qparts=2, vall=2, s=B * H, mx=B * H, nmp=4 * B, nmt=4 * B, nmc=4 * B,
                    st=B * H, p=B * H, pv=4 * B, oe=B, ot=B, on=B, fin_t=2, fin_e=2, fin=2)
        at = {n: sem(f"at_{n}") for n in (*adds, "u", "ue", "em")}
        at_kst = [None] + [[sem(f"at{L}_kst{h}") for h in range(NHALF)] for L in range(1, 4)]
        at_qst = [None] + [[sem(f"at{L}_qst{h}") for h in range(NHALF)] for L in range(1, 4)]
        at_nmd = [sem(f"at_nmd{g}") for g in range(4)]
        rt = {n: sem("rt_" + n) for n in ("logits", "shift", "exp", "parts", "tr", "wT", "wTf")}
        ring_in = [sem(f"ring_in{k}") for k in range(RING)]
        mo = [{n: sem(f"mo{L}_{n}") for n in ("up", "spread", "act", "gated", "hid", "y", "yT", "ytr")} for L in range(4)]
        x_done = sem("x_done")

        block = ctx.enter_context(nc.Block())
        glu_w = {0: t["glu0"], 1: t["glu1"]}
        mlp_w = {2: t["mlp2"], 3: t["mlp3"]}
        before = [[sum(len(range(k, ROUTE[M]["ENT"], RING)) for M in range(L)) for k in range(RING)] for L in range(4)]
        UP_AHEAD = 2
        LAG = 12
        NU = B * H

        def groups(entries):
            return (entries - 1) // RING

        @block.sync
        def _(sp):
            sp.dma_start(x[:, :, :], t["x"]).then_inc(ld_x, 16)
            sp.dma_start(consts[:, :], t["consts"]).then_inc(ld_const, 16)
            sp.dma_start(ctx_tok[:, :, :], t["ctx_tok"]).then_inc(ld_ctx, 16)
            sp.dma_start(ctx_nat[:, :, :], t["ctx_nat"]).then_inc(ld_ctx, 16)
            sp.dma_start(ctxT[:, :], t["ctxT"]).then_inc(ld_ctxT, 16)
            sp.dma_start(att_w[0][:, :], t["att_w0"]).then_inc(ld_att[0], 16)
            sp.dma_start(gates[:, :], t["gates"].partition_broadcast(P)).then_inc(ld_gate, 16)
            for L in range(4):
                sp.dma_start(wr[L][:, :], t[f"wr{L}"]).then_inc(ld_route, 16)
            sp.dma_start(br2[:, :], t["br2"]).then_inc(ld_route, 16)
            sp.dma_start(cbias[:, :], t["cbias"].partition_broadcast(P)).then_inc(ld_route, 16)
            for L in (2, 3):
                sp.dma_start(b2[L][:, :], t[f"b2_{L}"]).then_inc(ld_route, 16)
            for L in range(1, 4):
                sp.dma_start(att_w[L][:, :], t[f"att_w{L}"]).then_inc(ld_att[L], 16)
                sp.dma_start(att_row[L][:, :], t[f"att_row{L}"]).then_inc(ld_att[L], 16)
                if L != 2:
                    sp.dma_start(bo[L][:, :], t[f"bo{L}"].partition_broadcast(P)).then_inc(ld_att[L], 16)

            def load_ring(L, w, cols):
                M = mo[L]
                n = ROUTE[L]["ENT"]
                for k in range(RING):
                    if L > 0 and k == 0:
                        sp.wait_ge(mo[L - 1]["y"], UP_AHEAD + 2 * ROUTE[L - 1]["ENT"])
                    sp.dma_start(ring[:, k, 0:cols], w[k, :, :]).then_inc(ring_in[k], 16)
                with sp.Fori(0, n // RING - 1) as i:
                    for k in range(RING):
                        sp.wait_ge(M["y"], 2 * RING * i + 2 * (k + 1) + UP_AHEAD)
                        sp.dma_start(ring[:, k, 0:cols], w[RING * i + RING + k, :, :]).then_inc(ring_in[k], 16)
                for e in range(n - n % RING, n):
                    sp.wait_ge(M["y"], 2 * (e - RING) + 2 + UP_AHEAD)
                    sp.dma_start(ring[:, e % RING, 0:cols], w[e, :, :]).then_inc(ring_in[e % RING], 16)
                if L < 3:
                    stack_keys(L + 1)

            def stack_keys(L):
                if L == 1:
                    sp.wait_ge(stacks_set, 8)
                else:
                    sp.wait_ge(at["p"], (L - 1) * NU)
                for hf in range(NHALF):
                    sp.wait_ge(at["kparts"], (L - 1) * adds["kparts"] + hf + 1)
                    for n, (_, g) in enumerate(PAIRS):
                        sp.dma_start(kst[n * HD:(n + 1) * HD, :, hf * HALF:(hf + 1) * HALF],
                                     kp[:, g, hf * HALF:(hf + 1) * HALF]).then_inc(at_kst[L][hf], 16)

            def attention(L):
                A, pre = at, {n: (L - 1) * k for n, k in adds.items()}
                if L == 1:
                    sp.wait_ge(mo[0]["ytr"], 2)
                    sp.dma_start(mask_i[:, 0, :, :], t["mask_q"]).then_inc(ld_mask, 16)
                    sp.dma_start(mask_i[:, 1, :, :], t["mask_k"]).then_inc(ld_mask, 16)
                for hf in range(NHALF):
                    sp.wait_ge(A["qparts"], pre["qparts"] + hf + 1)
                    for n, (g, _) in enumerate(PAIRS):
                        sp.dma_start(qst[n * HD:(n + 1) * HD, :, hf * HALF:(hf + 1) * HALF],
                                     qp[:, g, hf * HALF:(hf + 1) * HALF]).then_inc(at_qst[L][hf], 16)
                for G in range(4 * B):
                    b, g = divmod(G, 4)
                    sp.wait_ge(A["nmc"], pre["nmc"] + G + 1)
                    for q in range(TB):
                        sp.dma_start(qst[KROWS:SROWS, 4 * g:4 * g + 4, b * S + q * P:b * S + (q + 1) * P],
                                     nmT[q * PARTS * 4:(q + 1) * PARTS * 4, G, :]).then_inc(at_nmd[g], 16)

            load_ring(0, glu_w[0], GLU_COLS)
            attention(1)
            load_ring(1, glu_w[1], GLU_COLS)
            attention(2)
            load_ring(2, mlp_w[2], MLP_COLS)
            attention(3)
            load_ring(3, mlp_w[3], MLP_COLS)
            sp.wait_ge(x_done, NHALF)
            sp.dma_start(out, x[:, :, :]).then_inc(stored, 16)
            sp.wait_ge(stored, 16)

        @block.gpsimd
        def _(pool):
            pool.memset(mhalf[:, :], -0.5).then_inc(set_pool, 1)
            pool.memset(ones_row[:, :], 1.0).then_inc(set_pool, 1)
            pool.memset(zerob[:, :], 0.0).then_inc(set_pool, 1)

            def stacks():
                pool.wait_ge(stacks_set, 2)
                n = 2
                for stack, lo, value in ((kst, 32, 0.0), (kst, 64, 0.0), (qst, 32, 0.0), (qst, 64, 0.0), (kst, 96, 1.0)):
                    rows = stack[lo:lo + 32, :, :]
                    pool.memset(rows.bitcast(f32) if value == 0.0 else rows, value).then_inc(stacks_set, 1)
                    n += 1
                    pool.wait_ge(stacks_set, n)
                pool.wait_ge(ld_const, 16)
                pool.tensor_copy(pick128[:, :, :], consts[0:PARTS * EP, C_ID3:C_ID3 + EP].unsqueeze(2)
                                 .broadcast_to([PARTS * EP, EP, P])).then_inc(stacks_set, 1)

            def split_keys(L):
                pre = {n: (L - 1) * k for n, k in adds.items()}
                for hf in range(NHALF):
                    c = slice(hf * HALF, (hf + 1) * HALF)
                    n = 6 * (L - 1) + 3 * hf
                    pool.wait_ge(at["kf"], pre["kf"] + 2 * hf + 2)
                    if L > 1:
                        for h in range(NHALF):
                            pool.wait_ge(at_kst[L - 1][h], 16 * len(PAIRS))
                    pool.tensor_tensor(kf[:, c], kf[:, c], kp[:, 0, c], ALU.subtract).then_inc(kstep, 1)
                    pool.wait_ge(kstep, n + 1)
                    pool.tensor_copy(kp[:, 1, c], kf[:, c]).then_inc(kstep, 1)
                    pool.wait_ge(kstep, n + 2)
                    pool.tensor_tensor(kp[:, 2, c], kf[:, c], kp[:, 1, c], ALU.subtract).then_inc(kstep, 1)
                    pool.wait_ge(kstep, n + 3)
                    pool.sem_inc(at["kparts"], 1)

            def layer_norm(s):
                for hf in range(NHALF):
                    pool.wait_ge(ln_var, NHALF * s + hf + 1)
                    c = slice(4 * hf, 4 * hf + 4)
                    pool.tensor_tensor(rstd[:, c], veps[:, c], mhalf[:, c], ALU.pow).then_inc(ln_rstd, 1)

            def output_bias(L):
                if L == 2:
                    return
                n = 0 if L == 1 else 2
                pool.wait_ge(ld_att[L], 48)
                pool.wait_ge(gate_ready, 1)
                pool.wait_ge(ln_rstd, NHALF * (2 * L + 1))
                pool.tensor_scalar(bo[L][:, :], bo[L][:, :], gtan[:, L:L + 1], None, ALU.mult).then_inc(biased, 1)
                pool.wait_ge(biased, n + 1)
                pool.wait_ge(ln_xn, NT * (2 * L + 1))
                pool.tensor_tensor(x[:, :, :], x[:, :, :], bo[L][:, :].unsqueeze(1).broadcast_to([P, NT, D]),
                                   ALU.add).then_inc(biased, 1)

            pool.memset(vall[:, :, :, 8:9], 1.0).then_inc(stacks_set, 1)
            pool.memset(vall[:, :, :, 9:32], 0.0).then_inc(stacks_set, 1)
            pool.wait_ge(set_pool, 3)
            pool.wait_ge(stacks_set, 2)
            layer_norm(0)
            layer_norm(1)
            pool.wait_ge(ln_rstd, 2 * NHALF)
            stacks()
            pool.wait_ge(stacks_set, 8)
            for L in range(1, 4):
                split_keys(L)
                layer_norm(2 * L)
                output_bias(L)
                layer_norm(2 * L + 1)

        @block.tensor
        def _(pe):
            def layer_norm(s):
                if s % 2 == 1 and s < 7:
                    pe.wait_ge(at["vall"], (s + 1) // 2 * adds["vall"])
                for hf in range(NHALF):
                    pe.wait_ge(ln_xn, NT * s + 4 * hf + 4)
                    for k in range(4):
                        mm = pe.transpose(PS[:, 6 + hf, k * P:(k + 1) * P], xn[:, 4 * hf + k, :], ident)
                    mm.then_inc(ln_tr, 1)

            def autocorrelation():
                W = att_w[0]
                dft = consts[:, C_DFT:C_DFT + 2 * S]
                inv = consts[:, C_INV:C_INV + 3 * S]

                def dft_tokens(src, bank, done):
                    for b in range(B):
                        for k in range(TB):
                            mm = pe.matmul(PS[:, bank + b // 2, (b % 2) * S:(b % 2 + 1) * S], src[:, TB * b + k, :],
                                           dft[:, k * S:(k + 1) * S], start=(k == 0), stop=(k == TB - 1))
                    mm.then_inc(done, 1)

                def project(bank, w, done):
                    for f in range(2):
                        for b in range(B):
                            mm = pe.matmul(PS[:, bank + f, b * P:(b + 1) * P],
                                           dft_in[:, b * S + f * P:b * S + (f + 1) * P], w, start=True, stop=True)
                    mm.then_inc(done, 1)

                pe.wait_ge(ld_const, 16)
                pe.wait_ge(ld_ctx, 32)
                dft_tokens(ctx_tok, 0, ac["kin"])
                pe.wait_ge(ac["kine"], 2)
                pe.wait_ge(ld_att[0], 16)
                project(2, W[:, P:2 * P], ac["kfreq"])
                pe.wait_ge(ld_ctx, 32)
                for i in range(NT):
                    mm = pe.matmul(PS[:, 4 + i // 4, (i % 4) * P:(i % 4 + 1) * P], ctx_nat[:, i, :], W[:, 3 * P:4 * P],
                                   start=True, stop=True)
                mm.then_inc(ac["z"], 1)
                pe.wait_ge(ac["ze"], 1)
                for hf in range(NHALF):
                    mm = pe.matmul(PS[:, 6 + hf, :], W[:, 2 * P:3 * P], vo[:, hf * HALF:(hf + 1) * HALF],
                                   start=True, stop=True)
                mm.then_inc(ac["vo"], 1)
                pe.wait_ge(ac["voe"], 1)
                layer_norm(0)
                dft_tokens(xn, 0, ac["qin"])
                pe.wait_ge(ac["qine"], 2)
                project(4, W[:, 0:P], ac["qfreq"])
                pe.wait_ge(ac["prod"], 5)
                for b in range(B):
                    o = PS[:, b // 2, (b % 2) * S:(b % 2 + 1) * S]
                    for n, j in enumerate((0, 1, 4)):
                        mm = pe.matmul(o, prod[:, j, b * P:(b + 1) * P], inv[:, n * S:(n + 1) * S],
                                       start=(n == 0), stop=(n == 2))
                mm.then_inc(ac["corr"], 1)
                pe.wait_ge(ac["mix"], B)
                for b in range(B):
                    mm = pe.transpose(PS[:, 2, b * P:(b + 1) * P], mixT[:, b, :], ident)
                mm.then_inc(ac["mo"], 1)
                pe.wait_ge(ac["moe"], 1)
                for b in range(B):
                    mm = pe.matmul(PS[:, 4 + b // 2, (b % 2) * S:(b % 2 + 1) * S], mixo[:, b * P:(b + 1) * P],
                                   vo[:, b * S:(b + 1) * S], start=True, stop=True)
                mm.then_inc(ac["out"], 1)

            def route(L):
                E = ROUTE[L]["E"]
                if L == 0:
                    pe.wait_ge(ld_route, 16 * 8)
                if L < 3:
                    pe.wait_ge(at["kf"], (L + 1) * adds["kf"])
                for i in range(NT):
                    o = PS[:, 0, i * E:(i + 1) * E]
                    if i % 4 == 0:
                        pe.wait_ge(ln_xnT[i // 4], 2 * L + 2)
                    mm = pe.matmul(o, xnT[:, i * P:(i + 1) * P], wr[L][:, :], start=True, stop=(L != 2))
                    if L == 2:
                        mm = pe.matmul(o, ones_row[:, :], br2[:, :], start=False, stop=True)
                mm.then_inc(rt["logits"], 1)

            def turn_weights(L):
                pe.wait_ge(rt["parts"], L + 1)
                for i in range(NT):
                    mm = pe.transpose(PS[0:PARTS * EP, 1 - i // 4, (i % 4) * 64:(i % 4 + 1) * 64].bitcast(bf16),
                                      wpart[:, i, :, :].rearrange("p a e -> p (a e)"), identb[:, :])
                if L >= 2:
                    for i in range(NT):
                        mm = pe.transpose(PS[0:EP, 4 + i // 4, (i % 4) * P:(i % 4 + 1) * P], wtab[:, i, :], ident)
                mm.then_inc(rt["tr"], 1)
                pe.wait_ge(rt["wT"], 2 * (L + 1))
                if L >= 2:
                    pe.wait_ge(rt["wTf"], L - 1)

            def experts(L, glu):
                M, n = mo[L], ROUTE[L]["ENT"]
                pick = (pick64[:, :, :].rearrange("k e f -> k (e f)") if glu
                        else pick128[:, :, :].rearrange("k e f -> k (e f)"))

                def up(unit, slot, hf, full):
                    if hf == 0:
                        pe.wait_ge(ring_in[slot], full)
                    pe.wait_ge(M["gated"] if glu else M["hid"], unit + 1)
                    rhs = xnT[:, hf * HALF:(hf + 1) * HALF]
                    mm = pe.matmul(PS[:, 2 + hf, :], ring[:, slot, 0:P], rhs, start=True, stop=True)
                    if glu:
                        mm = pe.matmul(PS[:, 4 + hf, :], ring[:, slot, P:2 * P], rhs, start=True, stop=True)
                    mm.then_inc(M["up"], 1)

                def spread(unit, entry, hf):
                    pe.wait_ge(M["hid"], unit + 1)
                    pe.matmul(PS[:, 6 + hf, :], pick[:, bass.ds(entry * P, P)], wT[:, hf * HALF:(hf + 1) * HALF],
                              start=True, stop=True).then_inc(M["spread"], 1)

                def down(unit, slot, hf):
                    pe.wait_ge(M["hid"], unit + 1 + UP_AHEAD)
                    w = ring[:, slot, 2 * P:3 * P] if glu else ring[:, slot, P:2 * P]
                    pe.matmul(PS[:, hf, :], w, hid[:, hf, :], start=False, stop=False,
                              skip_group_check=True).then_inc(M["y"], 1)

                for hf in range(NHALF):
                    up(hf, 0, hf, 16 * (before[L][0] + 1))
                turn_weights(L)
                for hf in range(NHALF):
                    if glu:
                        mm = pe.matmul(PS[:, hf, :], zerob[:, 0:P], zerob[:, :], start=True, stop=False,
                                       skip_group_check=True)
                    else:
                        mm = pe.matmul(PS[:, hf, :], b2[L][:, :], wTf[:, hf * HALF:(hf + 1) * HALF], start=True,
                                       stop=False, skip_group_check=True)
                    mm.then_inc(M["y"], 1)
                spread(0, 0, 0)
                with pe.Fori(0, groups(n)) as i:
                    for k in range(RING):
                        nk, wrap = (k + 1) % RING, (k + 1) // RING
                        for hf in range(NHALF):
                            u = 2 * RING * i + 2 * k + hf
                            spread(u + 1, RING * i + k + hf, 1 - hf)
                            down(u, k, hf)
                            up(u + 2, nk, hf, 16 * i + 16 * (before[L][nk] + 1 + wrap))
                for e in range(RING * groups(n), n):
                    ne = (e + 1) % RING
                    for hf in range(NHALF):
                        u = 2 * e + hf
                        if e + hf < n:
                            spread(u + 1, e + hf, 1 - hf)
                        down(u, e % RING, hf)
                        if e + 1 < n:
                            up(u + 2, ne, hf, 16 * (before[L][ne] + (e + 1) // RING + 1))
                pe.wait_ge(M["yT"], NHALF)
                for i in range(NT):
                    mm = pe.transpose(PS[:, 2 + i // 4, (i % 4) * P:(i % 4 + 1) * P], yT[:, i * P:(i + 1) * P], ident)
                    if i % 4 == 3:
                        mm.then_inc(M["ytr"], 1)

            def project_keys(L):
                W, row = att_w[L], att_row[L]
                pe.wait_ge(ld_att[L], 32 if L == 2 else 48)
                for hf in range(NHALF):
                    pe.matmul(PS[:, hf, :], W[:, P:2 * P], ctxT[:, hf * HALF:(hf + 1) * HALF],
                              start=True, stop=True).then_inc(at["k"], 1)
                if L > 1:
                    pe.wait_ge(at["on"], (L - 1) * adds["on"])
                    pe.wait_ge(at["fin_e"], (L - 1) * adds["fin_e"])
                else:
                    pe.wait_ge(ac["voe"], 1)
                for i in range(NT):
                    o = PS[:, 6 + i // 4, (i % 4) * P:(i % 4 + 1) * P]
                    pe.matmul(o, ctxT[:, i * P:(i + 1) * P], W[:, 2 * P:3 * P], start=True, stop=False)
                    mm = pe.matmul(o, ones_row[:, :], row[:, 0:P], start=False, stop=True)
                mm.then_inc(at["v"], 1)

            def attention(L):
                A, W, row = at, att_w[L], att_row[L]
                pre = {n: (L - 1) * k for n, k in adds.items()}
                for hf in range(NHALF):
                    pe.wait_ge(ln_xnT[hf], 2 * L + 1)
                    pe.matmul(PS[:, hf, :], W[:, 0:P], xnT[:, hf * HALF:(hf + 1) * HALF],
                              start=True, stop=True).then_inc(A["q"], 1)
                if L == 3:
                    pe.wait_ge(A["vall"], pre["vall"] + 2)
                    pe.wait_ge(masks_ready, 1)
                    for b in range(B):
                        if b >= 2:
                            pe.wait_ge(A["ue"], b - 1)
                        for q in range(TB):
                            for k in range(TB):
                                mm = pe.matmul(PS[:, 6 + b % 2, q * H * 9:(q + 1) * H * 9],
                                               maskedT[:, k, q * P:(q + 1) * P], vall[:, TB * b + k, :, 0:9],
                                               start=(k == 0), stop=(k == TB - 1))
                        mm.then_inc(A["u"], 1)
                    pe.wait_ge(A["ue"], B)
                if L == 2:
                    pe.wait_ge(masks_ready, 1)

                def max_scores(v):
                    b, u = divmod(v, H)
                    h0, q = u // 2 * 2, u % 2
                    if u == 0 and b % 2 == 0:
                        pe.wait_ge(at_kst[L][b // 2], 16 * len(PAIRS))
                        pe.wait_ge(at_qst[L][b // 2], 16 * len(PAIRS))
                    if v >= 2:
                        pe.wait_ge(A["mx"], pre["mx"] + v - 1)
                    if L >= 2:
                        pe.matmul(PS[:, v % 2, :], identb[:, :],
                                  negq[:, L - 2, q:q + 1, :].broadcast_to([P, 2, S]), start=True, stop=False,
                                  skip_group_check=True)
                    for j in range(2):
                        mm = pe.matmul(PS[:, v % 2, j * S:(j + 1) * S],
                                       qst[0:KROWS, h0 + j, b * S + q * P:b * S + (q + 1) * P],
                                       kst[0:KROWS, h0 + j, b * S:(b + 1) * S], start=(L == 1), stop=True,
                                       skip_group_check=True)
                    mm.then_inc(A["s"], 1)

                def turn_max(G):
                    pe.wait_ge(A["nmp"], pre["nmp"] + G + 1)
                    if G >= 1:
                        pe.wait_ge(A["nmc"], pre["nmc"] + G)
                    if 4 * G >= H + LAG + 2:
                        pe.wait_ge(A["on"], pre["on"] + (4 * G - H - LAG - 2) // H + 1)
                    pe.transpose(PS[0:TB * PARTS * 4, 6, 0:64].bitcast(bf16),
                                 nmpart[:, G, :, :, :].rearrange("p q a n -> p (q a n)"), identb[:, :]).then_inc(A["nmt"], 1)

                def shifted_scores(w):
                    b, h = divmod(w, H)
                    if h % 4 == 0:
                        pe.wait_ge(at_nmd[h // 4], 16 * TB * (B * (L - 1) + b + 1))
                    if w >= 2:
                        pe.wait_ge(A["p"], pre["p"] + w - 1)
                    if L >= 2:
                        neg = (negq[:, 0, :, :] if L == 2 else negk[:, :, :]).rearrange("p k n -> p (k n)")
                        pe.matmul(PS[:, 2 + w % 2, :], identb[:, :], neg, start=True, stop=False,
                                  skip_group_check=True)
                    for k in range(TB):
                        mm = pe.matmul(PS[:, 2 + w % 2, k * S:(k + 1) * S],
                                       kst[0:SROWS, h, b * S + k * P:b * S + (k + 1) * P],
                                       qst[0:SROWS, h, b * S:(b + 1) * S], start=(L == 1), stop=True,
                                       skip_group_check=True)
                    mm.then_inc(A["st"], 1)

                def weigh_values(b, g):
                    pe.wait_ge(A["p"], pre["p"] + H * b + 4 * g + 4)
                    if g == 0:
                        if b > 0:
                            pe.wait_ge(A["oe"], pre["oe"] + b)
                        else:
                            pe.wait_ge(A["vall"], pre["vall"] + 2)
                    for k in range(TB):
                        for j in range(4):
                            h = 4 * g + j
                            mm = pe.matmul(PS[32 * j:32 * j + 32, 4 + g // 2, (g % 2) * S:(g % 2 + 1) * S],
                                           vall[:, TB * b + k, h, :], pT[:, (H * b + h) % 8, k * S:(k + 1) * S],
                                           start=(k == 0), stop=(k == TB - 1), skip_group_check=True)
                    mm.then_inc(A["pv"], 1)

                def turn_outputs(b):
                    pe.wait_ge(A["oe"], pre["oe"] + b + 1)
                    pe.wait_ge(A["nmc"], pre["nmc"] + min(4 * b + 8, 4 * B))
                    if b >= 1:
                        pe.wait_ge(A["on"], pre["on"] + b)
                    for q in range(TB):
                        for g in range(4):
                            mm = pe.transpose(PS[:, 6 + q, g * P:(g + 1) * P],
                                              oT[:, g * S + q * P:g * S + (q + 1) * P], ident)
                    mm.then_inc(A["ot"], 1)

                pe.wait_ge(A["qf"], pre["qf"] + 4)
                def turn_normalised(hf):
                    pe.wait_ge(A["on"], pre["on"] + 2 * hf + 2)
                    if hf == 0:
                        pe.wait_ge(A["mx"], pre["mx"] + NU)
                    for k in range(4):
                        mm = pe.transpose(PS[:, 0, k * P:(k + 1) * P], onrm[:, 4 * hf + k, :], ident)
                    mm.then_inc(A["fin_t"], 1)

                def project_outputs(hf):
                    pe.wait_ge(A["fin_e"], pre["fin_e"] + hf + 1)
                    if hf == 1:
                        pe.wait_ge(A["p"], pre["p"] + NU)
                    for k in range(4):
                        i = 4 * hf + k
                        mm = pe.matmul(PS[:, 1 + hf, k * P:(k + 1) * P], onT[:, i * P:(i + 1) * P],
                                       W[:, 3 * P:4 * P], start=True, stop=True)
                    mm.then_inc(A["fin"], 1)

                for p in range(NU + LAG):
                    if p < NU:
                        max_scores(p)
                    if p % 4 == 2 and 0 <= (p - 6) // 4 < 4 * B:
                        turn_max((p - 6) // 4)
                    w = p - LAG
                    if w >= 0:
                        shifted_scores(w)
                        if w >= 5 and w % 4 == 1:
                            weigh_values(*divmod((w - 5) // 4, 4))
                        if w >= H + 7 and w % H == 7:
                            turn_outputs(w // H - 1)
                    if p == NU + 2:
                        turn_normalised(0)
                    if p == NU + 6:
                        project_outputs(0)
                weigh_values(B - 1, 3)
                turn_outputs(B - 1)
                turn_normalised(1)
                project_outputs(1)

            pe.wait_ge(set_pool, 3)
            pe.wait_ge(set_dve, 3)
            autocorrelation()
            project_keys(1)
            layer_norm(1)
            route(0)
            experts(0, True)
            for L in range(1, 4):
                layer_norm(2 * L)
                attention(L)
                if L < 3:
                    project_keys(L + 1)
                layer_norm(2 * L + 1)
                route(L)
                experts(L, L < 2)

        @block.scalar
        def _(act):
            def layer_norm(s):
                act.wait_ge(ln_tr, 2 * s + 1)
                act.activation(xnT[:, 0:HALF], PS[:, 6, :], ACT.Copy).then_inc(ln_xnT[0], 1)

            def take_keys(L):
                for hf in range(NHALF):
                    c = slice(hf * HALF, (hf + 1) * HALF)
                    act.wait_ge(at["k"], (L - 1) * adds["k"] + hf + 1)
                    if L > 1 and hf == 0:
                        for h in range(NHALF):
                            act.wait_ge(at_kst[L - 1][h], 16 * len(PAIRS))
                    for dst in (kf[:, c], kp[:, 0, c]):
                        act.activation(dst, PS[:, hf, :], ACT.Identity,
                                       bias=att_w[L][:, 4 * P + 1:4 * P + 2]).then_inc(at["kf"], 1)
                act.wait_ge(at["v"], L)
                if L == 1:
                    act.wait_ge(stacks_set, 2)
                for hf in range(NHALF):
                    act.activation(vall[:, 4 * hf:4 * hf + 4, :, 0:HD],
                                   PS[:, 6 + hf, :].rearrange("p (t h d) -> p t h d", t=4, h=H),
                                   ACT.Copy).then_inc(at["vall"], 1)

            def route(L):
                SM = ROUTE[L]["SM"]
                act.wait_ge(rt["shift"], L + 1)
                act.activation(probs[:, :, 0:SM], shifted[:, :, 0:SM], ACT.Exp).then_inc(rt["exp"], 1)
                if L == 1:
                    act.activation(zsg[:, :], shifted[:, :, 16], ACT.Exp, scale=-1.0).then_inc(rt["exp"], 1)
                func = ACT.Silu if L < 2 else (ACT.Gelu if L == 2 else ACT.Relu)
                act.activation(warm[:, :], gates[:, 0:1], func).then_inc(astep, 1)

            def take_weights(L):
                act.wait_ge(rt["tr"], L + 1)
                if L >= 2:
                    act.activation(wTf[:, :], PS[0:EP, 4:6, :].rearrange("p a n -> p (a n)"), ACT.Copy).then_inc(rt["wTf"], 1)
                act.activation(wT[:, 0:HALF], PS[0:PARTS * EP, 1, 0:S].bitcast(bf16), ACT.Copy).then_inc(rt["wT"], 1)

            def experts(L, glu):
                M, n = mo[L], ROUTE[L]["ENT"]
                func = ACT.Silu if glu else (ACT.Gelu if L == 2 else ACT.Relu)

                def unit(u, slot, hf):
                    act.wait_ge(M["up"], u + 1)
                    act.wait_ge(M["gated"] if glu else M["hid"], u + 1)
                    bias = 0.0 if glu else ring[:, slot, 2 * P:2 * P + 1]
                    act.activation(act_out[:, hf, :], PS[:, 2 + hf, :], func, bias=bias).then_inc(M["act"], 1)

                take_weights(L)
                with act.Fori(0, groups(n)) as i:
                    for k in range(RING):
                        for hf in range(NHALF):
                            unit(2 * RING * i + 2 * k + hf, k, hf)
                for e in range(RING * groups(n), n):
                    for hf in range(NHALF):
                        unit(2 * e + hf, e % RING, hf)
                act.wait_ge(M["y"], UP_AHEAD + 2 * n - 1)
                act.activation(yT[:, 0:HALF], PS[:, 0, :], ACT.Copy, scale=gtan[:, 4 + L:5 + L]).then_inc(M["yT"], 1)

            def attention(L):
                A, W, sc = at, att_w[L], SCALE[L]
                pre = {n: (L - 1) * k for n, k in adds.items()}
                for hf in range(NHALF):
                    act.wait_ge(A["q"], pre["q"] + hf + 1)
                    c = slice(hf * HALF, (hf + 1) * HALF)
                    for dst in (qf[:, c], qp[:, 0, c]):
                        act.activation(dst, PS[:, hf, :], ACT.Identity, bias=W[:, 4 * P:4 * P + 1]).then_inc(A["qf"], 1)
                if L == 3:
                    for b in range(B):
                        act.wait_ge(A["u"], b + 1)
                        act.activation(umask[:, b, :, :], PS[:, 6 + b % 2, 0:TB * H * 9].rearrange("p (q n) -> p q n", q=TB),
                                       ACT.Copy).then_inc(A["ue"], 1)

                def copy_max(G):
                    b, g = divmod(G, 4)
                    act.wait_ge(A["nmt"], pre["nmt"] + G + 1)
                    act.activation(nmT[:, G, :], PS[0:TB * PARTS * 4, 6, 0:64].bitcast(bf16), ACT.Copy).then_inc(A["nmc"], 1)
                    if L == 3 and g == 3:
                        act.activation(emask[:, b, :, :], emask[:, b, :, :], ACT.Exp, scale=sc).then_inc(A["em"], 1)

                def take_outputs(b):
                    if L == 1 and b == 0:
                        act.wait_ge(masks_ready, 1)
                    act.wait_ge(A["pv"], pre["pv"] + 4 * (b + 1))
                    if b >= 1:
                        act.wait_ge(A["ot"], pre["ot"] + b)
                    act.activation(oT[:, :], banks(4), ACT.Copy).then_inc(A["oe"], 1)

                act.activation(warm[:, :], gates[:, 0:1], ACT.Exp).then_inc(astep, 1)
                for w in range(-2, NU):
                    if w % 4 == 2 and (w + 6) // 4 < 4 * B:
                        copy_max((w + 6) // 4 - (w < 0))
                        if w < 0:
                            copy_max(1)
                    if w < 0:
                        continue
                    if w >= H + 3 and w % H == 3:
                        take_outputs(w // H - 1)
                    if w == NU - LAG + 4:
                        act.wait_ge(A["fin_t"], pre["fin_t"] + 1)
                        act.activation(onT[:, 0:HALF], PS[:, 0, :], ACT.Copy).then_inc(A["fin_e"], 1)
                    act.wait_ge(A["st"], pre["st"] + w + 1)
                    if w >= 8:
                        act.wait_ge(A["pv"], pre["pv"] + (w - 8) // 4 + 1)
                    act.activation(pT[:, w % 8, :], PS[:, 2 + w % 2, :], ACT.Exp, scale=sc).then_inc(A["p"], 1)
                take_outputs(B - 1)
                act.wait_ge(A["fin_t"], pre["fin_t"] + 2)
                act.activation(onT[:, HALF:N], PS[:, 0, :], ACT.Copy).then_inc(A["fin_e"], 1)

            act.wait_ge(ac["kin"], 1)
            act.activation(dft_in[:, 0:HALF], PS[:, 0, :], ACT.Copy).then_inc(ac["kine"], 1)
            act.wait_ge(ac["kfreq"], 1)
            act.activation(kfreq[:, 0, :], PS[:, 2, :], ACT.Copy).then_inc(ac["kfe"], 1)
            act.activation(kfreq[:, 1, :], PS[:, 3, :], ACT.Copy).then_inc(ac["kfe"], 1)
            act.wait_ge(ac["z"], 1)
            act.activation(vo[:, :], banks(4), ACT.Copy).then_inc(ac["ze"], 1)
            act.wait_ge(ac["vo"], 1)
            act.activation(vo[:, :], banks(6), ACT.Copy).then_inc(ac["voe"], 1)
            act.wait_ge(ld_gate, 16)
            act.activation(gtan[:, :], gates[:, :], ACT.Tanh).then_inc(gate_ready, 1)
            layer_norm(0)
            act.wait_ge(ac["qin"], 1)
            act.activation(dft_in[:, 0:HALF], PS[:, 0, :], ACT.Copy).then_inc(ac["qine"], 1)
            act.wait_ge(ac["top"], 1)
            act.activation(cw[:, 1, :], cw[:, 0, :], ACT.Exp).then_inc(ac["exp"], 1)
            act.wait_ge(ac["mo"], 1)
            act.activation(mixo, PS[:, 2, :], ACT.Copy).then_inc(ac["moe"], 1)
            take_keys(1)
            layer_norm(1)
            route(0)
            experts(0, True)
            for L in range(1, 4):
                layer_norm(2 * L)
                attention(L)
                if L < 3:
                    take_keys(L + 1)
                layer_norm(2 * L + 1)
                route(L)
                experts(L, L < 2)

        @block.vector
        def _(dve):
            steps = [0]

            def link(ins):
                steps[0] += 1
                ins.then_inc(dstep, 1)
                dve.wait_ge(dstep, steps[0])

            def run(instructions):
                for n, ins in enumerate(instructions):
                    steps[0] += 1
                    ins.then_inc(dstep, 1)
                dve.wait_ge(dstep, steps[0])

            def ln_statistics(s, hf):
                tiles = range(4 * hf, 4 * hf + 4)
                run(dve.bn_stats(stats[:, i, :], x[:, i, :]) for i in tiles)
                run(dve.bn_aggr(mv[:, i, :], stats[:, i, :]) for i in tiles)
                c = slice(4 * hf, 4 * hf + 4)
                dve.tensor_scalar(veps[:, c], mv[:, c, 1], LN_EPS, None, ALU.add).then_inc(ln_var, 1)

            def ln_apply(s, hf):
                dve.wait_ge(ln_rstd, NHALF * s + hf + 1)
                for i in range(4 * hf, 4 * hf + 4):
                    dve.tensor_scalar(xn[:, i, :], x[:, i, :], mv[:, i, 0:1], rstd[:, i:i + 1],
                                      ALU.subtract, ALU.mult).then_inc(ln_xn, 1)

            def ln_turned(s):
                dve.wait_ge(ln_tr, 2 * s + 2)
                dve.tensor_copy(xnT[:, HALF:N], PS[:, 7, :]).then_inc(ln_xnT[1], 1)

            def layer_norm(s, add=None):
                for hf in range(NHALF):
                    if add:
                        add(hf)
                    ln_statistics(s, hf)
                for hf in range(NHALF):
                    ln_apply(s, hf)
                ln_turned(s)

            def add_half(hf, bank, g, ready, count):
                dve.wait_ge(ready, count)
                xs = x[:, 4 * hf:4 * hf + 4, :].rearrange("p a n -> p (a n)")
                if g is None:
                    link(dve.tensor_tensor(xs, PS[:, bank, :], xs, ALU.add))
                else:
                    link(dve.scalar_tensor_tensor(out=xs, in0=PS[:, bank, :], scalar=gtan[:, g:g + 1], in1=xs,
                                                  op0=ALU.mult, op1=ALU.add))

            def autocorrelation():
                dve.wait_ge(ac["kin"], 1)
                dve.tensor_copy(dft_in[:, HALF:N], PS[:, 1, :]).then_inc(ac["kine"], 1)
                layer_norm(0)
                dve.wait_ge(ac["qin"], 1)
                dve.tensor_copy(dft_in[:, HALF:N], PS[:, 1, :]).then_inc(ac["qine"], 1)
                dve.wait_ge(ac["kfe"], 2)
                dve.wait_ge(ac["qfreq"], 1)
                for j, (qx, kx) in enumerate(((0, 0), (1, 1), (1, 0), (0, 1))):
                    dve.tensor_tensor(prod[:, j, :], PS[:, 4 + qx, :], kfreq[:, kx, :], ALU.mult).then_inc(ac["prod"], 1)
                dve.wait_ge(ac["prod"], 4)
                dve.tensor_tensor(prod[:, 4, :], prod[:, 2, :], prod[:, 3, :], ALU.subtract).then_inc(ac["prod"], 1)
                dve.wait_ge(ac["corr"], 1)
                for b in range(B):
                    c = PS[:, b // 2, (b % 2) * S:(b % 2 + 1) * S]
                    link(dve.max(corr8[:, b, :], c))
                    link(dve.max_index(lag8[:, b, :], corr8[:, b, :], c))
                top = corr8[:, :, 0:TOPLAGS]
                w0, w1, w2, w3 = (cw[:, j, :].rearrange("p (b i) -> p b i", b=B) for j in range(4))
                dve.tensor_tensor(w0, top, corr8[:, :, 0:1].broadcast_to([P, B, TOPLAGS]), ALU.subtract).then_inc(ac["top"], 1)
                link(dve.tensor_scalar(roll_i[:, 0, :].rearrange("p (b i) -> p b i", b=B), lag8[:, :, 0:TOPLAGS], -1.0,
                                       consts[:, C_DPOS:C_DPOS + 1], ALU.mult, ALU.add))
                link(dve.tensor_scalar(roll_i[:, 1, :], roll_i[:, 0, :], HD - 1, None, ALU.bitwise_and))
                dve.wait_ge(ac["exp"], 1)
                link(dve.tensor_reduce(csum[:, 0, :], w1, AX.X, ALU.add))
                link(dve.reciprocal(csum[:, 1, :], csum[:, 0, :]))
                link(dve.tensor_tensor(w2, w1, csum[:, 1, :].unsqueeze(2).broadcast_to([P, B, TOPLAGS]), ALU.mult))
                link(dve.tensor_tensor(sel[:, :, :], roll_i[:, 1, :].unsqueeze(2).broadcast_to([P, B * TOPLAGS, HD]),
                                       consts[:, C_IOTA:C_IOTA + HD].unsqueeze(1).broadcast_to([P, B * TOPLAGS, HD]),
                                       ALU.is_equal))
                link(dve.tensor_tensor(sel[:, :, :], sel[:, :, :],
                                       cw[:, 2, :].unsqueeze(2).broadcast_to([P, B * TOPLAGS, HD]), ALU.mult))
                link(dve.tensor_reduce(mix8[:, :, :], sel[:, :, :].rearrange("p (b i) r -> p b r i", b=B), AX.X, ALU.add))
                for b in range(B):
                    dve.tensor_tensor(mixT[:, b, :].rearrange("p (h r) -> p h r", h=H),
                                      mix8[:, b:b + 1, :].broadcast_to([P, H, HD]),
                                      consts[:, C_BLK:C_BLK + H].unsqueeze(2).broadcast_to([P, H, HD]),
                                      ALU.mult).then_inc(ac["mix"], 1)
                dve.wait_ge(gate_ready, 1)

            def route(L):
                r = ROUTE[L]
                E, SM, K = r["E"], r["SM"], r["K"]
                if L < 2:
                    dve.sem_inc(mo[L]["gated"], UP_AHEAD)
                dve.sem_inc(mo[L]["hid"], UP_AHEAD)
                dve.wait_ge(rt["logits"], L + 1)
                lg = PS[:, 0, 0:NT * E].rearrange("p (t e) -> p t e", t=NT)
                link(dve.tensor_reduce(rmax[:, :], lg[:, :, 0:SM], AX.X, ALU.max))
                if L == 1:
                    link(dve.tensor_copy(shifted[:, :, 16], lg[:, :, 16]))
                dve.tensor_tensor(shifted[:, :, 0:SM], lg[:, :, 0:SM],
                                  rmax[:, :].unsqueeze(2).broadcast_to([P, NT, SM]), ALU.subtract).then_inc(rt["shift"], 1)
                dve.wait_ge(rt["exp"], L + 1 + (L >= 1))
                link(dve.tensor_reduce(rsum[:, :], probs[:, :, 0:SM], AX.X, ALU.add))
                link(dve.reciprocal(rrec[:, :], rsum[:, :]))
                link(dve.tensor_tensor(probs[:, :, 0:SM], probs[:, :, 0:SM],
                                       rrec[:, :].unsqueeze(2).broadcast_to([P, NT, SM]), ALU.mult))
                ranking = probs
                if L == 0:
                    ranking = ranked
                    link(dve.tensor_tensor(ranked[:, :, 0:SM], probs[:, :, 0:SM],
                                           cbias[:, :].unsqueeze(1).broadcast_to([P, NT, SM]), ALU.add))
                run(dve.max(top8[:, i, :], ranking[:, i, 0:SM]) for i in range(NT))
                link(dve.memset(top8[:, :, K:8], FLAG))
                run(dve.match_replace(out=flagged[:, i, 0:SM], in_to_replace=top8[:, i, :],
                                      in_values=ranking[:, i, 0:SM], imm_value=FLAG) for i in range(NT))
                link(dve.scalar_tensor_tensor(out=picked[:, :, 0:SM], in0=flagged[:, :, 0:SM], scalar=FLAG,
                                              in1=probs[:, :, 0:SM], op0=ALU.is_equal, op1=ALU.mult))
                if L == 0:
                    link(dve.tensor_scalar(wtab[:, :, :], picked[:, :, 0:R_REAL], 2.5, None, ALU.mult))
                    link(dve.tensor_reduce(rsum[:, :], picked[:, :, R_REAL:SM], AX.X, ALU.add))
                    link(dve.tensor_scalar(gzero[:, :], rsum[:, :], 2.5, gtan[:, 4:5], ALU.mult, ALU.mult))
                elif L == 1:
                    link(dve.memset(wtab[:, :, SM + 2 * SHARED_TILES:EP], 0.0))
                    link(dve.tensor_reduce(rsum[:, :], picked[:, :, 0:SM], AX.X, ALU.add))
                    link(dve.reciprocal(rrec[:, :], rsum[:, :]))
                    link(dve.tensor_tensor(wtab[:, :, 0:SM], picked[:, :, 0:SM],
                                           rrec[:, :].unsqueeze(2).broadcast_to([P, NT, SM]), ALU.mult))
                    link(dve.tensor_scalar(rsum[:, :], zsg[:, :], 1.0, None, ALU.add))
                    link(dve.reciprocal(rrec[:, :], rsum[:, :]))
                    link(dve.tensor_copy(wtab[:, :, SM:SM + 2 * SHARED_TILES],
                                         rrec[:, :].unsqueeze(2).broadcast_to([P, NT, 2 * SHARED_TILES])))
                elif L == 2:
                    link(dve.tensor_copy(wtab[:, :, 0:SM], picked[:, :, 0:SM]))
                    link(dve.memset(wtab[:, :, SM:EP], 1.0))
                else:
                    link(dve.memset(wtab[:, :, 2 * SM:EP], 0.0))
                    for i in range(2):
                        link(dve.tensor_copy(wtab[:, :, i:2 * SM:2], picked[:, :, 0:SM]))
                link(dve.tensor_copy(wpart[:, :, 0, :], wtab[:, :, :]))
                link(dve.tensor_tensor(wrest[:, :, :], wtab[:, :, :], wpart[:, :, 0, :], ALU.subtract))
                link(dve.tensor_copy(wpart[:, :, 1, :], wrest[:, :, :]))
                dve.tensor_tensor(wpart[:, :, 2, :], wrest[:, :, :], wpart[:, :, 1, :], ALU.subtract).then_inc(rt["parts"], 1)

            def experts(L, glu):
                M, n = mo[L], ROUTE[L]["ENT"]
                dve.wait_ge(rt["tr"], L + 1)
                dve.tensor_copy(wT[:, HALF:N], PS[0:PARTS * EP, 0, 0:S].bitcast(bf16)).then_inc(rt["wT"], 1)
                if L == 0:
                    run(dve.scalar_tensor_tensor(out=x[:, i, :], in0=xn[:, i, :], scalar=gzero[:, i:i + 1],
                                                 in1=x[:, i, :], op0=ALU.mult, op1=ALU.add) for i in range(NT))
                if L == 2:
                    link(dve.scalar_tensor_tensor(out=x[:, :, :], in0=xn[:, :, :], scalar=gtan[:, 4 + L:5 + L],
                                                  in1=x[:, :, :], op0=ALU.mult, op1=ALU.add))

                def unit(u, hf):
                    dve.wait_ge(M["act"], u + 1)
                    src = act_out
                    if glu:
                        dve.tensor_tensor(gated[:, hf, :], act_out[:, hf, :], PS[:, 4 + hf, :],
                                          ALU.mult).then_inc(M["gated"], 1)
                        dve.wait_ge(M["gated"], u + 1 + UP_AHEAD)
                        src = gated
                    dve.wait_ge(M["spread"], u + 1)
                    dve.wait_ge(M["y"], u + 1)
                    dve.tensor_tensor(hid[:, hf, :], src[:, hf, :], PS[:, 6 + hf, :], ALU.mult).then_inc(M["hid"], 1)

                with dve.Fori(0, groups(n)) as i:
                    for k in range(RING):
                        for hf in range(NHALF):
                            unit(2 * RING * i + 2 * k + hf, hf)
                for u in range(2 * RING * groups(n), 2 * n):
                    unit(u, u % 2)
                dve.wait_ge(M["y"], UP_AHEAD + 2 * n)
                dve.tensor_scalar(yT[:, HALF:N], PS[:, 1, :], gtan[:, 4 + L:5 + L], None, ALU.mult).then_inc(M["yT"], 1)
                if L == 3:
                    for hf in range(NHALF):
                        dve.wait_ge(M["ytr"], hf + 1)
                        xs = x[:, 4 * hf:4 * hf + 4, :].rearrange("p a n -> p (a n)")
                        dve.tensor_tensor(xs, PS[:, 2 + hf, :], xs, ALU.add).then_inc(x_done, 1)

            def prepare_masks():
                dve.wait_ge(ld_const, 16)
                dve.wait_ge(ld_mask, 32)
                link(dve.tensor_copy(negq[:, 0, :, :].rearrange("p k n -> p (k n)"), consts[:, C_BAND:C_BAND + TB * S]))
                link(dve.tensor_scalar(negq[:, 1, :, :], mask_i[:, 0, :, :], 0.0, NEG, ALU.is_equal, ALU.mult))
                link(dve.tensor_scalar(negk[:, :, :], mask_i[:, 1, :, :], 0.0, NEG, ALU.is_equal, ALU.mult))
                link(dve.tensor_scalar(maskedT[:, :, :], mask_i[:, 1, :, :], 0.0, None, ALU.is_equal))
                link(dve.tensor_scalar(maskq_f, mask_i[:, 0, :, :], 0.0, None, ALU.is_equal))
                link(dve.tensor_reduce(negfloor[:, :], maskq_f, AX.X, ALU.max))
                dve.tensor_scalar(negfloor[:, :], negfloor[:, :], -3.0e37, 3.0e37, ALU.mult, ALU.add).then_inc(dstep, 1)
                steps[0] += 1
                dve.wait_ge(dstep, steps[0])
                dve.tensor_scalar(negfloor[:, :], negfloor[:, :], -MASKED / SCALE[3], None, ALU.max).then_inc(masks_ready, 1)

            maskq_f = qf[:, 0:TB * S].rearrange("p (k n) -> p k n", k=TB)

            def attention(L):
                A, pre = at, {n: (L - 1) * k for n, k in adds.items()}
                for f, parts, ready, done in ((qf, qp, A["qf"], A["qparts"]),):
                    for hf in range(NHALF):
                        c = slice(hf * HALF, (hf + 1) * HALF)
                        dve.wait_ge(ready, 4 * (L - 1) + 2 * hf + 2)
                        link(dve.tensor_tensor(rest[:, :], f[:, c], parts[:, 0, c], ALU.subtract))
                        link(dve.tensor_copy(parts[:, 1, c], rest[:, :]))
                        dve.tensor_tensor(parts[:, 2, c], rest[:, :], parts[:, 1, c], ALU.subtract).then_inc(done, 1)
                        dve.wait_ge(done, 2 * (L - 1) + hf + 1)

                if L == 1:
                    prepare_masks()

                def split_max(b, g):
                    c = slice(4 * g, 4 * g + 4)
                    nm, part = negmax[:, b, :, c], nmpart[:, 4 * b + g, :, :, :]
                    if L == 3:
                        for q in range(TB):
                            link(dve.tensor_scalar(negmax[:, b, q, c], negmax[:, b, q, c], negfloor[:, q:q + 1], None,
                                                   ALU.min))
                        link(dve.tensor_scalar(emask[:, b, :, c], nm, MASKED / SCALE[3], 0.0, ALU.add, ALU.min))
                    link(dve.tensor_copy(part[:, :, 0, :], nm))
                    link(dve.tensor_tensor(nmrest[:, :, :], nm, part[:, :, 0, :], ALU.subtract))
                    link(dve.tensor_copy(part[:, :, 1, :], nmrest[:, :, :]))
                    dve.tensor_tensor(part[:, :, 2, :], nmrest[:, :, :], part[:, :, 1, :], ALU.subtract).then_inc(A["nmp"], 1)

                def normalise(b):
                    dve.wait_ge(A["ot"], pre["ot"] + b + 1)
                    o = PS[:, 6:8, :].rearrange("p q (h c) -> p q h c", h=H)[:, :, :, 0:9]
                    if L == 3:
                        dve.wait_ge(A["em"], b + 1)
                        for q in range(TB):
                            link(dve.tensor_tensor(ocor[:, q, :, :],
                                                   umask[:, b, q, :].rearrange("p (h c) -> p h c", h=H),
                                                   emask[:, b, q, :].unsqueeze(2).broadcast_to([P, H, 9]), ALU.mult))
                        link(dve.tensor_tensor(ocomb[:, :, :, :], o, ocor[:, :, :, :], ALU.add))
                        o = ocomb[:, :, :, :]
                    link(dve.reciprocal(orec[:, :, :], o[:, :, :, 8]))
                    for q in range(TB):
                        ins = dve.tensor_tensor(onrm[:, TB * b + q, :].rearrange("p (h d) -> p h d", h=H),
                                                o[:, q, :, 0:HD], orec[:, q, :].unsqueeze(2).broadcast_to([P, H, HD]),
                                                ALU.mult)
                        if q < TB - 1:
                            link(ins)
                    ins.then_inc(A["on"], 1)

                done_norm = 0
                for v in range(NU):
                    b, u = divmod(v, H)
                    h0, q = u // 2 * 2, u % 2
                    dve.wait_ge(A["s"], pre["s"] + v + 1)
                    dve.tensor_reduce(negmax[:, b, q, h0:h0 + 2], PS[:, v % 2, :].rearrange("p (h k) -> p h k", h=2),
                                      AX.X, ALU.max, negate=True).then_inc(A["mx"], 1)
                    if u % 4 == 3:
                        dve.wait_ge(A["mx"], pre["mx"] + v + 1)
                        split_max(b, u // 4)
                    if v >= LAG + H + 8 and (v - LAG) % H == 8:
                        normalise(done_norm)
                        done_norm += 1
                if L != 2:
                    dve.wait_ge(biased, 2 if L == 1 else 4)
                add_half(0, 1, L, A["fin"], pre["fin"] + 1)
                ln_statistics(2 * L + 1, 0)
                ln_apply(2 * L + 1, 0)
                for b in range(done_norm, B):
                    normalise(b)
                add_half(1, 2, L, A["fin"], pre["fin"] + 2)
                ln_statistics(2 * L + 1, 1)
                ln_apply(2 * L + 1, 1)
                ln_turned(2 * L + 1)

            dve.memset(cw[:, 3, :], 0.0).then_inc(set_dve, 1)
            dve.wait_ge(ld_const, 16)
            dve.tensor_copy(identb[:, :], ident).then_inc(set_dve, 1)
            id3 = consts[0:PARTS * EP, C_ID3:C_ID3 + EP]
            dve.tensor_copy(pick64[:, :, :], id3.unsqueeze(2).broadcast_to([PARTS * EP, EP, P // 2])).then_inc(set_dve, 1)
            dve.wait_ge(ld_x, 16)
            autocorrelation()
            layer_norm(1, lambda hf: add_half(hf, 4 + hf, 0, ac["out"], 1))
            route(0)
            experts(0, True)
            for L in range(1, 4):
                layer_norm(2 * L, lambda hf: add_half(hf, 2 + hf, None, mo[L - 1]["ytr"], hf + 1))
                attention(L)
                route(L)
                experts(L, L < 2)


def constants():
    c = np.zeros((P, C_ALL), np.float32)
    c[:, C_ID:C_ID + P] = np.eye(P)
    time, freq = np.arange(S), np.arange(P)
    angle = 2 * np.pi * np.outer(time, freq) / S
    nyq = (-1.0) ** time
    fwd = np.concatenate([np.cos(angle), np.sin(angle)], 1)
    fwd[:, P] = nyq
    c[:, C_DFT:C_DFT + 2 * S] = fwd.reshape(P, TB, 2 * P).reshape(P, -1)
    two = np.where(freq == 0, 1.0, 2.0)[:, None] / S
    icos, isin = two * np.cos(angle.T), two * np.sin(angle.T)
    icos2 = icos.copy()
    icos2[0] = nyq / S
    c[:, C_INV:C_INV + 3 * S] = np.concatenate([icos, icos2, isin], 1)
    c[:, C_BLK:C_BLK + H] = np.tile(np.eye(H), (HD, 1))
    c[:, C_DPOS] = np.arange(P) // H + S
    c[:, C_IOTA:C_IOTA + HD] = np.arange(HD)
    c[:PARTS * EP, C_ID3:C_ID3 + EP] = np.tile(np.eye(EP), (PARTS, 1))
    band = np.where(np.abs(np.subtract.outer(time, time)) <= BAND, 0.0, NEG)
    c[:, C_BAND:] = interleave(band)
    return c


def interleave(m):
    m = m.reshape(P, TB, P, TB)
    return m.transpose(0, 1, 3, 2).reshape(P, TB * S)


def tokens_on_partitions(a):
    return a.reshape(B, P, TB, D).transpose(1, 0, 2, 3).reshape(P, NT, D)


def arrays(i):
    i = {k: np.asarray(v) for k, v in i.items()}
    f = np.float32
    heads_minor = np.arange(P).reshape(H, HD).T.reshape(-1)
    col = lambda v: v.reshape(-1, 1)
    zero = np.zeros((P, 1), f)
    a = {"x": tokens_on_partitions(i["x"]), "ctx_tok": tokens_on_partitions(i["ctx_1024"]),
         "ctx_nat": i["ctx_1024"].reshape(NT, P, D).transpose(1, 0, 2),
         "ctxT": tokens_on_partitions(i["ctx_1024"]).transpose(2, 1, 0).reshape(D, N), "consts": constants(),
         "gates": np.concatenate([i["g_xattn"], i["g_ffn"]])}
    a["att_w0"] = np.concatenate([i["L0_xattn_wq"][:, heads_minor], i["L0_xattn_wk"][:, heads_minor], i["L0_xattn_wv"], i["L0_xattn_wo"], zero, zero], 1)
    wkv = i["L2_xattn_w_kv"]
    att = {1: (i["L1_xattn_Wq"].T, i["L1_xattn_Wk"].T, i["L1_xattn_Wv"].T, i["L1_xattn_Wo"].T, i["L1_xattn_bq"],
               i["L1_xattn_bk"], i["L1_xattn_bv"], i["L1_xattn_bo"]),
           2: (i["L2_xattn_w_q"], np.tile(wkv[:, :HD], (1, H)), np.tile(wkv[:, HD:], (1, H)), i["L2_xattn_w_o"],
               zero[:, 0], zero[:, 0], zero[:, 0], zero[:, 0]),
           3: (i["L3_xattn_wq"].T, i["L3_xattn_wk"].T, i["L3_xattn_wv"].T, i["L3_xattn_wo"].T, i["L3_xattn_bq"],
               i["L3_xattn_bk"], i["L3_xattn_bv"], i["L3_xattn_bo"])}
    for L, (wq, wk, wv, wo, bq, bk, bv, bo) in att.items():
        a[f"att_w{L}"] = np.concatenate([wq[:, heads_minor], wk[:, heads_minor], wv, wo, col(bq[heads_minor]),
                                         col(bk[heads_minor])], 1)
        a[f"att_row{L}"] = bv[None]
        if L != 2:
            a[f"bo{L}"] = bo
    a["wr0"] = i["L0_ffn_classifier_weight"].T
    a["wr1"] = np.concatenate([i["L1_ffn_gate_w"], i["L1_ffn_shared_gate_w"]]).T
    a["wr2"], a["wr3"] = i["L2_ffn_Wr"], i["L3_ffn_Wg"]
    a["br2"] = i["L2_ffn_br"][None]
    a["cbias"] = i["L0_ffn_e_score_correction_bias"]

    def glu(gate, up, down):
        pair = lambda w: w.reshape(-1, P, D)
        return np.concatenate([pair(gate).transpose(0, 2, 1), pair(up).transpose(0, 2, 1), pair(down)], 2)

    gu = i["L0_ffn_gate_up_proj"][:R_REAL]
    a["glu0"] = glu(gu[:, :64], gu[:, 64:], i["L0_ffn_down_proj"].transpose(0, 2, 1))
    gu = i["L1_ffn_w_gate_up"].transpose(0, 2, 1)
    pad = lambda w: np.concatenate([w, np.zeros((SHARED_TILES * P - w.shape[0], D), f)]).reshape(-1, 64, D)
    a["glu1"] = np.concatenate([
        glu(gu[:, :64], gu[:, 64:], i["L1_ffn_w_down"]),
        glu(pad(i["L1_ffn_shared_w_gate"]), pad(i["L1_ffn_shared_w_up"]), pad(i["L1_ffn_shared_w_down"].T))])
    a["mlp2"] = np.concatenate([np.concatenate([i["L2_ffn_We1"], i["L2_ffn_ws1"][None]]),
                                np.concatenate([i["L2_ffn_We2"], i["L2_ffn_ws2"][None]]),
                                np.concatenate([i["L2_ffn_Be1"], i["L2_ffn_bs1"][None]])[:, :, None]], 2)
    a["b2_2"] = np.concatenate([i["L2_ffn_Be2"], i["L2_ffn_bs2"][None]])
    w1 = i["L3_ffn_W1"].reshape(8, D, 2, P).transpose(0, 2, 1, 3).reshape(16, D, P)
    a["mlp3"] = np.concatenate([w1, i["L3_ffn_W2"].reshape(16, P, D), i["L3_ffn_b1"].reshape(16, P, 1)], 2)
    b23 = np.zeros((EP, P), f)
    b23[0:16:2] = i["L3_ffn_b2"]
    a["b2_3"] = b23
    m = i["mask_1x1xSxS2_ik1"].reshape(S, S)
    a["mask_q"] = interleave(m).reshape(P, TB, S)
    a["mask_k"] = interleave(m.T).reshape(P, TB, S)
    return {k: np.ascontiguousarray(v) for k, v in a.items()}


def kernel(**inputs):
    import concourse.bacc as bacc
    from concourse.bass_utils import run_bass_kernel_spmd

    nc = bacc.Bacc("TRN2", target_bir_lowering=False, num_devices=1)
    data = arrays(inputs)
    t = {k: nc.dram_tensor(f"in_{k}", v.shape, mybir.dt.from_np(v.dtype), kind="ExternalInput").ap()
         for k, v in data.items()}
    out = nc.dram_tensor("out_x", (P, NT, D), mybir.dt.float32, kind="ExternalOutput").ap()
    build(nc, t, out)
    r = run_bass_kernel_spmd(nc, [{f"in_{k}": v for k, v in data.items()}], core_ids=[0])
    got = np.asarray(r.results[0]["out_x"])
    return got.reshape(P, B, TB, D).transpose(1, 0, 2, 3).reshape(B, S, D)
```

```python
from contextlib import ExitStack

import numpy as np
import concourse.bass as bass
from concourse import mybir

B, S, D, H, HD = 4, 256, 128, 16, 8
N = B * S
P = 128
NT = N // P
TB = S // P
NHALF, HALF = 2, 512
PARTS = 3
PAIRS = ((0, 0), (0, 1), (1, 0), (1, 1), (0, 2), (2, 0))
QUERY_ORDER = sorted(enumerate(PAIRS), key=lambda pair: pair[1][0])
KROWS = 96
SROWS = KROWS + PARTS
TOPLAGS = 5
BAND = 32
EP = 32
RING = 4
KEPT = 4
NEG = -1.0e30
FLAG = -3.0e38
LN_EPS = 1e-5
MASKED = -10000.0

ROUTE = [dict(E=40, SM=40, K=6, ENT=16), dict(E=17, SM=16, K=2, ENT=11),
         dict(E=31, SM=31, K=3, ENT=32), dict(E=8, SM=8, K=2, ENT=16)]
GLU_COLS, MLP_COLS = 3 * P, 2 * P + 1
R_REAL = 32
SHARED_TILES = 3
SCALE = [None, 1.0 / HD ** 0.5, 1.0, 1.0 / HD ** 0.5]

C_ID, C_DFT, C_INV, C_BLK, C_DPOS, C_IOTA, C_ID3, C_BAND = 0, 128, 640, 1408, 1424, 1425, 1433, 1465
C_ALL = C_BAND + TB * S


def even(L):
    return ROUTE[L]["E"] + ROUTE[L]["E"] % 2


def build(nc, t, out):
    f32, f32r, bf16, i32, u32 = mybir.dt.float32, mybir.dt.float32r, mybir.dt.bfloat16, mybir.dt.int32, mybir.dt.uint32
    ALU, ACT, AX = mybir.AluOpType, mybir.ActivationFunctionType, mybir.AxisListType
    ctx = ExitStack()
    with ctx:
        def sb(name, shape, dt=f32):
            return ctx.enter_context(nc.sbuf_tensor(name, shape, dt))

        def sem(name):
            return ctx.enter_context(nc.semaphore(name))

        x = sb("x_res", [P, NT, D])
        xn = sb("xn", [P, NT, D])
        xhi, xlo = sb("xhi", [P, N], f32r), sb("xlo", [P, N], f32r)
        wpair = sb("wpair", [P, 2, 2, GLU_COLS], f32r)
        wqpair = sb("wqpair", [P, 2, P], f32r)
        hid_hi, hid_lo = sb("hid_hi", [P, KEPT, HALF], f32r), sb("hid_lo", [P, KEPT, HALF], f32r)
        ctx_tok = sb("ctx_tok", [P, NT, D])
        ctxT = sb("ctxT", [P, N])
        consts = sb("consts", [P, C_ALL])
        ident = consts[:, C_ID:C_ID + P]
        identb = sb("identb", [P, P], bf16)
        ones_row = sb("ones_row", [1, P])
        ones_col = sb("ones_col", [P, 1])
        zerob = sb("zerob", [P, HALF], bf16)
        pick = sb("pick", [PARTS * EP, EP], bf16)
        gates = sb("gates", [P, 8])
        gtan = sb("gtan", [P, 8])
        warm = sb("warm", [P, 1])
        stats = sb("stats", [P, NT, 6])
        mv = sb("mv", [P, NT, 2])
        veps = sb("veps", [P, NT])
        mhalf = sb("mhalf", [P, NT])
        rstd = sb("rstd", [P, NT])
        att_w = [sb(f"att_w{L}", [P, 4 * P + 2]) for L in range(4)]
        att_row = [None] + [sb(f"att_row{L}", [1, P]) for L in range(1, 4)]
        bo = {L: sb(f"bo{L}", [P, P]) for L in (1, 3)}
        wr = [sb(f"wr{L}", [P, even(L)]) for L in range(4)]
        wrpair = [sb(f"wrpair{L}", [P, 2 * even(L)], f32r) for L in range(4)]
        br2 = sb("br2", [P, ROUTE[2]["E"]])
        cbias = sb("cbias", [P, ROUTE[0]["E"]])
        b2 = {L: sb(f"b2_{L}", [PARTS * EP, P]) for L in (2, 3)}
        b2part = {L: sb(f"b2part{L}", [PARTS * EP, PARTS, P], bf16) for L in (2, 3)}
        rmax = sb("rmax", [P, NT])
        rsum = sb("rsum", [P, NT])
        rrec = sb("rrec", [P, NT])
        top8 = sb("top8", [P, NT, 8])
        gzero = sb("gzero", [P, NT])
        zsg = sb("zsg", [P, NT])
        ring = sb("ring", [P, RING, GLU_COLS])
        qf, kf = sb("qf", [P, N]), sb("kf", [P, N])
        qp, kp = sb("qp", [P, PARTS, N], bf16), sb("kp", [P, PARTS, N], bf16)
        qst, kst = sb("qst", [P, H, N], bf16), sb("kst", [P, H, N], bf16)
        vall = sb("vall", [P, NT, H, 32])
        pT = sb("pT", [P, 8, 2 * S])
        negmax = sb("negmax", [P, B, TB, H])
        nmrest = sb("nmrest", [P, TB, 4])
        nmpart = sb("nmpart", [P, 4 * B, TB, PARTS, 4], bf16)
        nmT = sb("nmT", [TB * PARTS * 4, 4 * B, P], bf16)
        oT = sb("oT", [P, 4 * S])
        orec = sb("orec", [P, TB, H])
        ocor = sb("ocor", [P, TB, H, 9])
        ocomb = sb("ocomb", [P, TB, H, 9])
        emask = sb("emask", [P, B, TB, H])
        onrm = xn
        onT = qf
        act_out, hid = pT[:, 0:2, :], pT[:, 2:4, :]
        routing = pT[:, :, :].rearrange("p a n -> p (a n)")
        shifted, probs, flagged, picked = (routing[:, n * NT * 40:(n + 1) * NT * 40].rearrange("p (t e) -> p t e", t=NT)
                                           for n in range(4))
        ranked = shifted
        wtab, wrest = (pT[:, 4, n * NT * EP:(n + 1) * NT * EP].rearrange("p (t e) -> p t e", t=NT) for n in range(2))
        wpart = pT[:, 5, 0:NT * PARTS * EP // 2].bitcast(bf16).rearrange("p (t a e) -> p t a e", t=NT, a=PARTS)
        wT = pT[0:PARTS * EP, 6, :].bitcast(bf16)
        rest = pT[:, 0, :]
        yT = oT
        pick64 = qf[0:PARTS * EP, :].bitcast(bf16)
        mask_i = qp[:, 0:2, :].rearrange("p a n -> p (a n)").bitcast(i32).rearrange("p (a k n) -> p a k n", a=2, k=TB)
        negq = ctx_tok[:, 4:8, :].rearrange("p a n -> p (a n)").bitcast(bf16).rearrange("p (a k n) -> p a k n", a=2, k=TB)
        negk = sb("negk", [P, TB, S], bf16)
        maskedT = ctx_tok[:, 0:4, :].rearrange("p a n -> p (a n)").rearrange("p (k n) -> p k n", k=TB)
        umask = consts[:, C_DFT:C_DFT + B * TB * H * 9].rearrange("p (b q n) -> p b q n", b=B, q=TB)
        masked = consts[:, C_BAND:C_BAND + TB * S].bitcast(bf16).rearrange("p (j n) -> p j n", j=4)
        negfloor = sb("negfloor", [P, TB])
        dft_in = kf
        kfreq = qf[:, :].rearrange("p (a n) -> p a n", a=2)
        prod = pT[:, 0:5, :]
        b2rest = pT[0:PARTS * EP, 7, 0:P]
        small = pT[:, 5, :]
        corr8 = small[:, 0:32].rearrange("p (b n) -> p b n", b=B)
        lag8 = small[:, 32:64].bitcast(u32).rearrange("p (b n) -> p b n", b=B)
        mix8 = small[:, 64:96].rearrange("p (b n) -> p b n", b=B)
        sel = small[:, 96:256].rearrange("p (i n) -> p i n", n=HD)
        cw = small[:, 256:316].rearrange("p (a n) -> p a n", a=3)
        csum = small[:, 320:328].rearrange("p (a n) -> p a n", a=2)
        roll_i = small[:, 328:368].bitcast(i32).rearrange("p (a n) -> p a n", a=2)
        mixT = pT[:, 6, :].rearrange("p (b n) -> p b n", b=B)
        mixo = pT[:, 7, :]
        vo = oT
        ctx_nat = kp[:, 0:2, :].rearrange("p a n -> p (a n)").bitcast(f32).rearrange("p (t d) -> p t d", t=NT)

        PS = ctx.enter_context(nc.psum_tensor("PS", [P, 8, HALF], f32))

        def banks(a, n=2):
            return PS[:, a:a + n, :].rearrange("p a n -> p (a n)")

        ld_x, ld_ctx, ld_ctxT, ld_const, ld_gate = sem("ld_x"), sem("ld_ctx"), sem("ld_ctxT"), sem("ld_const"), sem("ld_gate")
        ld_att = [sem(f"ld_att{L}") for L in range(4)]
        ld_route = sem("ld_route")
        ld_mask = sem("ld_mask")
        stored = sem("stored")
        set_pool, set_dve, gate_ready = sem("set_pool"), sem("set_dve"), sem("gate_ready")
        dstep, astep = sem("dstep"), sem("astep")
        ln_var, ln_rstd, ln_xn, ln_tr, ln_xhi = sem("ln_var"), sem("ln_rstd"), sem("ln_xn"), sem("ln_tr"), sem("ln_xhi")
        ln_xlo, wq_split = sem("ln_xlo"), sem("wq_split")
        masks_ready, stacks_set, kstep, biased = (sem(n) for n in ("masks_ready", "stacks_set", "kstep", "biased"))
        ac = {n: sem("ac_" + n) for n in ("kin", "kine", "kfreq", "kfe", "qin", "qine", "qfreq", "prod", "corr", "top",
                                          "exp", "mix", "mo", "moe", "z", "ze", "vo", "voe", "out")}
        adds = dict(q=2, k=2, v=1, kf=4, qf=2, kparts=2, qparts=2, vall=2, s=B * H, mx=B * H, nmp=4 * B, nmt=4 * B, nmc=4 * B,
                    st=B * H, p=B * H, pv=4 * B, oe=B, ot=B, on=B, fin_t=2, fin_e=2, fin=2)
        at = {n: sem(f"at_{n}") for n in (*adds, "u", "ue", "em")}
        at_kst = [None] + [[sem(f"at{L}_kst{h}") for h in range(NHALF)] for L in range(1, 4)]
        emask_in, nmstep = sem("emask_in"), sem("nmstep")
        at_qst = [None] + [[sem(f"at{L}_qst{h}") for h in range(NHALF)] for L in range(1, 4)]
        at_nmd = [sem(f"at_nmd{g}") for g in range(4)]
        rt = {n: sem("rt_" + n) for n in ("logits", "shift", "exp", "parts", "tr", "wT")}
        ring_in = [sem(f"ring_in{k}") for k in range(RING)]
        mo = [{n: sem(f"mo{L}_{n}") for n in ("wstep", "wup", "wdown", "up", "spread", "act", "gated", "hid", "hi", "lo", "y",
                                            "yT", "ytr")} for L in range(4)]
        x_done = sem("x_done")

        block = ctx.enter_context(nc.Block())
        glu_w = {0: t["glu0"], 1: t["glu1"]}
        mlp_w = {2: t["mlp2"], 3: t["mlp3"]}
        before = [[sum(len(range(k, ROUTE[M]["ENT"], RING)) for M in range(L)) for k in range(RING)] for L in range(4)]
        UP_AHEAD = 2
        U_BANK = (0, 1, 4, 5)
        LAG = 12
        NU = B * H

        def groups(entries):
            return (entries - 1) // RING

        @block.sync
        def _(sp):
            sp.dma_start(x[:, :, :], t["x"]).then_inc(ld_x, 16)
            sp.dma_start(consts[:, :], t["consts"]).then_inc(ld_const, 16)
            sp.dma_start(ctx_tok[:, :, :], t["ctx_tok"]).then_inc(ld_ctx, 16)
            sp.dma_start(ctx_nat[:, :, :], t["ctx_nat"]).then_inc(ld_ctx, 16)
            sp.dma_start(ctxT[:, :], t["ctxT"]).then_inc(ld_ctxT, 16)
            sp.dma_start(att_w[0][:, :], t["att_w0"]).then_inc(ld_att[0], 16)
            sp.dma_start(gates[:, :], t["gates"].partition_broadcast(P)).then_inc(ld_gate, 16)
            for L in range(4):
                sp.dma_start(wr[L][:, :], t[f"wr{L}"]).then_inc(ld_route, 16)
            sp.dma_start(br2[:, :], t["br2"].partition_broadcast(P)).then_inc(ld_route, 16)
            sp.dma_start(cbias[:, :], t["cbias"].partition_broadcast(P)).then_inc(ld_route, 16)
            for L in (2, 3):
                sp.dma_start(b2[L][:, :], t[f"b2_{L}"]).then_inc(ld_route, 16)
            for L in range(1, 4):
                sp.dma_start(att_w[L][:, :], t[f"att_w{L}"]).then_inc(ld_att[L], 16)
                sp.dma_start(att_row[L][:, :], t[f"att_row{L}"]).then_inc(ld_att[L], 16)
                if L != 2:
                    sp.dma_start(bo[L][:, :], t[f"bo{L}"].partition_broadcast(P)).then_inc(ld_att[L], 16)

            def load_ring(L, w, cols):
                M = mo[L]
                n = ROUTE[L]["ENT"]
                for k in range(RING):
                    if L > 0 and k == 0:
                        sp.wait_ge(mo[L - 1]["y"], UP_AHEAD + 2 * ROUTE[L - 1]["ENT"])
                    sp.dma_start(ring[:, k, 0:cols], w[k, :, :]).then_inc(ring_in[k], 16)
                with sp.Fori(0, n // RING - 1) as i:
                    for k in range(RING):
                        sp.wait_ge(M["y"], 2 * RING * i + 2 * (k + 1) + UP_AHEAD)
                        sp.dma_start(ring[:, k, 0:cols], w[RING * i + RING + k, :, :]).then_inc(ring_in[k], 16)
                for e in range(n - n % RING, n):
                    sp.wait_ge(M["y"], 2 * (e - RING) + 2 + UP_AHEAD)
                    sp.dma_start(ring[:, e % RING, 0:cols], w[e, :, :]).then_inc(ring_in[e % RING], 16)
                if L < 3:
                    stack_keys(L + 1)

            def stack_keys(L):
                if L == 1:
                    sp.wait_ge(stacks_set, 7)
                else:
                    sp.wait_ge(at["p"], (L - 1) * NU)
                for hf in range(NHALF):
                    sp.wait_ge(at["kparts"], (L - 1) * adds["kparts"] + hf + 1)
                    for n, (_, g) in enumerate(PAIRS):
                        sp.dma_start(kst[n * HD:(n + 1) * HD, :, hf * HALF:(hf + 1) * HALF],
                                     kp[:, g, hf * HALF:(hf + 1) * HALF]).then_inc(at_kst[L][hf], 16)

            def attention(L):
                A, pre = at, {n: (L - 1) * k for n, k in adds.items()}
                for hf in range(NHALF):
                    for n, (g, _) in QUERY_ORDER:
                        if n == QUERY_ORDER[0][0]:
                            sp.wait_ge(A["qf"], pre["qf"] + hf + 1)
                        elif n == QUERY_ORDER[3][0]:
                            sp.wait_ge(A["qparts"], pre["qparts"] + hf + 1)
                        sp.dma_start(qst[n * HD:(n + 1) * HD, :, hf * HALF:(hf + 1) * HALF],
                                     qp[:, g, hf * HALF:(hf + 1) * HALF]).then_inc(at_qst[L][hf], 16)
                for G in range(4 * B):
                    b, g = divmod(G, 4)
                    sp.wait_ge(A["nmc"], pre["nmc"] + G + 1)
                    for q in range(TB):
                        sp.dma_start(qst[KROWS:SROWS, 4 * g:4 * g + 4, b * S + q * P:b * S + (q + 1) * P],
                                     nmT[q * PARTS * 4:(q + 1) * PARTS * 4, G, :]).then_inc(at_nmd[g], 16)

            load_ring(0, glu_w[0], GLU_COLS)
            attention(1)
            for hf in range(NHALF):
                sp.wait_ge(at_qst[1][hf], 16 * len(PAIRS))
            sp.dma_start(mask_i[:, 0, :, :], t["mask_q"]).then_inc(ld_mask, 16)
            sp.dma_start(mask_i[:, 1, :, :], t["mask_k"]).then_inc(ld_mask, 16)
            load_ring(1, glu_w[1], GLU_COLS)
            attention(2)
            load_ring(2, mlp_w[2], MLP_COLS)
            attention(3)
            load_ring(3, mlp_w[3], MLP_COLS)
            sp.wait_ge(x_done, NHALF)
            sp.dma_start(out, x[:, :, :]).then_inc(stored, 16)
            sp.wait_ge(stored, 16)

        @block.gpsimd
        def _(pool):
            pool.memset(mhalf[:, :], -0.5).then_inc(set_pool, 1)
            pool.memset(ones_row[:, :], 1.0).then_inc(set_pool, 1)
            pool.memset(zerob[:, :], 0.0).then_inc(set_pool, 1)
            pool.memset(ones_col[:, :], 1.0).then_inc(set_pool, 1)

            def stacks(which, n):
                for stack, lo, value in which:
                    pool.wait_ge(stacks_set, n)
                    pool.memset(stack[lo:lo + 32, :, :].bitcast(f32), value).then_inc(stacks_set, 1)
                    n += 1

            def split_weights(L, glu):
                M, n = mo[L], ROUTE[L]["ENT"]
                ups = 2 * P if glu else P

                def split(step, slot, pair, c, ready):
                    w = ring[:, slot, c]
                    ones = ones_col[:, :].broadcast_to([P, c.stop - c.start])
                    pool.tensor_tensor(wpair[:, pair, 0, c], w, ones, ALU.mult).then_inc(M["wstep"], 1)
                    pool.wait_ge(M["wstep"], step)
                    pool.tensor_tensor(wpair[:, pair, 1, c], ring[:, slot, c], wpair[:, pair, 0, c].bitcast(f32),
                                       ALU.subtract).then_inc(ready, 1)

                def hidden_part(e, slot, full, first=False):
                    pool.wait_ge(ring_in[slot], full)
                    if not first:
                        pool.wait_ge(M["up"], 2 * e - 2)
                    split(max(2 * e, 1) if first else 2 * e, slot, slot % 2, slice(0, ups), M["wup"])

                def result_part(e, slot, last, first=False):
                    if not first:
                        pool.wait_ge(M["y"], 2 * e - 2 + UP_AHEAD)
                    split(2 * e + (2 if last else 3), slot, slot % 2, slice(ups, ups + P), M["wdown"])

                hidden_part(0, 0, 16 * (before[L][0] + 1), first=True)
                if L < 3:
                    split_keys(L + 1)
                for e in range(RING):
                    ne = (e + 1) % RING
                    hidden_part(e + 1, ne, 16 * (before[L][ne] + 1 + (e + 1) // RING), first=(e + 1 < 2))
                    result_part(e, e, False, first=(e < 2))
                with pool.Fori(1, groups(n)) as i:
                    for k in range(RING):
                        nk = (k + 1) % RING
                        hidden_part(RING * i + k + 1, nk, 16 * i + 16 * (before[L][nk] + 1 + (k + 1) // RING))
                        result_part(RING * i + k, k, False)
                for e in range(RING * groups(n), n):
                    ne = (e + 1) % RING
                    if e + 1 < n:
                        hidden_part(e + 1, ne, 16 * (before[L][ne] + (e + 1) // RING + 1))
                    result_part(e, e % RING, e + 1 == n)

            def split_keys(L):
                pre = {n: (L - 1) * k for n, k in adds.items()}
                for hf in range(NHALF):
                    c = slice(hf * HALF, (hf + 1) * HALF)
                    n = 6 * (L - 1) + 3 * hf
                    pool.wait_ge(at["kf"], pre["kf"] + 2 * hf + 2)
                    if L > 1:
                        for h in range(NHALF):
                            pool.wait_ge(at_kst[L - 1][h], 16 * len(PAIRS))
                    pool.tensor_tensor(kf[:, c], kf[:, c], kp[:, 0, c], ALU.subtract).then_inc(kstep, 1)
                    pool.wait_ge(kstep, n + 1)
                    pool.tensor_copy(kp[:, 1, c], kf[:, c]).then_inc(kstep, 1)
                    pool.wait_ge(kstep, n + 2)
                    pool.tensor_tensor(kp[:, 2, c], kf[:, c], kp[:, 1, c], ALU.subtract).then_inc(kstep, 1)
                    pool.wait_ge(kstep, n + 3)
                    pool.sem_inc(at["kparts"], 1)

            def split_query_weights(L):
                pool.wait_ge(ld_att[L], 32 if L == 2 else 48)
                pool.tensor_copy(wqpair[:, 0, :], att_w[L][:, 0:P]).then_inc(wq_split, 1)
                pool.wait_ge(wq_split, 2 * L - 1)
                pool.tensor_tensor(wqpair[:, 1, :], att_w[L][:, 0:P], wqpair[:, 0, :].bitcast(f32),
                                   ALU.subtract).then_inc(wq_split, 1)

            def layer_norm(s):
                for hf in range(NHALF):
                    pool.wait_ge(ln_var, NHALF * s + hf + 1)
                    c = slice(4 * hf, 4 * hf + 4)
                    pool.tensor_tensor(rstd[:, c], veps[:, c], mhalf[:, c], ALU.pow).then_inc(ln_rstd, 1)

            def split_maxima(L):
                for G in range(4 * B):
                    b, g = divmod(G, 4)
                    done = 3 * (4 * B * (L - 1) + G)
                    nm, part = negmax[:, b, :, 4 * g:4 * g + 4], nmpart[:, G, :, :, :]
                    pool.wait_ge(at["mx"], (L - 1) * NU + 4 * G + 4)
                    if L == 3:
                        pool.wait_ge(emask_in, G + 1)
                    pool.tensor_copy(part[:, :, 0, :], nm).then_inc(nmstep, 1)
                    pool.wait_ge(nmstep, done + 1)
                    pool.tensor_tensor(nmrest[:, :, :], nm, part[:, :, 0, :], ALU.subtract).then_inc(nmstep, 1)
                    pool.wait_ge(nmstep, done + 2)
                    pool.tensor_copy(part[:, :, 1, :], nmrest[:, :, :]).then_inc(nmstep, 1)
                    pool.wait_ge(nmstep, done + 3)
                    pool.tensor_tensor(part[:, :, 2, :], nmrest[:, :, :], part[:, :, 1, :],
                                       ALU.subtract).then_inc(at["nmp"], 1)
                    pool.wait_ge(at["nmp"], 4 * B * (L - 1) + G + 1)

            def output_bias(L):
                if L == 2:
                    return
                n = 0 if L == 1 else 2
                pool.wait_ge(ld_att[L], 48)
                pool.wait_ge(gate_ready, 1)
                pool.wait_ge(ln_rstd, NHALF * (2 * L + 1))
                pool.tensor_scalar(bo[L][:, :], bo[L][:, :], gtan[:, L:L + 1], None, ALU.mult).then_inc(biased, 1)
                pool.wait_ge(biased, n + 1)
                pool.wait_ge(ln_xn, NT * (2 * L + 1))
                pool.tensor_tensor(x[:, :, :], x[:, :, :], bo[L][:, :].unsqueeze(1).broadcast_to([P, NT, D]),
                                   ALU.add).then_inc(biased, 1)

            ones_pair = float(np.array([0x3F803F80], np.uint32).view(np.float32)[0])
            pool.memset(vall[:, :, :, 8:9], 1.0).then_inc(stacks_set, 1)
            pool.memset(vall[:, :, :, 9:32], 0.0).then_inc(stacks_set, 1)
            pool.wait_ge(set_pool, 4)
            pool.wait_ge(stacks_set, 2)
            layer_norm(0)
            pool.wait_ge(ln_rstd, NHALF)
            stacks(((kst, 32, 0.0), (kst, 64, 0.0), (kst, 96, ones_pair), (qst, 32, 0.0), (qst, 64, 0.0)), 2)
            pool.wait_ge(stacks_set, 7)
            layer_norm(1)
            split_weights(0, True)
            for L in range(1, 4):
                split_query_weights(L)
                layer_norm(2 * L)
                output_bias(L)
                split_maxima(L)
                layer_norm(2 * L + 1)
                split_weights(L, L < 2)

        @block.tensor
        def _(pe):
            def layer_norm(s, halves=(0, 1)):
                if s % 2 == 1 and s < 7:
                    pe.wait_ge(at["vall"], (s + 1) // 2 * adds["vall"])
                for hf in halves:
                    pe.wait_ge(ln_xn, NT * s + 4 * hf + 4)
                    for k in range(4):
                        mm = pe.transpose(PS[:, 6 + hf, k * P:(k + 1) * P], xn[:, 4 * hf + k, :], ident)
                    mm.then_inc(ln_tr, 1)

            def autocorrelation():
                W = att_w[0]
                dft = consts[:, C_DFT:C_DFT + 2 * S]
                inv = consts[:, C_INV:C_INV + 3 * S]

                def dft_tokens(src, bank, done):
                    for b in range(B):
                        for k in range(TB):
                            mm = pe.matmul(PS[:, bank + b // 2, (b % 2) * S:(b % 2 + 1) * S], src[:, TB * b + k, :],
                                           dft[:, k * S:(k + 1) * S], start=(k == 0), stop=(k == TB - 1))
                    mm.then_inc(done, 1)

                def project(bank, w, done):
                    for f in range(2):
                        for b in range(B):
                            mm = pe.matmul(PS[:, bank + f, b * P:(b + 1) * P],
                                           dft_in[:, b * S + f * P:b * S + (f + 1) * P], w, start=True, stop=True)
                    mm.then_inc(done, 1)

                pe.wait_ge(ld_const, 16)
                pe.wait_ge(ld_ctx, 32)
                dft_tokens(ctx_tok, 0, ac["kin"])
                pe.wait_ge(ac["kine"], 2)
                pe.wait_ge(ld_att[0], 16)
                project(2, W[:, P:2 * P], ac["kfreq"])
                pe.wait_ge(ld_ctx, 32)
                for i in range(NT):
                    mm = pe.matmul(PS[:, 4 + i // 4, (i % 4) * P:(i % 4 + 1) * P], ctx_nat[:, i, :], W[:, 3 * P:4 * P],
                                   start=True, stop=True)
                mm.then_inc(ac["z"], 1)
                pe.wait_ge(ac["ze"], 1)
                for hf in range(NHALF):
                    mm = pe.matmul(PS[:, 6 + hf, :], W[:, 2 * P:3 * P], vo[:, hf * HALF:(hf + 1) * HALF],
                                   start=True, stop=True)
                mm.then_inc(ac["vo"], 1)
                pe.wait_ge(ln_xn, NT)
                dft_tokens(xn, 0, ac["qin"])
                pe.wait_ge(ac["qine"], 2)
                project(4, W[:, 0:P], ac["qfreq"])
                pe.wait_ge(ac["prod"], 5)
                for b in range(B):
                    o = PS[:, b // 2, (b % 2) * S:(b % 2 + 1) * S]
                    for n, j in enumerate((0, 1, 4)):
                        mm = pe.matmul(o, prod[:, j, b * P:(b + 1) * P], inv[:, n * S:(n + 1) * S],
                                       start=(n == 0), stop=(n == 2))
                mm.then_inc(ac["corr"], 1)
                pe.wait_ge(ac["mix"], B)
                for b in range(B):
                    mm = pe.transpose(PS[:, 2, b * P:(b + 1) * P], mixT[:, b, :], ident)
                mm.then_inc(ac["mo"], 1)
                pe.wait_ge(ac["moe"], 1)
                for b in range(B):
                    mm = pe.matmul(PS[:, 4 + b // 2, (b % 2) * S:(b % 2 + 1) * S], mixo[:, b * P:(b + 1) * P],
                                   vo[:, b * S:(b + 1) * S], start=True, stop=True)
                mm.then_inc(ac["out"], 1)

            def route(L):
                E = even(L)
                if L == 0:
                    pe.wait_ge(ld_route, 16 * 8)
                if L < 3:
                    pe.wait_ge(at["kf"], (L + 1) * adds["kf"])
                for i in range(NT):
                    hf, c = i // 4, slice(i * P, (i + 1) * P)
                    o = PS[:, hf, (i % 4) * 2 * E:(i % 4 + 1) * 2 * E]
                    if i % 4 == 0:
                        pe.wait_ge(ln_xlo, 2 * NHALF * L + hf + 1)
                    pe.matmul(o, xhi[:, c], wrpair[L][:, :], start=True, stop=True)
                    mm = pe.matmul(o[:, 0:E], xlo[:, c], wrpair[L][:, 0:E], start=False, stop=True, skip_group_check=True)
                mm.then_inc(rt["logits"], 1)

            def turn_weights(L):
                pe.wait_ge(rt["parts"], L + 1)
                for i in range(NT):
                    mm = pe.transpose(PS[0:PARTS * EP, 1 - i // 4, (i % 4) * 64:(i % 4 + 1) * 64].bitcast(bf16),
                                      wpart[:, i, :, :].rearrange("p a e -> p (a e)"), identb[:, :])
                mm.then_inc(rt["tr"], 1)
                pe.wait_ge(rt["wT"], 2 * (L + 1))

            def experts(L, glu):
                M, n = mo[L], ROUTE[L]["ENT"]

                def product(o, pair, c, hi, lo, start):
                    w_hi, w_lo = wpair[:, pair, 0, c], wpair[:, pair, 1, c]
                    pe.matmul(o, w_hi, hi, start=start, stop=False, skip_group_check=True)
                    pe.matmul(o, w_hi, lo, start=False, stop=False, skip_group_check=True)
                    return pe.matmul(o, w_lo, hi, start=False, stop=start, skip_group_check=True)

                def up(unit, entry, slot, hf):
                    if hf == 0:
                        pe.wait_ge(M["wup"], entry + 1)
                    pe.wait_ge(M["gated"] if glu else M["hid"], unit + 1)
                    c = slice(hf * HALF, (hf + 1) * HALF)
                    mm = product(PS[:, 2 + hf, :], slot % 2, slice(0, P), xhi[:, c], xlo[:, c], True)
                    if glu:
                        mm = product(PS[:, 4 + hf, :], slot % 2, slice(P, 2 * P), xhi[:, c], xlo[:, c], True)
                    mm.then_inc(M["up"], 1)

                def spread(unit, entry, hf):
                    pe.wait_ge(M["hid"], unit + 1)
                    if glu:
                        w = pick64[:, bass.ds(entry * P, P)]
                    else:
                        w = pick[:, bass.ds(entry, 1)].broadcast_to([PARTS * EP, P])
                    pe.matmul(PS[:, 6 + hf, :], w, wT[:, hf * HALF:(hf + 1) * HALF],
                              start=True, stop=True).then_inc(M["spread"], 1)

                def down(unit, entry, kept):
                    slot, hf = kept // 2, kept % 2
                    if hf == 0:
                        pe.wait_ge(M["wdown"], entry + 1)
                    pe.wait_ge(M["lo"], unit + 1)
                    c = slice(2 * P, 3 * P) if glu else slice(P, 2 * P)
                    product(PS[:, hf, :], slot % 2, c, hid_hi[:, kept, :], hid_lo[:, kept, :], False).then_inc(M["y"], 1)

                for hf in range(NHALF):
                    up(hf, 0, 0, hf)
                turn_weights(L)
                for hf in range(NHALF):
                    if glu:
                        mm = pe.matmul(PS[:, hf, :], zerob[:, 0:P], zerob[:, :], start=True, stop=False,
                                       skip_group_check=True)
                    else:
                        for j in range(PARTS):
                            mm = pe.matmul(PS[:, hf, :], b2part[L][:, j, :], wT[:, hf * HALF:(hf + 1) * HALF],
                                           start=(j == 0), stop=False, skip_group_check=True)
                    mm.then_inc(M["y"], 1)
                if glu:
                    pe.wait_ge(astep, (1, 4)[L])
                for hf in range(NHALF):
                    spread(hf, 0, hf)
                for u in range(2 * RING):
                    up(u + 2, u // 2 + 1, (u // 2 + 1) % RING, u % 2)
                    spread(u + 2, u // 2 + 1, u % 2)
                    if u > 0:
                        down(u - 1, (u - 1) // 2, (u - 1) % KEPT)
                with pe.Fori(1, groups(n)) as i:
                    for k in range(RING):
                        for hf in range(NHALF):
                            u = 2 * RING * i + 2 * k + hf
                            up(u + 2, RING * i + k + 1, (k + 1) % RING, hf)
                            spread(u + 2, RING * i + k + 1, hf)
                            down(u - 1, RING * i + (k if hf else k - 1), (2 * k + hf - 1) % KEPT)
                for u in range(2 * RING * groups(n), 2 * n + 1):
                    if u + 2 < 2 * n:
                        up(u + 2, u // 2 + 1, (u // 2 + 1) % RING, u % 2)
                        spread(u + 2, u // 2 + 1, u % 2)
                    down(u - 1, (u - 1) // 2, (u - 1) % KEPT)
                pe.wait_ge(M["yT"], NHALF)
                for i in range(NT):
                    mm = pe.transpose(PS[:, 2 + i // 4, (i % 4) * P:(i % 4 + 1) * P], yT[:, i * P:(i + 1) * P], ident)
                    if i % 4 == 3:
                        mm.then_inc(M["ytr"], 1)

            def project_keys(L):
                W, row = att_w[L], att_row[L]
                pe.wait_ge(ld_att[L], 32 if L == 2 else 48)
                for hf in range(NHALF):
                    pe.matmul(PS[:, hf, :], W[:, P:2 * P], ctxT[:, hf * HALF:(hf + 1) * HALF],
                              start=True, stop=True).then_inc(at["k"], 1)
                if L > 1:
                    pe.wait_ge(at["on"], (L - 1) * adds["on"])
                    pe.wait_ge(at["fin_e"], (L - 1) * adds["fin_e"])
                else:
                    pe.wait_ge(ac["voe"], 1)
                for i in range(NT):
                    o = PS[:, 6 + i // 4, (i % 4) * P:(i % 4 + 1) * P]
                    pe.matmul(o, ctxT[:, i * P:(i + 1) * P], W[:, 2 * P:3 * P], start=True, stop=False)
                    mm = pe.matmul(o, ones_row[:, :], row[:, 0:P], start=False, stop=True)
                mm.then_inc(at["v"], 1)

            def attention(L):
                A, W, row = at, att_w[L], att_row[L]
                pre = {n: (L - 1) * k for n, k in adds.items()}
                if L == 3:
                    pe.wait_ge(A["vall"], pre["vall"] + 2)
                    pe.wait_ge(masks_ready, 1)
                    for b in range(B):
                        for q in range(TB):
                            for k in range(TB):
                                mm = pe.matmul(PS[:, U_BANK[b], q * H * 9:(q + 1) * H * 9],
                                               maskedT[:, k, q * P:(q + 1) * P], vall[:, TB * b + k, :, 0:9],
                                               start=(k == 0), stop=(k == TB - 1))
                        mm.then_inc(A["u"], 1)
                for hf in range(NHALF):
                    layer_norm(2 * L, (hf,))
                    pe.wait_ge(ln_xlo, NHALF * (2 * L - 1) + hf + 1)
                    if hf == 0:
                        pe.wait_ge(wq_split, 2 * L)
                    c = slice(hf * HALF, (hf + 1) * HALF)
                    pe.matmul(PS[:, 2 + hf, :], wqpair[:, 0, :], xhi[:, c], start=True, stop=False)
                    pe.matmul(PS[:, 2 + hf, :], wqpair[:, 0, :], xlo[:, c], start=False, stop=False)
                    pe.matmul(PS[:, 2 + hf, :], wqpair[:, 1, :], xhi[:, c], start=False, stop=True).then_inc(A["q"], 1)
                if L == 3:
                    pe.wait_ge(A["ue"], B)
                if L == 2:
                    pe.wait_ge(masks_ready, 1)

                def max_scores(v):
                    b, u = divmod(v, H)
                    h0, q = u // 2 * 2, u % 2
                    if u == 0 and b % 2 == 0:
                        pe.wait_ge(at_kst[L][b // 2], 16 * len(PAIRS))
                        pe.wait_ge(at_qst[L][b // 2], 16 * len(PAIRS))
                    if v >= 2:
                        pe.wait_ge(A["mx"], pre["mx"] + v - 1)
                    for j in range(2):
                        mm = pe.matmul(PS[:, v % 2, j * S:(j + 1) * S],
                                       qst[0:KROWS, h0 + j, b * S + q * P:b * S + (q + 1) * P],
                                       kst[0:KROWS, h0 + j, b * S:(b + 1) * S], start=True, stop=True)
                    mm.then_inc(A["s"], 1)

                def turn_max(G):
                    pe.wait_ge(A["nmp"], pre["nmp"] + G + 1)
                    if G >= 1:
                        pe.wait_ge(A["nmc"], pre["nmc"] + G)
                    if 4 * G >= H + LAG + 2:
                        pe.wait_ge(A["on"], pre["on"] + (4 * G - H - LAG - 2) // H + 1)
                    pe.transpose(PS[0:TB * PARTS * 4, 6, 0:64].bitcast(bf16),
                                 nmpart[:, G, :, :, :].rearrange("p q a n -> p (q a n)"), identb[:, :]).then_inc(A["nmt"], 1)

                def shifted_scores(w):
                    b, h = divmod(w, H)
                    if h % 4 == 0:
                        pe.wait_ge(at_nmd[h // 4], 16 * TB * (B * (L - 1) + b + 1))
                    if w == 0:
                        pe.wait_ge(A["qparts"], pre["qparts"] + 2)
                    if w >= 2:
                        pe.wait_ge(A["p"], pre["p"] + w - 1)
                    if L >= 2:
                        neg = (negq[:, 0, :, :] if L == 2 else negk[:, :, :]).rearrange("p k n -> p (k n)")
                        pe.matmul(PS[:, 2 + w % 2, :], identb[:, :], neg, start=True, stop=False,
                                  skip_group_check=True)
                    for k in range(TB):
                        mm = pe.matmul(PS[:, 2 + w % 2, k * S:(k + 1) * S],
                                       kst[0:SROWS, h, b * S + k * P:b * S + (k + 1) * P],
                                       qst[0:SROWS, h, b * S:(b + 1) * S], start=(L == 1), stop=True,
                                       skip_group_check=True)
                    mm.then_inc(A["st"], 1)

                def weigh_values(b, g):
                    pe.wait_ge(A["p"], pre["p"] + H * b + 4 * g + 4)
                    if g == 0:
                        if b > 0:
                            pe.wait_ge(A["oe"], pre["oe"] + b)
                        else:
                            pe.wait_ge(A["vall"], pre["vall"] + 2)
                    for k in range(TB):
                        for j in range(4):
                            h = 4 * g + j
                            mm = pe.matmul(PS[32 * j:32 * j + 32, 4 + g // 2, (g % 2) * S:(g % 2 + 1) * S],
                                           vall[:, TB * b + k, h, :], pT[:, (H * b + h) % 8, k * S:(k + 1) * S],
                                           start=(k == 0), stop=(k == TB - 1), skip_group_check=True)
                    mm.then_inc(A["pv"], 1)

                def turn_outputs(b):
                    pe.wait_ge(A["oe"], pre["oe"] + b + 1)
                    pe.wait_ge(A["nmc"], pre["nmc"] + min(4 * b + 8, 4 * B))
                    if b >= 1:
                        pe.wait_ge(A["on"], pre["on"] + b)
                    for q in range(TB):
                        for g in range(4):
                            mm = pe.transpose(PS[:, 6 + q, g * P:(g + 1) * P],
                                              oT[:, g * S + q * P:g * S + (q + 1) * P], ident)
                    mm.then_inc(A["ot"], 1)

                def turn_normalised(hf):
                    pe.wait_ge(A["on"], pre["on"] + 2 * hf + 2)
                    if hf == 0:
                        pe.wait_ge(A["mx"], pre["mx"] + NU)
                    for k in range(4):
                        mm = pe.transpose(PS[:, 0, k * P:(k + 1) * P], onrm[:, 4 * hf + k, :], ident)
                    mm.then_inc(A["fin_t"], 1)

                def project_outputs(hf):
                    pe.wait_ge(A["fin_e"], pre["fin_e"] + hf + 1)
                    if hf == 1:
                        pe.wait_ge(A["p"], pre["p"] + NU)
                    for k in range(4):
                        i = 4 * hf + k
                        mm = pe.matmul(PS[:, 1 + hf, k * P:(k + 1) * P], onT[:, i * P:(i + 1) * P],
                                       W[:, 3 * P:4 * P], start=True, stop=True)
                    mm.then_inc(A["fin"], 1)

                for p in range(NU + LAG):
                    if p < NU:
                        max_scores(p)
                    if p % 4 == 2 and 0 <= (p - 6) // 4 < 4 * B:
                        turn_max((p - 6) // 4)
                    w = p - LAG
                    if w >= 0:
                        shifted_scores(w)
                        if w >= 5 and w % 4 == 1:
                            weigh_values(*divmod((w - 5) // 4, 4))
                        if w >= H + 7 and w % H == 7:
                            turn_outputs(w // H - 1)
                    if p == NU + 2:
                        turn_normalised(0)
                    if p == NU + 6:
                        project_outputs(0)
                weigh_values(B - 1, 3)
                turn_outputs(B - 1)
                turn_normalised(1)
                project_outputs(1)

            pe.wait_ge(set_pool, 3)
            pe.wait_ge(set_dve, 2)
            autocorrelation()
            project_keys(1)
            layer_norm(1)
            route(0)
            experts(0, True)
            for L in range(1, 4):
                attention(L)
                if L < 3:
                    project_keys(L + 1)
                layer_norm(2 * L + 1)
                route(L)
                experts(L, L < 2)

        @block.scalar
        def _(act):
            def layer_norm(s, halves=(0, 1)):
                for hf in halves:
                    act.wait_ge(ln_tr, NHALF * (s - 1) + hf + 1)
                    c = slice(hf * HALF, (hf + 1) * HALF)
                    act.activation(xhi[:, c], PS[:, 6 + hf, :], ACT.Copy).then_inc(ln_xhi, 1)

            def take_keys(L):
                for hf in range(NHALF):
                    c = slice(hf * HALF, (hf + 1) * HALF)
                    act.wait_ge(at["k"], (L - 1) * adds["k"] + hf + 1)
                    if L > 1 and hf == 0:
                        for h in range(NHALF):
                            act.wait_ge(at_kst[L - 1][h], 16 * len(PAIRS))
                    for dst in (kf[:, c], kp[:, 0, c]):
                        act.activation(dst, PS[:, hf, :], ACT.Identity,
                                       bias=att_w[L][:, 4 * P + 1:4 * P + 2]).then_inc(at["kf"], 1)
                act.wait_ge(at["v"], L)
                if L == 1:
                    act.wait_ge(stacks_set, 2)
                for hf in range(NHALF):
                    act.activation(vall[:, 4 * hf:4 * hf + 4, :, 0:HD],
                                   PS[:, 6 + hf, :].rearrange("p (t h d) -> p t h d", t=4, h=H),
                                   ACT.Copy).then_inc(at["vall"], 1)

            def route(L):
                SM = ROUTE[L]["SM"]
                act.wait_ge(rt["shift"], L + 1)
                act.activation(probs[:, :, 0:SM], shifted[:, :, 0:SM], ACT.Exp).then_inc(rt["exp"], 1)
                if L == 1:
                    act.activation(zsg[:, :], shifted[:, :, 16], ACT.Exp, scale=-1.0).then_inc(rt["exp"], 1)
                if L < 2:
                    act.activation(pick64.rearrange("k (e f) -> k e f", e=EP),
                                   pick[:, :].unsqueeze(2).broadcast_to([PARTS * EP, EP, P // 2]), ACT.Copy).then_inc(astep, 1)
                func = ACT.Silu if L < 2 else (ACT.Gelu if L == 2 else ACT.Relu)
                act.activation(warm[:, :], gates[:, 0:1], func).then_inc(astep, 1)

            def take_weights(L):
                act.wait_ge(rt["tr"], L + 1)
                act.activation(wT[:, 0:HALF], PS[0:PARTS * EP, 1, 0:S].bitcast(bf16), ACT.Copy).then_inc(rt["wT"], 1)

            def experts(L, glu):
                M, n = mo[L], ROUTE[L]["ENT"]
                func = ACT.Silu if glu else (ACT.Gelu if L == 2 else ACT.Relu)

                def unit(u, slot, hf):
                    act.wait_ge(M["up"], u + 1)
                    act.wait_ge(M["gated"] if glu else M["hid"], u + 1)
                    bias = 0.0 if glu else ring[:, slot, 2 * P:2 * P + 1]
                    act.activation(act_out[:, hf, :], PS[:, 2 + hf, :], func, bias=bias).then_inc(M["act"], 1)

                def first_part(u, kept, first=False):
                    hf = kept % 2
                    act.wait_ge(M["hid"], u + 1 + UP_AHEAD)
                    if not first:
                        act.wait_ge(M["y"], u + 1 + UP_AHEAD - KEPT)
                    act.activation(hid_hi[:, kept, :], hid[:, hf, :], ACT.Copy).then_inc(M["hi"], 1)

                take_weights(L)
                for u in range(2 * RING):
                    unit(u, u // 2, u % 2)
                    if u > 0:
                        first_part(u - 1, (u - 1) % KEPT, first=(u - 1 < KEPT))
                with act.Fori(1, groups(n)) as i:
                    for k in range(RING):
                        for hf in range(NHALF):
                            unit(2 * RING * i + 2 * k + hf, k, hf)
                            first_part(2 * RING * i + 2 * k + hf - 1, (2 * k + hf - 1) % KEPT)
                for u in range(2 * RING * groups(n), 2 * n):
                    unit(u, u // 2 % RING, u % 2)
                    first_part(u - 1, (u - 1) % KEPT)
                first_part(2 * n - 1, (2 * n - 1) % KEPT)
                act.wait_ge(M["y"], UP_AHEAD + 2 * n - 1)
                act.activation(yT[:, 0:HALF], PS[:, 0, :], ACT.Copy, scale=gtan[:, 4 + L:5 + L]).then_inc(M["yT"], 1)

            def attention(L):
                A, W, sc = at, att_w[L], SCALE[L]
                pre = {n: (L - 1) * k for n, k in adds.items()}
                if L == 3:
                    for b in range(B):
                        act.wait_ge(A["u"], b + 1)
                        act.activation(umask[:, b, :, :], PS[:, U_BANK[b], 0:TB * H * 9].rearrange("p (q n) -> p q n", q=TB),
                                       ACT.Copy).then_inc(A["ue"], 1)
                for hf in range(NHALF):
                    layer_norm(2 * L, (hf,))
                    act.wait_ge(A["q"], pre["q"] + hf + 1)
                    c = slice(hf * HALF, (hf + 1) * HALF)
                    act.activation(qp[:, 0, c], PS[:, 2 + hf, :], ACT.Identity,
                                   bias=W[:, 4 * P:4 * P + 1]).then_inc(A["qf"], 1)
                def copy_max(G):
                    b, g = divmod(G, 4)
                    act.wait_ge(A["nmt"], pre["nmt"] + G + 1)
                    act.activation(nmT[:, G, :], PS[0:TB * PARTS * 4, 6, 0:64].bitcast(bf16), ACT.Copy).then_inc(A["nmc"], 1)
                    if L == 3 and g == 3:
                        act.activation(emask[:, b, :, :], emask[:, b, :, :], ACT.Exp, scale=sc).then_inc(A["em"], 1)

                def take_outputs(b):
                    act.wait_ge(A["pv"], pre["pv"] + 4 * (b + 1))
                    if b >= 1:
                        act.wait_ge(A["ot"], pre["ot"] + b)
                    act.activation(oT[:, :], banks(4), ACT.Copy).then_inc(A["oe"], 1)

                act.activation(warm[:, :], gates[:, 0:1], ACT.Exp).then_inc(astep, 1)
                for w in range(-2, NU):
                    if w % 4 == 2 and (w + 6) // 4 < 4 * B:
                        copy_max((w + 6) // 4 - (w < 0))
                        if w < 0:
                            copy_max(1)
                    if w < 0:
                        continue
                    if w >= H + 3 and w % H == 3:
                        take_outputs(w // H - 1)
                    if w == NU - LAG + 4:
                        act.wait_ge(A["fin_t"], pre["fin_t"] + 1)
                        act.activation(onT[:, 0:HALF], PS[:, 0, :], ACT.Copy).then_inc(A["fin_e"], 1)
                    act.wait_ge(A["st"], pre["st"] + w + 1)
                    if w >= 8:
                        act.wait_ge(A["pv"], pre["pv"] + (w - 8) // 4 + 1)
                    act.activation(pT[:, w % 8, :], PS[:, 2 + w % 2, :], ACT.Exp, scale=sc).then_inc(A["p"], 1)
                take_outputs(B - 1)
                act.wait_ge(A["fin_t"], pre["fin_t"] + 2)
                act.activation(onT[:, HALF:N], PS[:, 0, :], ACT.Copy).then_inc(A["fin_e"], 1)

            act.wait_ge(ac["kin"], 1)
            act.activation(dft_in[:, 0:HALF], PS[:, 0, :], ACT.Copy).then_inc(ac["kine"], 1)
            act.wait_ge(ac["kfreq"], 1)
            act.activation(kfreq[:, 0, :], PS[:, 2, :], ACT.Copy).then_inc(ac["kfe"], 1)
            act.activation(kfreq[:, 1, :], PS[:, 3, :], ACT.Copy).then_inc(ac["kfe"], 1)
            act.wait_ge(ac["z"], 1)
            act.activation(vo[:, :], banks(4), ACT.Copy).then_inc(ac["ze"], 1)
            act.wait_ge(ac["vo"], 1)
            act.activation(vo[:, :], banks(6), ACT.Copy).then_inc(ac["voe"], 1)
            act.wait_ge(ld_gate, 16)
            act.activation(gtan[:, :], gates[:, :], ACT.Tanh).then_inc(gate_ready, 1)
            act.wait_ge(ac["qin"], 1)
            act.activation(dft_in[:, 0:HALF], PS[:, 0, :], ACT.Copy).then_inc(ac["qine"], 1)
            act.wait_ge(ac["top"], 1)
            act.activation(cw[:, 1, :], cw[:, 0, :], ACT.Exp).then_inc(ac["exp"], 1)
            act.wait_ge(ac["mo"], 1)
            act.activation(mixo, PS[:, 2, :], ACT.Copy).then_inc(ac["moe"], 1)
            take_keys(1)
            layer_norm(1)
            route(0)
            experts(0, True)
            for L in range(1, 4):
                attention(L)
                if L < 3:
                    take_keys(L + 1)
                layer_norm(2 * L + 1)
                route(L)
                experts(L, L < 2)

        @block.vector
        def _(dve):
            steps = [0]

            def link(ins):
                steps[0] += 1
                ins.then_inc(dstep, 1)
                dve.wait_ge(dstep, steps[0])

            def run(instructions):
                for n, ins in enumerate(instructions):
                    steps[0] += 1
                    ins.then_inc(dstep, 1)
                dve.wait_ge(dstep, steps[0])

            def ln_statistics(s, hf):
                tiles = range(4 * hf, 4 * hf + 4)
                run(dve.bn_stats(stats[:, i, :], x[:, i, :]) for i in tiles)
                run(dve.bn_aggr(mv[:, i, :], stats[:, i, :]) for i in tiles)
                c = slice(4 * hf, 4 * hf + 4)
                dve.tensor_scalar(veps[:, c], mv[:, c, 1], LN_EPS, None, ALU.add).then_inc(ln_var, 1)

            def ln_apply(s, hf):
                dve.wait_ge(ln_rstd, NHALF * s + hf + 1)
                for i in range(4 * hf, 4 * hf + 4):
                    dve.tensor_scalar(xn[:, i, :], x[:, i, :], mv[:, i, 0:1], rstd[:, i:i + 1],
                                      ALU.subtract, ALU.mult).then_inc(ln_xn, 1)

            def ln_turned(s, halves=(0, 1)):
                for hf in halves if s > 0 else ():
                    dve.wait_ge(ln_xhi, NHALF * (s - 1) + hf + 1)
                    c = slice(hf * HALF, (hf + 1) * HALF)
                    dve.tensor_tensor(xlo[:, c], PS[:, 6 + hf, :], xhi[:, c].bitcast(f32), ALU.subtract).then_inc(ln_xlo, 1)

            def layer_norm(s, add=None):
                for hf in range(NHALF):
                    if add:
                        add(hf)
                    if hf == 0:
                        ln_statistics(s, 0)
                if s % 2 == 0 and s > 0:
                    ln_apply(s, 0)
                    ln_statistics(s, 1)
                    ln_turned(s, (0,))
                    ln_apply(s, 1)
                    return
                ln_statistics(s, 1)
                for hf in range(NHALF):
                    ln_apply(s, hf)
                ln_turned(s)

            def add_half(hf, bank, g, ready, count):
                dve.wait_ge(ready, count)
                xs = x[:, 4 * hf:4 * hf + 4, :].rearrange("p a n -> p (a n)")
                if g is None:
                    link(dve.tensor_tensor(xs, PS[:, bank, :], xs, ALU.add))
                else:
                    link(dve.scalar_tensor_tensor(out=xs, in0=PS[:, bank, :], scalar=gtan[:, g:g + 1], in1=xs,
                                                  op0=ALU.mult, op1=ALU.add))

            def prepare_routing():
                dve.wait_ge(ld_route, 16 * 8)
                E = [even(L) for L in range(4)]
                run(dve.tensor_copy(wrpair[L][:, 0:E[L]], wr[L][:, :]) for L in range(4))
                run(dve.tensor_tensor(wrpair[L][:, E[L]:2 * E[L]], wr[L][:, :], wrpair[L][:, 0:E[L]].bitcast(f32),
                                      ALU.subtract) for L in range(4))
                for L in (2, 3):
                    link(dve.tensor_copy(b2part[L][:, 0, :], b2[L][:, :]))
                    link(dve.tensor_tensor(b2rest[:, :], b2[L][:, :], b2part[L][:, 0, :], ALU.subtract))
                    link(dve.tensor_copy(b2part[L][:, 1, :], b2rest[:, :]))
                    link(dve.tensor_tensor(b2part[L][:, 2, :], b2rest[:, :], b2part[L][:, 1, :], ALU.subtract))

            def autocorrelation():
                dve.wait_ge(ac["kin"], 1)
                dve.tensor_copy(dft_in[:, HALF:N], PS[:, 1, :]).then_inc(ac["kine"], 1)
                layer_norm(0)
                dve.wait_ge(ac["qin"], 1)
                dve.tensor_copy(dft_in[:, HALF:N], PS[:, 1, :]).then_inc(ac["qine"], 1)
                dve.wait_ge(ac["kfe"], 2)
                dve.wait_ge(ac["qfreq"], 1)
                for j, (qx, kx) in enumerate(((0, 0), (1, 1), (1, 0), (0, 1))):
                    dve.tensor_tensor(prod[:, j, :], PS[:, 4 + qx, :], kfreq[:, kx, :], ALU.mult).then_inc(ac["prod"], 1)
                dve.wait_ge(ac["prod"], 4)
                dve.tensor_tensor(prod[:, 4, :], prod[:, 2, :], prod[:, 3, :], ALU.subtract).then_inc(ac["prod"], 1)
                prepare_routing()
                dve.wait_ge(ac["corr"], 1)
                for b in range(B):
                    c = PS[:, b // 2, (b % 2) * S:(b % 2 + 1) * S]
                    link(dve.max(corr8[:, b, :], c))
                    link(dve.max_index(lag8[:, b, :], corr8[:, b, :], c))
                top = corr8[:, :, 0:TOPLAGS]
                w0, w1, w2 = (cw[:, j, :].rearrange("p (b i) -> p b i", b=B) for j in range(3))
                dve.tensor_tensor(w0, top, corr8[:, :, 0:1].broadcast_to([P, B, TOPLAGS]), ALU.subtract).then_inc(ac["top"], 1)
                link(dve.tensor_scalar(roll_i[:, 0, :].rearrange("p (b i) -> p b i", b=B), lag8[:, :, 0:TOPLAGS], -1.0,
                                       consts[:, C_DPOS:C_DPOS + 1], ALU.mult, ALU.add))
                link(dve.tensor_scalar(roll_i[:, 1, :], roll_i[:, 0, :], HD - 1, None, ALU.bitwise_and))
                dve.wait_ge(ac["exp"], 1)
                link(dve.tensor_reduce(csum[:, 0, :], w1, AX.X, ALU.add))
                link(dve.reciprocal(csum[:, 1, :], csum[:, 0, :]))
                link(dve.tensor_tensor(w2, w1, csum[:, 1, :].unsqueeze(2).broadcast_to([P, B, TOPLAGS]), ALU.mult))
                link(dve.tensor_tensor(sel[:, :, :], roll_i[:, 1, :].unsqueeze(2).broadcast_to([P, B * TOPLAGS, HD]),
                                       consts[:, C_IOTA:C_IOTA + HD].unsqueeze(1).broadcast_to([P, B * TOPLAGS, HD]),
                                       ALU.is_equal))
                link(dve.tensor_tensor(sel[:, :, :], sel[:, :, :],
                                       cw[:, 2, :].unsqueeze(2).broadcast_to([P, B * TOPLAGS, HD]), ALU.mult))
                link(dve.tensor_reduce(mix8[:, :, :], sel[:, :, :].rearrange("p (b i) r -> p b r i", b=B), AX.X, ALU.add))
                for b in range(B):
                    dve.tensor_tensor(mixT[:, b, :].rearrange("p (h r) -> p h r", h=H),
                                      mix8[:, b:b + 1, :].broadcast_to([P, H, HD]),
                                      consts[:, C_BLK:C_BLK + H].unsqueeze(2).broadcast_to([P, H, HD]),
                                      ALU.mult).then_inc(ac["mix"], 1)
                dve.wait_ge(gate_ready, 1)

            def route(L):
                r = ROUTE[L]
                E, SM, K = r["E"], r["SM"], r["K"]
                if L < 2:
                    dve.sem_inc(mo[L]["gated"], UP_AHEAD)
                dve.sem_inc(mo[L]["hid"], UP_AHEAD)
                dve.wait_ge(rt["logits"], L + 1)
                lg = PS[:, 0:2, 0:4 * 2 * even(L)].rearrange("p b (t w) -> p b t w", t=4)
                raw = shifted[:, :, 0:E].rearrange("p (b t) e -> p b t e", b=2)
                link(dve.tensor_copy(raw, lg[:, :, :, even(L):even(L) + E]))
                link(dve.tensor_tensor(raw, lg[:, :, :, 0:E], raw, ALU.add))
                if L == 2:
                    link(dve.tensor_tensor(shifted[:, :, 0:E], shifted[:, :, 0:E],
                                           br2[:, :].unsqueeze(1).broadcast_to([P, NT, E]), ALU.add))
                link(dve.tensor_reduce(rmax[:, :], shifted[:, :, 0:SM], AX.X, ALU.max))
                dve.tensor_tensor(shifted[:, :, 0:SM], shifted[:, :, 0:SM],
                                  rmax[:, :].unsqueeze(2).broadcast_to([P, NT, SM]), ALU.subtract).then_inc(rt["shift"], 1)
                dve.wait_ge(rt["exp"], L + 1 + (L >= 1))
                link(dve.tensor_reduce(rsum[:, :], probs[:, :, 0:SM], AX.X, ALU.add))
                link(dve.reciprocal(rrec[:, :], rsum[:, :]))
                link(dve.tensor_tensor(probs[:, :, 0:SM], probs[:, :, 0:SM],
                                       rrec[:, :].unsqueeze(2).broadcast_to([P, NT, SM]), ALU.mult))
                ranking = probs
                if L == 0:
                    ranking = ranked
                    link(dve.tensor_tensor(ranked[:, :, 0:SM], probs[:, :, 0:SM],
                                           cbias[:, :].unsqueeze(1).broadcast_to([P, NT, SM]), ALU.add))
                run(dve.max(top8[:, i, :], ranking[:, i, 0:SM]) for i in range(NT))
                link(dve.memset(top8[:, :, K:8], FLAG))
                run(dve.match_replace(out=flagged[:, i, 0:SM], in_to_replace=top8[:, i, :],
                                      in_values=ranking[:, i, 0:SM], imm_value=FLAG) for i in range(NT))
                link(dve.scalar_tensor_tensor(out=picked[:, :, 0:SM], in0=flagged[:, :, 0:SM], scalar=FLAG,
                                              in1=probs[:, :, 0:SM], op0=ALU.is_equal, op1=ALU.mult))
                if L == 0:
                    link(dve.tensor_scalar(wtab[:, :, :], picked[:, :, 0:R_REAL], 2.5, None, ALU.mult))
                    link(dve.tensor_reduce(rsum[:, :], picked[:, :, R_REAL:SM], AX.X, ALU.add))
                    link(dve.tensor_scalar(gzero[:, :], rsum[:, :], 2.5, gtan[:, 4:5], ALU.mult, ALU.mult))
                elif L == 1:
                    link(dve.memset(wtab[:, :, SM + 2 * SHARED_TILES:EP], 0.0))
                    link(dve.tensor_reduce(rsum[:, :], picked[:, :, 0:SM], AX.X, ALU.add))
                    link(dve.reciprocal(rrec[:, :], rsum[:, :]))
                    link(dve.tensor_tensor(wtab[:, :, 0:SM], picked[:, :, 0:SM],
                                           rrec[:, :].unsqueeze(2).broadcast_to([P, NT, SM]), ALU.mult))
                    link(dve.tensor_scalar(rsum[:, :], zsg[:, :], 1.0, None, ALU.add))
                    link(dve.reciprocal(rrec[:, :], rsum[:, :]))
                    link(dve.tensor_copy(wtab[:, :, SM:SM + 2 * SHARED_TILES],
                                         rrec[:, :].unsqueeze(2).broadcast_to([P, NT, 2 * SHARED_TILES])))
                elif L == 2:
                    link(dve.tensor_copy(wtab[:, :, 0:SM], picked[:, :, 0:SM]))
                    link(dve.memset(wtab[:, :, SM:EP], 1.0))
                else:
                    link(dve.memset(wtab[:, :, 2 * SM:EP], 0.0))
                    for i in range(2):
                        link(dve.tensor_copy(wtab[:, :, i:2 * SM:2], picked[:, :, 0:SM]))
                link(dve.tensor_copy(wpart[:, :, 0, :], wtab[:, :, :]))
                link(dve.tensor_tensor(wrest[:, :, :], wtab[:, :, :], wpart[:, :, 0, :], ALU.subtract))
                link(dve.tensor_copy(wpart[:, :, 1, :], wrest[:, :, :]))
                dve.tensor_tensor(wpart[:, :, 2, :], wrest[:, :, :], wpart[:, :, 1, :], ALU.subtract).then_inc(rt["parts"], 1)
                if L == 1:
                    prepare_masks()

            def experts(L, glu):
                M, n = mo[L], ROUTE[L]["ENT"]
                dve.wait_ge(rt["tr"], L + 1)
                dve.tensor_copy(wT[:, HALF:N], PS[0:PARTS * EP, 0, 0:S].bitcast(bf16)).then_inc(rt["wT"], 1)
                if L == 0:
                    run(dve.scalar_tensor_tensor(out=x[:, i, :], in0=xn[:, i, :], scalar=gzero[:, i:i + 1],
                                                 in1=x[:, i, :], op0=ALU.mult, op1=ALU.add) for i in range(NT))
                if L == 2:
                    link(dve.scalar_tensor_tensor(out=x[:, :, :], in0=xn[:, :, :], scalar=gtan[:, 4 + L:5 + L],
                                                  in1=x[:, :, :], op0=ALU.mult, op1=ALU.add))

                def unit(u, kept, hf_first=False, first=False):
                    hf = kept % 2
                    dve.wait_ge(M["act"], u + 1)
                    if not hf_first:
                        dve.wait_ge(M["lo"], u - 1)
                    src = act_out
                    if glu:
                        dve.tensor_tensor(hid[:, hf, :], act_out[:, hf, :], PS[:, 4 + hf, :],
                                          ALU.mult).then_inc(M["gated"], 1)
                        src = hid
                        if not first:
                            second_part(u - 1, (kept - 1) % KEPT)
                        dve.wait_ge(M["gated"], u + 1 + UP_AHEAD)
                    dve.wait_ge(M["spread"], u + 1)
                    dve.tensor_tensor(hid[:, hf, :], src[:, hf, :], PS[:, 6 + hf, :], ALU.mult).then_inc(M["hid"], 1)
                    if not glu and not first:
                        second_part(u - 1, (kept - 1) % KEPT)

                def second_part(u, kept):
                    dve.wait_ge(M["hi"], u + 1)
                    dve.tensor_tensor(hid_lo[:, kept, :], hid[:, kept % 2, :], hid_hi[:, kept, :].bitcast(f32),
                                      ALU.subtract).then_inc(M["lo"], 1)

                for u in range(2 * RING):
                    unit(u, u % KEPT, hf_first=(u < 2), first=(u == 0))
                with dve.Fori(1, groups(n)) as i:
                    for k in range(RING):
                        for hf in range(NHALF):
                            unit(2 * RING * i + 2 * k + hf, (2 * k + hf) % KEPT)
                for u in range(2 * RING * groups(n), 2 * n):
                    unit(u, u % KEPT)
                second_part(2 * n - 1, (2 * n - 1) % KEPT)
                dve.wait_ge(M["y"], UP_AHEAD + 2 * n)
                dve.tensor_scalar(yT[:, HALF:N], PS[:, 1, :], gtan[:, 4 + L:5 + L], None, ALU.mult).then_inc(M["yT"], 1)
                if L == 3:
                    for hf in range(NHALF):
                        dve.wait_ge(M["ytr"], hf + 1)
                        xs = x[:, 4 * hf:4 * hf + 4, :].rearrange("p a n -> p (a n)")
                        dve.tensor_tensor(xs, PS[:, 2 + hf, :], xs, ALU.add).then_inc(x_done, 1)

            def prepare_masks():
                dve.wait_ge(ld_const, 16)
                dve.wait_ge(ld_mask, 32)
                link(dve.tensor_copy(negq[:, 0, :, :].rearrange("p k n -> p (k n)"), consts[:, C_BAND:C_BAND + TB * S]))
                link(dve.tensor_scalar(negq[:, 1, :, :], mask_i[:, 0, :, :], 0.0, NEG, ALU.is_equal, ALU.mult))
                link(dve.tensor_scalar(negk[:, :, :], mask_i[:, 1, :, :], 0.0, NEG, ALU.is_equal, ALU.mult))
                link(dve.tensor_scalar(maskedT[:, :, :], mask_i[:, 1, :, :], 0.0, None, ALU.is_equal))
                link(dve.tensor_scalar(maskq_f, mask_i[:, 0, :, :], 0.0, None, ALU.is_equal))
                link(dve.tensor_reduce(negfloor[:, :], maskq_f, AX.X, ALU.max))
                dve.tensor_scalar(negfloor[:, :], negfloor[:, :], -3.0e37, 3.0e37, ALU.mult, ALU.add).then_inc(dstep, 1)
                steps[0] += 1
                dve.wait_ge(dstep, steps[0])
                dve.tensor_scalar(negfloor[:, :], negfloor[:, :], -MASKED / SCALE[3], None, ALU.max).then_inc(masks_ready, 1)

            maskq_f = pT[:, 7, 0:TB * S].rearrange("p (k n) -> p k n", k=TB)

            def attention(L):
                A, pre = at, {n: (L - 1) * k for n, k in adds.items()}
                for hf in range(NHALF):
                    if hf == 1:
                        ln_turned(2 * L, (1,))
                    c, done = slice(hf * HALF, (hf + 1) * HALF), A["qparts"]
                    dve.wait_ge(A["qf"], pre["qf"] + hf + 1)
                    link(dve.scalar_tensor_tensor(out=rest[:, :], in0=PS[:, 2 + hf, :], scalar=att_w[L][:, 4 * P:4 * P + 1],
                                                  in1=qp[:, 0, c], op0=ALU.add, op1=ALU.subtract))
                    link(dve.tensor_copy(qp[:, 1, c], rest[:, :]))
                    dve.tensor_tensor(qp[:, 2, c], rest[:, :], qp[:, 1, c], ALU.subtract).then_inc(done, 1)
                    dve.wait_ge(done, pre["qparts"] + hf + 1)


                def normalise(b):
                    dve.wait_ge(A["ot"], pre["ot"] + b + 1)
                    o = PS[:, 6:8, :].rearrange("p q (h c) -> p q h c", h=H)[:, :, :, 0:9]
                    if L == 3:
                        dve.wait_ge(A["em"], b + 1)
                        for q in range(TB):
                            link(dve.tensor_tensor(ocor[:, q, :, :],
                                                   umask[:, b, q, :].rearrange("p (h c) -> p h c", h=H),
                                                   emask[:, b, q, :].unsqueeze(2).broadcast_to([P, H, 9]), ALU.mult))
                        link(dve.tensor_tensor(ocomb[:, :, :, :], o, ocor[:, :, :, :], ALU.add))
                        o = ocomb[:, :, :, :]
                    link(dve.reciprocal(orec[:, :, :], o[:, :, :, 8]))
                    for q in range(TB):
                        ins = dve.tensor_tensor(onrm[:, TB * b + q, :].rearrange("p (h d) -> p h d", h=H),
                                                o[:, q, :, 0:HD], orec[:, q, :].unsqueeze(2).broadcast_to([P, H, HD]),
                                                ALU.mult)
                        if q < TB - 1:
                            link(ins)
                    ins.then_inc(A["on"], 1)

                done_norm = 0
                for v in range(NU):
                    b, u = divmod(v, H)
                    h0, q = u // 2 * 2, u % 2
                    dve.wait_ge(A["s"], pre["s"] + v + 1)
                    if L == 1:
                        dve.tensor_reduce(negmax[:, b, q, h0:h0 + 2], PS[:, v % 2, :].rearrange("p (h k) -> p h k", h=2),
                                          AX.X, ALU.max, negate=True).then_inc(A["mx"], 1)
                    else:
                        if v >= 2:
                            dve.wait_ge(A["mx"], pre["mx"] + v - 1)
                        least = 3.4e38 if L == 2 else negfloor[:, q:q + 1]
                        for j in range(2):
                            ins = dve.tensor_tensor_reduce(masked[:, v % 2 * 2 + j, :], PS[:, v % 2, j * S:(j + 1) * S],
                                                           negq[:, L - 2, q, :], -1.0, least, ALU.add, ALU.min,
                                                           negmax[:, b, q, h0 + j:h0 + j + 1])
                        ins.then_inc(A["mx"], 1)
                    if L == 3 and u % 4 == 3:
                        dve.wait_ge(A["mx"], pre["mx"] + v + 1)
                        c = slice(u - 3, u + 1)
                        dve.tensor_scalar(emask[:, b, :, c], negmax[:, b, :, c], MASKED / SCALE[3], 0.0, ALU.add,
                                          ALU.min).then_inc(emask_in, 1)
                    if v >= LAG + H + 8 and (v - LAG) % H == 8:
                        normalise(done_norm)
                        done_norm += 1
                if L != 2:
                    dve.wait_ge(biased, 2 if L == 1 else 4)
                add_half(0, 1, L, A["fin"], pre["fin"] + 1)
                ln_statistics(2 * L + 1, 0)
                ln_apply(2 * L + 1, 0)
                for b in range(done_norm, B):
                    normalise(b)
                add_half(1, 2, L, A["fin"], pre["fin"] + 2)
                ln_statistics(2 * L + 1, 1)
                ln_apply(2 * L + 1, 1)
                ln_turned(2 * L + 1)

            dve.wait_ge(ld_const, 16)
            dve.tensor_copy(identb[:, :], ident).then_inc(set_dve, 1)
            id3 = consts[0:PARTS * EP, C_ID3:C_ID3 + EP]
            dve.tensor_copy(pick[:, :], id3).then_inc(set_dve, 1)
            dve.wait_ge(ld_x, 16)
            autocorrelation()
            layer_norm(1, lambda hf: add_half(hf, 4 + hf, 0, ac["out"], 1))
            route(0)
            experts(0, True)
            for L in range(1, 4):
                layer_norm(2 * L, lambda hf: add_half(hf, 2 + hf, None, mo[L - 1]["ytr"], hf + 1))
                attention(L)
                route(L)
                experts(L, L < 2)


def constants():
    c = np.zeros((P, C_ALL), np.float32)
    c[:, C_ID:C_ID + P] = np.eye(P)
    time, freq = np.arange(S), np.arange(P)
    angle = 2 * np.pi * np.outer(time, freq) / S
    nyq = (-1.0) ** time
    fwd = np.concatenate([np.cos(angle), np.sin(angle)], 1)
    fwd[:, P] = nyq
    c[:, C_DFT:C_DFT + 2 * S] = fwd.reshape(P, TB, 2 * P).reshape(P, -1)
    two = np.where(freq == 0, 1.0, 2.0)[:, None] / S
    icos, isin = two * np.cos(angle.T), two * np.sin(angle.T)
    icos2 = icos.copy()
    icos2[0] = nyq / S
    c[:, C_INV:C_INV + 3 * S] = np.concatenate([icos, icos2, isin], 1)
    c[:, C_BLK:C_BLK + H] = np.tile(np.eye(H), (HD, 1))
    c[:, C_DPOS] = np.arange(P) // H + S
    c[:, C_IOTA:C_IOTA + HD] = np.arange(HD)
    c[:PARTS * EP, C_ID3:C_ID3 + EP] = np.tile(np.eye(EP), (PARTS, 1))
    band = np.where(np.abs(np.subtract.outer(time, time)) <= BAND, 0.0, NEG)
    c[:, C_BAND:] = interleave(band)
    return c


def interleave(m):
    m = m.reshape(P, TB, P, TB)
    return m.transpose(0, 1, 3, 2).reshape(P, TB * S)


def tokens_on_partitions(a):
    return a.reshape(B, P, TB, D).transpose(1, 0, 2, 3).reshape(P, NT, D)


def arrays(i):
    i = {k: np.asarray(v) for k, v in i.items()}
    f = np.float32
    heads_minor = np.arange(P).reshape(H, HD).T.reshape(-1)
    col = lambda v: v.reshape(-1, 1)
    zero = np.zeros((P, 1), f)
    a = {"x": tokens_on_partitions(i["x"]), "ctx_tok": tokens_on_partitions(i["ctx_1024"]),
         "ctx_nat": i["ctx_1024"].reshape(NT, P, D).transpose(1, 0, 2),
         "ctxT": tokens_on_partitions(i["ctx_1024"]).transpose(2, 1, 0).reshape(D, N), "consts": constants(),
         "gates": np.concatenate([i["g_xattn"], i["g_ffn"]])}
    a["att_w0"] = np.concatenate([i["L0_xattn_wq"][:, heads_minor], i["L0_xattn_wk"][:, heads_minor], i["L0_xattn_wv"], i["L0_xattn_wo"], zero, zero], 1)
    wkv = i["L2_xattn_w_kv"]
    att = {1: (i["L1_xattn_Wq"].T, i["L1_xattn_Wk"].T, i["L1_xattn_Wv"].T, i["L1_xattn_Wo"].T, i["L1_xattn_bq"],
               i["L1_xattn_bk"], i["L1_xattn_bv"], i["L1_xattn_bo"]),
           2: (i["L2_xattn_w_q"], np.tile(wkv[:, :HD], (1, H)), np.tile(wkv[:, HD:], (1, H)), i["L2_xattn_w_o"],
               zero[:, 0], zero[:, 0], zero[:, 0], zero[:, 0]),
           3: (i["L3_xattn_wq"].T, i["L3_xattn_wk"].T, i["L3_xattn_wv"].T, i["L3_xattn_wo"].T, i["L3_xattn_bq"],
               i["L3_xattn_bk"], i["L3_xattn_bv"], i["L3_xattn_bo"])}
    for L, (wq, wk, wv, wo, bq, bk, bv, bo) in att.items():
        a[f"att_w{L}"] = np.concatenate([wq[:, heads_minor], wk[:, heads_minor], wv, wo, col(bq[heads_minor]),
                                         col(bk[heads_minor])], 1)
        a[f"att_row{L}"] = bv[None]
        if L != 2:
            a[f"bo{L}"] = bo
    a["wr0"] = i["L0_ffn_classifier_weight"].T
    a["wr1"] = np.concatenate([i["L1_ffn_gate_w"], i["L1_ffn_shared_gate_w"]]).T
    a["wr2"], a["wr3"] = i["L2_ffn_Wr"], i["L3_ffn_Wg"]
    for L in range(4):
        a[f"wr{L}"] = np.concatenate([a[f"wr{L}"], zero[:, :even(L) - ROUTE[L]["E"]]], 1)
    a["br2"] = i["L2_ffn_br"]
    a["cbias"] = i["L0_ffn_e_score_correction_bias"]

    def glu(gate, up, down):
        pair = lambda w: w.reshape(-1, P, D)
        return np.concatenate([pair(gate).transpose(0, 2, 1), pair(up).transpose(0, 2, 1), pair(down)], 2)

    gu = i["L0_ffn_gate_up_proj"][:R_REAL]
    a["glu0"] = glu(gu[:, :64], gu[:, 64:], i["L0_ffn_down_proj"].transpose(0, 2, 1))
    gu = i["L1_ffn_w_gate_up"].transpose(0, 2, 1)
    pad = lambda w: np.concatenate([w, np.zeros((SHARED_TILES * P - w.shape[0], D), f)]).reshape(-1, 64, D)
    a["glu1"] = np.concatenate([
        glu(gu[:, :64], gu[:, 64:], i["L1_ffn_w_down"]),
        glu(pad(i["L1_ffn_shared_w_gate"]), pad(i["L1_ffn_shared_w_up"]), pad(i["L1_ffn_shared_w_down"].T))])
    a["mlp2"] = np.concatenate([np.concatenate([i["L2_ffn_We1"], i["L2_ffn_ws1"][None]]),
                                np.concatenate([i["L2_ffn_We2"], i["L2_ffn_ws2"][None]]),
                                np.concatenate([i["L2_ffn_Be1"], i["L2_ffn_bs1"][None]])[:, :, None]], 2)
    a["b2_2"] = np.concatenate([i["L2_ffn_Be2"], i["L2_ffn_bs2"][None]] * PARTS)
    w1 = i["L3_ffn_W1"].reshape(8, D, 2, P).transpose(0, 2, 1, 3).reshape(16, D, P)
    a["mlp3"] = np.concatenate([w1, i["L3_ffn_W2"].reshape(16, P, D), i["L3_ffn_b1"].reshape(16, P, 1)], 2)
    b23 = np.zeros((EP, P), f)
    b23[0:16:2] = i["L3_ffn_b2"]
    a["b2_3"] = np.tile(b23, (PARTS, 1))
    m = i["mask_1x1xSxS2_ik1"].reshape(S, S)
    a["mask_q"] = interleave(m).reshape(P, TB, S)
    a["mask_k"] = interleave(m.T).reshape(P, TB, S)
    return {k: np.ascontiguousarray(v) for k, v in a.items()}


def kernel(**inputs):
    import concourse.bacc as bacc
    from concourse.bass_utils import run_bass_kernel_spmd

    nc = bacc.Bacc("TRN2", target_bir_lowering=False, num_devices=1)
    data = arrays(inputs)
    t = {k: nc.dram_tensor(f"in_{k}", v.shape, mybir.dt.from_np(v.dtype), kind="ExternalInput").ap()
         for k, v in data.items()}
    out = nc.dram_tensor("out_x", (P, NT, D), mybir.dt.float32, kind="ExternalOutput").ap()
    build(nc, t, out)
    r = run_bass_kernel_spmd(nc, [{f"in_{k}": v for k, v in data.items()}], core_ids=[0])
    got = np.asarray(r.results[0]["out_x"])
    return got.reshape(P, B, TB, D).transpose(1, 0, 2, 3).reshape(B, S, D)
```
